# Optimizing a Trainium2 kernel written in Bass

```python
import numpy as np
import jax
import jax.numpy as jnp

def _softmax(x, axis=-1):
    return jax.nn.softmax(x, axis=axis)

def _gelu(x):
    return jax.nn.gelu(x, approximate=True)

def _silu(x):
    return jax.nn.silu(x)

def _sigmoid(x):
    return jax.nn.sigmoid(x)

def _layernorm(x, axis=-1, eps=1e-05):
    m = jnp.mean(x, axis=axis, keepdims=True)
    v = jnp.var(x, axis=axis, keepdims=True)
    return (x - m) / jnp.sqrt(v + eps)

def _scatter_add(tgt, idx, src, axis=0):
    return tgt.at[idx].add(src)

def _segment_sum(src, seg, n):
    return jax.ops.segment_sum(src, seg, n)
kernel_name = 'mk_pixart_seq_d4_seqx_r8_c0f1c3'

def setup_inputs(seed: int=0):
    np.random.seed(seed)
    _w = jnp.asarray

    def _rec_inputs():
        import jax
        import jax.numpy as jnp
        _rk = jax.random.key(seed)
        x = -0.0002928 + 1 * jax.random.normal(jax.random.fold_in(_rk, 1), (16, 56, 128), jnp.float32)
        _lenS = 56 - jax.random.randint(jax.random.fold_in(_rk, 7), (16,), 0, max(1, 56 // 4) + 1, jnp.int32)
        _lenS2 = 1500 - jax.random.randint(jax.random.fold_in(_rk, 8), (16,), 0, max(1, 1500 // 4) + 1, jnp.int32)
        cond_1024 = 0.0061147 + 1.02565 * jax.random.normal(jax.random.fold_in(_rk, 11), (16, 128), jnp.float32)
        _ctx_1024P = jax.random.normal(jax.random.fold_in(_rk, 12), (16, 16, 128), jnp.float32)
        _ctx_1024c = jax.random.dirichlet(jax.random.fold_in(_rk, 512), 0.3 * jnp.ones((16,), jnp.float32), (16, 1500))
        _ctx_1024t = jnp.einsum('bsk,bkd->bsd', _ctx_1024c, _ctx_1024P)
        _ctx_1024t = _ctx_1024t * jax.lax.rsqrt(jnp.mean(jnp.square(_ctx_1024t)) + 1e-12) * 0.953939
        ctx_1024 = -0.00265004 + 0.998804 * (_ctx_1024t + 0.3 * jax.random.normal(jax.random.fold_in(_rk, 612), (16, 1500, 128), jnp.float32))
        _validS = jnp.arange(56)[None, :] < _lenS[:, None]
        _validS2 = jnp.arange(1500)[None, :] < _lenS2[:, None]
        _causal = jnp.tril(jnp.ones((56, 56), dtype=bool))
        mask_BxS2_bf0 = jnp.logical_not(jnp.ones((16, 1500), dtype=bool))
        return (x, cond_1024, ctx_1024, mask_BxS2_bf0)
    x, cond_1024, ctx_1024, mask_BxS2_bf0 = _rec_inputs()

    def _L0_xcond_setup():
        import jax, jax.numpy as jnp
        import numpy as np
        LN_EPS = 1e-06

        def _ln(x):
            mu = jnp.mean(x, axis=-1, keepdims=True)
            var = jnp.var(x, axis=-1, keepdims=True)
            return (x - mu) * jax.lax.rsqrt(var + LN_EPS)
        key = jax.random.key(seed)
        H, NH = (128, 16)
        B, N, S = (4, 128, 77)
        MLP = int(H * 4.0)
        ks = jax.random.split(key, 20)
        s = 1.0 / np.sqrt(H)
        return {'x': jax.random.normal(ks[0], (B, N, H), jnp.float32), 'c': jax.random.normal(ks[1], (B, H), jnp.float32), 'context': jax.random.normal(ks[2], (B, S, H), jnp.float32), 'W_mod': jax.random.normal(ks[3], (H, 6 * H), jnp.float32) * s, 'b_mod': jnp.zeros((6 * H,), jnp.float32), 'W_qkv': jax.random.normal(ks[4], (H, 3 * H), jnp.float32) * s, 'b_qkv': jnp.zeros((3 * H,), jnp.float32), 'W_proj': jax.random.normal(ks[5], (H, H), jnp.float32) * s, 'b_proj': jnp.zeros((H,), jnp.float32), 'W_qc': jax.random.normal(ks[6], (H, H), jnp.float32) * s, 'b_qc': jnp.zeros((H,), jnp.float32), 'W_kvc': jax.random.normal(ks[7], (H, 2 * H), jnp.float32) * s, 'b_kvc': jnp.zeros((2 * H,), jnp.float32), 'W_cproj': jax.random.normal(ks[8], (H, H), jnp.float32) * s, 'b_cproj': jnp.zeros((H,), jnp.float32), 'W_mlp1': jax.random.normal(ks[9], (H, MLP), jnp.float32) * s, 'b_mlp1': jnp.zeros((MLP,), jnp.float32), 'W_mlp2': jax.random.normal(ks[10], (MLP, H), jnp.float32) * (1.0 / np.sqrt(MLP)), 'b_mlp2': jnp.zeros((H,), jnp.float32)}
    _L0_xcond_all = _L0_xcond_setup()
    _L0_xcond_in = {k: v for k, v in _L0_xcond_all.items() if k in ('W_mod', 'b_mod', 'W_qkv', 'b_qkv', 'W_proj', 'b_proj', 'W_qc', 'b_qc', 'W_kvc', 'b_kvc', 'W_cproj', 'b_cproj', 'W_mlp1', 'b_mlp1', 'W_mlp2', 'b_mlp2')}
    del _L0_xcond_all

    def _L1_xcond_setup():
        import jax, jax.numpy as jnp
        import numpy as np
        EPS = 1e-06
        H = 16

        def layer_norm(x, gamma=None, beta=None):
            x32 = x.astype(jnp.float32)
            mu = jnp.mean(x32, axis=-1, keepdims=True)
            var = jnp.var(x32, axis=-1, keepdims=True)
            y = (x32 - mu) * jax.lax.rsqrt(var + EPS)
            if gamma is not None:
                y = y * gamma + beta
            return y.astype(x.dtype)

        def mha(q, k, v):
            B, Nq, C = q.shape
            d = C // H
            qh = q.reshape(B, Nq, H, d)
            kh = k.reshape(B, k.shape[1], H, d)
            vh = v.reshape(B, v.shape[1], H, d)
            scores = jnp.einsum('bqhd,bkhd->bhqk', qh, kh) / jnp.sqrt(jnp.asarray(d, q.dtype))
            attn = jax.nn.softmax(scores, axis=-1)
            out = jnp.einsum('bhqk,bkhd->bqhd', attn, vh)
            return out.reshape(B, Nq, C)
        key = jax.random.key(seed)
        ks = jax.random.split(key, 24)
        B, N, C, M, Cc = (4, 256, 128, 128, 128)
        hid = 4 * C
        s = 0.02
        return {'x': jax.random.normal(ks[0], (B, N, C), jnp.float32), 'mod': jax.random.normal(ks[1], (B, C), jnp.float32), 'context': jax.random.normal(ks[2], (B, M, Cc), jnp.float32), 'ada_w': jax.random.normal(ks[3], (C, 6 * C), jnp.float32) * s, 'ada_b': jnp.zeros((6 * C,), jnp.float32), 'qkv_w': jax.random.normal(ks[4], (C, 3 * C), jnp.float32) * s, 'qkv_b': jnp.zeros((3 * C,), jnp.float32), 'self_o_w': jax.random.normal(ks[5], (C, C), jnp.float32) * s, 'self_o_b': jnp.zeros((C,), jnp.float32), 'norm2_g': jnp.ones((C,), jnp.float32), 'norm2_b': jnp.zeros((C,), jnp.float32), 'q_w': jax.random.normal(ks[6], (C, C), jnp.float32) * s, 'q_b': jnp.zeros((C,), jnp.float32), 'kv_w': jax.random.normal(ks[7], (Cc, 2 * C), jnp.float32) * s, 'kv_b': jnp.zeros((2 * C,), jnp.float32), 'cross_o_w': jax.random.normal(ks[8], (C, C), jnp.float32) * s, 'cross_o_b': jnp.zeros((C,), jnp.float32), 'mlp_w1': jax.random.normal(ks[9], (C, hid), jnp.float32) * s, 'mlp_b1': jnp.zeros((hid,), jnp.float32), 'mlp_w2': jax.random.normal(ks[10], (hid, C), jnp.float32) * s, 'mlp_b2': jnp.zeros((C,), jnp.float32)}
    _L1_xcond_all = _L1_xcond_setup()
    _L1_xcond_in = {k: v for k, v in _L1_xcond_all.items() if k in ('ada_w', 'ada_b', 'qkv_w', 'qkv_b', 'self_o_w', 'self_o_b', 'norm2_g', 'norm2_b', 'q_w', 'q_b', 'kv_w', 'kv_b', 'cross_o_w', 'cross_o_b', 'mlp_w1', 'mlp_b1', 'mlp_w2', 'mlp_b2')}
    del _L1_xcond_all

    def _L2_xcond_setup():
        import jax, jax.numpy as jnp
        import numpy as np
        D, H, B, N, S = (128, 16, 4, 128, 77)
        HD = D // H
        DF = 4 * D
        EPS = 1e-06
        SCALE = HD ** (-0.5)

        def _ln(x):
            m = jnp.mean(x, axis=-1, keepdims=True)
            v = jnp.mean((x - m) ** 2, axis=-1, keepdims=True)
            return (x - m) / jnp.sqrt(v + EPS)
        key = jax.random.key(seed)
        ks = jax.random.split(key, 24)
        s = 0.02
        inp = {'x': jax.random.normal(ks[0], (B, N, D), jnp.float32), 't_emb': jax.random.normal(ks[1], (B, D), jnp.float32), 'context': jax.random.normal(ks[2], (B, S, D), jnp.float32), 'context_mask': jnp.zeros((B, S), jnp.bool_), 'ada_w': jax.random.normal(ks[3], (D, 6 * D), jnp.float32) * s, 'ada_b': jnp.zeros((6 * D,), jnp.float32), 'qkv_w': jax.random.normal(ks[4], (D, 3 * D), jnp.float32) * s, 'qkv_b': jnp.zeros((3 * D,), jnp.float32), 'sa_proj_w': jax.random.normal(ks[5], (D, D), jnp.float32) * s, 'sa_proj_b': jnp.zeros((D,), jnp.float32), 'q_w': jax.random.normal(ks[6], (D, D), jnp.float32) * s, 'q_b': jnp.zeros((D,), jnp.float32), 'kv_w': jax.random.normal(ks[7], (D, 2 * D), jnp.float32) * s, 'kv_b': jnp.zeros((2 * D,), jnp.float32), 'ca_proj_w': jax.random.normal(ks[8], (D, D), jnp.float32) * s, 'ca_proj_b': jnp.zeros((D,), jnp.float32), 'fc1_w': jax.random.normal(ks[9], (D, DF), jnp.float32) * s, 'fc1_b': jnp.zeros((DF,), jnp.float32), 'fc2_w': jax.random.normal(ks[10], (DF, D), jnp.float32) * s, 'fc2_b': jnp.zeros((D,), jnp.float32)}
        return inp
    _L2_xcond_all = _L2_xcond_setup()
    _L2_xcond_in = {k: v for k, v in _L2_xcond_all.items() if k in ('ada_w', 'ada_b', 'qkv_w', 'qkv_b', 'sa_proj_w', 'sa_proj_b', 'q_w', 'q_b', 'kv_w', 'kv_b', 'ca_proj_w', 'ca_proj_b', 'fc1_w', 'fc1_b', 'fc2_w', 'fc2_b')}
    del _L2_xcond_all

    def _L3_xcond_setup():
        import jax, jax.numpy as jnp
        import numpy as np
        D = 128
        H = 16
        HD = D // H
        MLP = 4 * D
        EPS = 1e-06
        SCALE = HD ** (-0.5)

        def _p(key, shape, s=0.02):
            return jax.random.normal(key, shape, dtype=jnp.float32) * s

        def _ln(x):
            mu = jnp.mean(x, axis=-1, keepdims=True)
            var = jnp.var(x, axis=-1, keepdims=True)
            return (x - mu) * jax.lax.rsqrt(var + EPS)

        def _heads(t):
            B, L, _ = t.shape
            return t.reshape(B, L, H, HD).transpose(0, 2, 1, 3)

        def _attend(q, k, v):
            attn = jnp.einsum('bhnd,bhsd->bhns', q, k) * SCALE
            attn = jax.nn.softmax(attn, axis=-1)
            o = jnp.einsum('bhns,bhsd->bhnd', attn, v)
            B, _, N, _ = q.shape
            return o.transpose(0, 2, 1, 3).reshape(B, N, D)
        key = jax.random.key(seed)
        ks = jax.random.split(key, 24)
        B, N, S = (4, 128, 77)
        return {'x': jax.random.normal(ks[0], (B, N, D), dtype=jnp.float32), 't_emb': jax.random.normal(ks[1], (B, D), dtype=jnp.float32), 'context': jax.random.normal(ks[2], (B, S, D), dtype=jnp.float32), 'adaln_w': _p(ks[3], (D, 6 * D)), 'adaln_b': _p(ks[4], (6 * D,)), 'qkv_w': _p(ks[5], (D, 3 * D)), 'qkv_b': _p(ks[6], (3 * D,)), 'sa_proj_w': _p(ks[7], (D, D)), 'sa_proj_b': _p(ks[8], (D,)), 'q_w': _p(ks[9], (D, D)), 'q_b': _p(ks[10], (D,)), 'kv_w': _p(ks[11], (D, 2 * D)), 'kv_b': _p(ks[12], (2 * D,)), 'ca_proj_w': _p(ks[13], (D, D)), 'ca_proj_b': _p(ks[14], (D,)), 'fc1_w': _p(ks[15], (D, MLP)), 'fc1_b': _p(ks[16], (MLP,)), 'fc2_w': _p(ks[17], (MLP, D)), 'fc2_b': _p(ks[18], (D,))}
    _L3_xcond_all = _L3_xcond_setup()
    _L3_xcond_in = {k: v for k, v in _L3_xcond_all.items() if k in ('adaln_w', 'adaln_b', 'qkv_w', 'qkv_b', 'sa_proj_w', 'sa_proj_b', 'q_w', 'q_b', 'kv_w', 'kv_b', 'ca_proj_w', 'ca_proj_b', 'fc1_w', 'fc1_b', 'fc2_w', 'fc2_b')}
    del _L3_xcond_all
    return {'x': x, 'cond_1024': cond_1024, 'ctx_1024': ctx_1024, 'mask_BxS2_bf0': mask_BxS2_bf0, 'L0_xcond_W_mod': _L0_xcond_in['W_mod'], 'L0_xcond_b_mod': _L0_xcond_in['b_mod'], 'L0_xcond_W_qkv': _L0_xcond_in['W_qkv'], 'L0_xcond_b_qkv': _L0_xcond_in['b_qkv'], 'L0_xcond_W_proj': _L0_xcond_in['W_proj'], 'L0_xcond_b_proj': _L0_xcond_in['b_proj'], 'L0_xcond_W_qc': _L0_xcond_in['W_qc'], 'L0_xcond_b_qc': _L0_xcond_in['b_qc'], 'L0_xcond_W_kvc': _L0_xcond_in['W_kvc'], 'L0_xcond_b_kvc': _L0_xcond_in['b_kvc'], 'L0_xcond_W_cproj': _L0_xcond_in['W_cproj'], 'L0_xcond_b_cproj': _L0_xcond_in['b_cproj'], 'L0_xcond_W_mlp1': _L0_xcond_in['W_mlp1'], 'L0_xcond_b_mlp1': _L0_xcond_in['b_mlp1'], 'L0_xcond_W_mlp2': _L0_xcond_in['W_mlp2'], 'L0_xcond_b_mlp2': _L0_xcond_in['b_mlp2'], 'L1_xcond_ada_w': _L1_xcond_in['ada_w'], 'L1_xcond_ada_b': _L1_xcond_in['ada_b'], 'L1_xcond_qkv_w': _L1_xcond_in['qkv_w'], 'L1_xcond_qkv_b': _L1_xcond_in['qkv_b'], 'L1_xcond_self_o_w': _L1_xcond_in['self_o_w'], 'L1_xcond_self_o_b': _L1_xcond_in['self_o_b'], 'L1_xcond_norm2_g': _L1_xcond_in['norm2_g'], 'L1_xcond_norm2_b': _L1_xcond_in['norm2_b'], 'L1_xcond_q_w': _L1_xcond_in['q_w'], 'L1_xcond_q_b': _L1_xcond_in['q_b'], 'L1_xcond_kv_w': _L1_xcond_in['kv_w'], 'L1_xcond_kv_b': _L1_xcond_in['kv_b'], 'L1_xcond_cross_o_w': _L1_xcond_in['cross_o_w'], 'L1_xcond_cross_o_b': _L1_xcond_in['cross_o_b'], 'L1_xcond_mlp_w1': _L1_xcond_in['mlp_w1'], 'L1_xcond_mlp_b1': _L1_xcond_in['mlp_b1'], 'L1_xcond_mlp_w2': _L1_xcond_in['mlp_w2'], 'L1_xcond_mlp_b2': _L1_xcond_in['mlp_b2'], 'L2_xcond_ada_w': _L2_xcond_in['ada_w'], 'L2_xcond_ada_b': _L2_xcond_in['ada_b'], 'L2_xcond_qkv_w': _L2_xcond_in['qkv_w'], 'L2_xcond_qkv_b': _L2_xcond_in['qkv_b'], 'L2_xcond_sa_proj_w': _L2_xcond_in['sa_proj_w'], 'L2_xcond_sa_proj_b': _L2_xcond_in['sa_proj_b'], 'L2_xcond_q_w': _L2_xcond_in['q_w'], 'L2_xcond_q_b': _L2_xcond_in['q_b'], 'L2_xcond_kv_w': _L2_xcond_in['kv_w'], 'L2_xcond_kv_b': _L2_xcond_in['kv_b'], 'L2_xcond_ca_proj_w': _L2_xcond_in['ca_proj_w'], 'L2_xcond_ca_proj_b': _L2_xcond_in['ca_proj_b'], 'L2_xcond_fc1_w': _L2_xcond_in['fc1_w'], 'L2_xcond_fc1_b': _L2_xcond_in['fc1_b'], 'L2_xcond_fc2_w': _L2_xcond_in['fc2_w'], 'L2_xcond_fc2_b': _L2_xcond_in['fc2_b'], 'L3_xcond_adaln_w': _L3_xcond_in['adaln_w'], 'L3_xcond_adaln_b': _L3_xcond_in['adaln_b'], 'L3_xcond_qkv_w': _L3_xcond_in['qkv_w'], 'L3_xcond_qkv_b': _L3_xcond_in['qkv_b'], 'L3_xcond_sa_proj_w': _L3_xcond_in['sa_proj_w'], 'L3_xcond_sa_proj_b': _L3_xcond_in['sa_proj_b'], 'L3_xcond_q_w': _L3_xcond_in['q_w'], 'L3_xcond_q_b': _L3_xcond_in['q_b'], 'L3_xcond_kv_w': _L3_xcond_in['kv_w'], 'L3_xcond_kv_b': _L3_xcond_in['kv_b'], 'L3_xcond_ca_proj_w': _L3_xcond_in['ca_proj_w'], 'L3_xcond_ca_proj_b': _L3_xcond_in['ca_proj_b'], 'L3_xcond_fc1_w': _L3_xcond_in['fc1_w'], 'L3_xcond_fc1_b': _L3_xcond_in['fc1_b'], 'L3_xcond_fc2_w': _L3_xcond_in['fc2_w'], 'L3_xcond_fc2_b': _L3_xcond_in['fc2_b']}

def reference(x, cond_1024, ctx_1024, mask_BxS2_bf0, L0_xcond_W_mod, L0_xcond_b_mod, L0_xcond_W_qkv, L0_xcond_b_qkv, L0_xcond_W_proj, L0_xcond_b_proj, L0_xcond_W_qc, L0_xcond_b_qc, L0_xcond_W_kvc, L0_xcond_b_kvc, L0_xcond_W_cproj, L0_xcond_b_cproj, L0_xcond_W_mlp1, L0_xcond_b_mlp1, L0_xcond_W_mlp2, L0_xcond_b_mlp2, L1_xcond_ada_w, L1_xcond_ada_b, L1_xcond_qkv_w, L1_xcond_qkv_b, L1_xcond_self_o_w, L1_xcond_self_o_b, L1_xcond_norm2_g, L1_xcond_norm2_b, L1_xcond_q_w, L1_xcond_q_b, L1_xcond_kv_w, L1_xcond_kv_b, L1_xcond_cross_o_w, L1_xcond_cross_o_b, L1_xcond_mlp_w1, L1_xcond_mlp_b1, L1_xcond_mlp_w2, L1_xcond_mlp_b2, L2_xcond_ada_w, L2_xcond_ada_b, L2_xcond_qkv_w, L2_xcond_qkv_b, L2_xcond_sa_proj_w, L2_xcond_sa_proj_b, L2_xcond_q_w, L2_xcond_q_b, L2_xcond_kv_w, L2_xcond_kv_b, L2_xcond_ca_proj_w, L2_xcond_ca_proj_b, L2_xcond_fc1_w, L2_xcond_fc1_b, L2_xcond_fc2_w, L2_xcond_fc2_b, L3_xcond_adaln_w, L3_xcond_adaln_b, L3_xcond_qkv_w, L3_xcond_qkv_b, L3_xcond_sa_proj_w, L3_xcond_sa_proj_b, L3_xcond_q_w, L3_xcond_q_b, L3_xcond_kv_w, L3_xcond_kv_b, L3_xcond_ca_proj_w, L3_xcond_ca_proj_b, L3_xcond_fc1_w, L3_xcond_fc1_b, L3_xcond_fc2_w, L3_xcond_fc2_b):
    import jax
    import jax.numpy as jnp

    def _L0_xcond_ref(x, c, context, W_mod, b_mod, W_qkv, b_qkv, W_proj, b_proj, W_qc, b_qc, W_kvc, b_kvc, W_cproj, b_cproj, W_mlp1, b_mlp1, W_mlp2, b_mlp2):
        import jax, jax.numpy as jnp
        import numpy as np
        LN_EPS = 1e-06

        def _ln(x):
            mu = jnp.mean(x, axis=-1, keepdims=True)
            var = jnp.var(x, axis=-1, keepdims=True)
            return (x - mu) * jax.lax.rsqrt(var + LN_EPS)
        B, N, H = x.shape
        NH = 16
        hd = H // NH
        scale = hd ** (-0.5)
        c_proj = jax.nn.silu(c) @ W_mod + b_mod
        shift_a, scale_a, gate_a, shift_m, scale_m, gate_m = jnp.split(c_proj, 6, axis=-1)

        def modulate(t, shift, sc):
            return t * (1 + sc[:, None]) + shift[:, None]
        x_norm = modulate(_ln(x), shift_a, scale_a)
        qkv = x_norm @ W_qkv + b_qkv
        q, k, v = jnp.split(qkv, 3, axis=-1)
        q = q.reshape(B, N, NH, hd).transpose(0, 2, 1, 3)
        k = k.reshape(B, N, NH, hd).transpose(0, 2, 1, 3)
        v = v.reshape(B, N, NH, hd).transpose(0, 2, 1, 3)
        attn_w = jax.nn.softmax(jnp.einsum('bhqd,bhkd->bhqk', q, k) * scale, axis=-1)
        attn_out = jnp.einsum('bhqk,bhkd->bhqd', attn_w, v)
        attn_out = attn_out.transpose(0, 2, 1, 3).reshape(B, N, H)
        attn_out = attn_out @ W_proj + b_proj
        x = x + gate_a[:, None] * attn_out
        S = context.shape[1]
        q_c = _ln(x) @ W_qc + b_qc
        kv_c = _ln(context) @ W_kvc + b_kvc
        k_c, v_c = jnp.split(kv_c, 2, axis=-1)
        q_c = q_c.reshape(B, N, NH, hd).transpose(0, 2, 1, 3)
        k_c = k_c.reshape(B, S, NH, hd).transpose(0, 2, 1, 3)
        v_c = v_c.reshape(B, S, NH, hd).transpose(0, 2, 1, 3)
        c_attn_w = jax.nn.softmax(jnp.einsum('bhqd,bhsd->bhqs', q_c, k_c) * scale, axis=-1)
        c_attn_out = jnp.einsum('bhqs,bhsd->bhqd', c_attn_w, v_c)
        c_attn_out = c_attn_out.transpose(0, 2, 1, 3).reshape(B, N, H)
        c_attn_out = c_attn_out @ W_cproj + b_cproj
        x = x + c_attn_out
        x_norm2 = modulate(_ln(x), shift_m, scale_m)
        h = jax.nn.gelu(x_norm2 @ W_mlp1 + b_mlp1)
        h = h @ W_mlp2 + b_mlp2
        x = x + gate_m[:, None] * h
        return x

    def _L1_xcond_ref(x, mod, context, ada_w, ada_b, qkv_w, qkv_b, self_o_w, self_o_b, norm2_g, norm2_b, q_w, q_b, kv_w, kv_b, cross_o_w, cross_o_b, mlp_w1, mlp_b1, mlp_w2, mlp_b2):
        import jax, jax.numpy as jnp
        import numpy as np
        EPS = 1e-06
        H = 16

        def layer_norm(x, gamma=None, beta=None):
            x32 = x.astype(jnp.float32)
            mu = jnp.mean(x32, axis=-1, keepdims=True)
            var = jnp.var(x32, axis=-1, keepdims=True)
            y = (x32 - mu) * jax.lax.rsqrt(var + EPS)
            if gamma is not None:
                y = y * gamma + beta
            return y.astype(x.dtype)

        def mha(q, k, v):
            B, Nq, C = q.shape
            d = C // H
            qh = q.reshape(B, Nq, H, d)
            kh = k.reshape(B, k.shape[1], H, d)
            vh = v.reshape(B, v.shape[1], H, d)
            scores = jnp.einsum('bqhd,bkhd->bhqk', qh, kh) / jnp.sqrt(jnp.asarray(d, q.dtype))
            attn = jax.nn.softmax(scores, axis=-1)
            out = jnp.einsum('bhqk,bkhd->bqhd', attn, vh)
            return out.reshape(B, Nq, C)
        C = x.shape[-1]
        m = jax.nn.silu(mod) @ ada_w + ada_b
        shift_msa, scale_msa, gate_msa, shift_mlp, scale_mlp, gate_mlp = [c[:, None, :] for c in jnp.split(m, 6, axis=-1)]
        h = layer_norm(x)
        h = h * (1.0 + scale_msa) + shift_msa
        qkv = h @ qkv_w + qkv_b
        q, k, v = jnp.split(qkv, 3, axis=-1)
        h = mha(q, k, v) @ self_o_w + self_o_b
        x = x + h * gate_msa
        h = layer_norm(x, norm2_g, norm2_b)
        q = h @ q_w + q_b
        kv = context @ kv_w + kv_b
        k, v = jnp.split(kv, 2, axis=-1)
        h = mha(q, k, v) @ cross_o_w + cross_o_b
        x = x + h
        h = layer_norm(x)
        h = h * (1.0 + scale_mlp) + shift_mlp
        h = jax.nn.gelu(h @ mlp_w1 + mlp_b1) @ mlp_w2 + mlp_b2
        x = x + h * gate_mlp
        return x

    def _L2_xcond_ref(x, t_emb, context, context_mask, ada_w, ada_b, qkv_w, qkv_b, sa_proj_w, sa_proj_b, q_w, q_b, kv_w, kv_b, ca_proj_w, ca_proj_b, fc1_w, fc1_b, fc2_w, fc2_b):
        import jax, jax.numpy as jnp
        import numpy as np
        D, H, B, N, S = (128, 16, 4, 128, 77)
        HD = D // H
        DF = 4 * D
        EPS = 1e-06
        SCALE = HD ** (-0.5)

        def _ln(x):
            m = jnp.mean(x, axis=-1, keepdims=True)
            v = jnp.mean((x - m) ** 2, axis=-1, keepdims=True)
            return (x - m) / jnp.sqrt(v + EPS)
        Bx, Nx, C = x.shape
        Sx = context.shape[1]
        mod = jax.nn.silu(t_emb) @ ada_w + ada_b
        shift_sa, scale_sa, gate_sa, shift_ff, scale_ff, gate_ff = [m[:, None, :] for m in jnp.split(mod, 6, axis=-1)]
        xm1 = _ln(x) * (1 + scale_sa) + shift_sa
        qkv = (xm1 @ qkv_w + qkv_b).reshape(Bx, Nx, 3, H, HD)
        q, k, v = (qkv[:, :, 0], qkv[:, :, 1], qkv[:, :, 2])
        attn = jnp.einsum('bnhd,bmhd->bhnm', q, k) * SCALE
        attn = jax.nn.softmax(attn, axis=-1)
        sa = jnp.einsum('bhnm,bmhd->bnhd', attn, v).reshape(Bx, Nx, C)
        sa = sa @ sa_proj_w + sa_proj_b
        x = x + gate_sa * sa
        xn2 = _ln(x)
        qc = (xn2 @ q_w + q_b).reshape(Bx, Nx, H, HD)
        kvc = (context @ kv_w + kv_b).reshape(Bx, Sx, 2, H, HD)
        kc, vc = (kvc[:, :, 0], kvc[:, :, 1])
        attn_c = jnp.einsum('bnhd,bshd->bhns', qc, kc) * SCALE
        attn_c = jnp.where(context_mask[:, None, None, :], -jnp.inf, attn_c)
        attn_c = jax.nn.softmax(attn_c, axis=-1)
        ca = jnp.einsum('bhns,bshd->bnhd', attn_c, vc).reshape(Bx, Nx, C)
        ca = ca @ ca_proj_w + ca_proj_b
        x = x + ca
        xm3 = _ln(x) * (1 + scale_ff) + shift_ff
        h = jax.nn.gelu(xm3 @ fc1_w + fc1_b, approximate=False)
        ff = h @ fc2_w + fc2_b
        x = x + gate_ff * ff
        return x

    def _L3_xcond_ref(x, t_emb, context, adaln_w, adaln_b, qkv_w, qkv_b, sa_proj_w, sa_proj_b, q_w, q_b, kv_w, kv_b, ca_proj_w, ca_proj_b, fc1_w, fc1_b, fc2_w, fc2_b):
        import jax, jax.numpy as jnp
        import numpy as np
        D = 128
        H = 16
        HD = D // H
        MLP = 4 * D
        EPS = 1e-06
        SCALE = HD ** (-0.5)

        def _p(key, shape, s=0.02):
            return jax.random.normal(key, shape, dtype=jnp.float32) * s

        def _ln(x):
            mu = jnp.mean(x, axis=-1, keepdims=True)
            var = jnp.var(x, axis=-1, keepdims=True)
            return (x - mu) * jax.lax.rsqrt(var + EPS)

        def _heads(t):
            B, L, _ = t.shape
            return t.reshape(B, L, H, HD).transpose(0, 2, 1, 3)

        def _attend(q, k, v):
            attn = jnp.einsum('bhnd,bhsd->bhns', q, k) * SCALE
            attn = jax.nn.softmax(attn, axis=-1)
            o = jnp.einsum('bhns,bhsd->bhnd', attn, v)
            B, _, N, _ = q.shape
            return o.transpose(0, 2, 1, 3).reshape(B, N, D)
        B, N, _ = x.shape
        S = context.shape[1]
        mod = jax.nn.silu(t_emb) @ adaln_w + adaln_b
        sh_sa, sc_sa, g_sa, sh_ff, sc_ff, g_ff = jnp.split(mod[:, None, :], 6, axis=-1)
        xm = _ln(x) * (1.0 + sc_sa) + sh_sa
        qkv = (xm @ qkv_w + qkv_b).reshape(B, N, 3, H, HD)
        q = qkv[:, :, 0].transpose(0, 2, 1, 3)
        k = qkv[:, :, 1].transpose(0, 2, 1, 3)
        v = qkv[:, :, 2].transpose(0, 2, 1, 3)
        x_sa = _attend(q, k, v) @ sa_proj_w + sa_proj_b
        x = x + g_sa * x_sa
        xn = _ln(x)
        q = _heads(xn @ q_w + q_b)
        kv = (context @ kv_w + kv_b).reshape(B, S, 2, H, HD)
        k = kv[:, :, 0].transpose(0, 2, 1, 3)
        v = kv[:, :, 1].transpose(0, 2, 1, 3)
        x_ca = _attend(q, k, v) @ ca_proj_w + ca_proj_b
        x = x + x_ca
        xm = _ln(x) * (1.0 + sc_ff) + sh_ff
        h = jax.nn.gelu(xm @ fc1_w + fc1_b, approximate=True)
        x_ff = h @ fc2_w + fc2_b
        x = x + g_ff * x_ff
        return x
    x = _L0_xcond_ref(x, cond_1024, ctx_1024, L0_xcond_W_mod, L0_xcond_b_mod, L0_xcond_W_qkv, L0_xcond_b_qkv, L0_xcond_W_proj, L0_xcond_b_proj, L0_xcond_W_qc, L0_xcond_b_qc, L0_xcond_W_kvc, L0_xcond_b_kvc, L0_xcond_W_cproj, L0_xcond_b_cproj, L0_xcond_W_mlp1, L0_xcond_b_mlp1, L0_xcond_W_mlp2, L0_xcond_b_mlp2)
    x = _L1_xcond_ref(x, cond_1024, ctx_1024, L1_xcond_ada_w, L1_xcond_ada_b, L1_xcond_qkv_w, L1_xcond_qkv_b, L1_xcond_self_o_w, L1_xcond_self_o_b, L1_xcond_norm2_g, L1_xcond_norm2_b, L1_xcond_q_w, L1_xcond_q_b, L1_xcond_kv_w, L1_xcond_kv_b, L1_xcond_cross_o_w, L1_xcond_cross_o_b, L1_xcond_mlp_w1, L1_xcond_mlp_b1, L1_xcond_mlp_w2, L1_xcond_mlp_b2)
    x = _L2_xcond_ref(x, cond_1024, ctx_1024, mask_BxS2_bf0, L2_xcond_ada_w, L2_xcond_ada_b, L2_xcond_qkv_w, L2_xcond_qkv_b, L2_xcond_sa_proj_w, L2_xcond_sa_proj_b, L2_xcond_q_w, L2_xcond_q_b, L2_xcond_kv_w, L2_xcond_kv_b, L2_xcond_ca_proj_w, L2_xcond_ca_proj_b, L2_xcond_fc1_w, L2_xcond_fc1_b, L2_xcond_fc2_w, L2_xcond_fc2_b)
    x = _L3_xcond_ref(x, cond_1024, ctx_1024, L3_xcond_adaln_w, L3_xcond_adaln_b, L3_xcond_qkv_w, L3_xcond_qkv_b, L3_xcond_sa_proj_w, L3_xcond_sa_proj_b, L3_xcond_q_w, L3_xcond_q_b, L3_xcond_kv_w, L3_xcond_kv_b, L3_xcond_ca_proj_w, L3_xcond_ca_proj_b, L3_xcond_fc1_w, L3_xcond_fc1_b, L3_xcond_fc2_w, L3_xcond_fc2_b)
    return x

_drawn_inputs = setup_inputs


def setup_inputs(seed=0):
    import zlib

    import numpy as np

    out = dict(_drawn_inputs(seed))
    spreads = {'L0_xcond_b_mod': (0.0, 0.1),
     'L0_xcond_b_qkv': (0.0, 0.1),
     'L0_xcond_b_proj': (0.0, 0.1),
     'L0_xcond_b_qc': (0.0, 0.554),
     'L0_xcond_b_kvc': (0.0, 0.1),
     'L0_xcond_b_cproj': (0.0, 0.1),
     'L0_xcond_b_mlp1': (0.0, 0.1),
     'L0_xcond_b_mlp2': (0.0, 0.1),
     'L1_xcond_ada_b': (0.0, 0.767),
     'L1_xcond_qkv_b': (0.0, 0.8),
     'L1_xcond_self_o_b': (0.0, 0.723),
     'L1_xcond_norm2_g': (1.0, 0.6),
     'L1_xcond_norm2_b': (0.0, 2.0),
     'L1_xcond_q_b': (0.0, 2.0),
     'L1_xcond_kv_b': (0.0, 1.713),
     'L1_xcond_cross_o_b': (0.0, 0.435),
     'L1_xcond_mlp_b1': (0.0, 0.8),
     'L1_xcond_mlp_b2': (0.0, 0.618),
     'L2_xcond_ada_b': (0.0, 0.8),
     'L2_xcond_qkv_b': (0.0, 0.8),
     'L2_xcond_sa_proj_b': (0.0, 0.735),
     'L2_xcond_q_b': (0.0, 2.0),
     'L2_xcond_kv_b': (0.0, 2.0),
     'L2_xcond_ca_proj_b': (0.0, 0.8),
     'L2_xcond_fc1_b': (0.0, 0.8),
     'L2_xcond_fc2_b': (0.0, 0.684)}
    factors = {'L1_xcond_ada_w': 3.453,
     'L1_xcond_qkv_w': 8.0,
     'L1_xcond_self_o_w': 8.0,
     'L1_xcond_q_w': 29.952,
     'L1_xcond_kv_w': 8.916,
     'L1_xcond_mlp_w1': 8.0,
     'L1_xcond_mlp_w2': 7.648,
     'L2_xcond_ada_w': 3.783,
     'L2_xcond_qkv_w': 8.0,
     'L2_xcond_sa_proj_w': 8.0,
     'L2_xcond_q_w': 64.0,
     'L2_xcond_kv_w': 19.327,
     'L2_xcond_fc1_w': 8.0,
     'L2_xcond_fc2_w': 7.921,
     'L3_xcond_adaln_w': 8.0,
     'L3_xcond_adaln_b': 8.0,
     'L3_xcond_qkv_w': 8.0,
     'L3_xcond_qkv_b': 8.0,
     'L3_xcond_sa_proj_w': 8.0,
     'L3_xcond_sa_proj_b': 33.782,
     'L3_xcond_q_w': 57.432,
     'L3_xcond_q_b': 64.0,
     'L3_xcond_kv_w': 8.544,
     'L3_xcond_kv_b': 61.837,
     'L3_xcond_ca_proj_w': 8.311,
     'L3_xcond_ca_proj_b': 31.568,
     'L3_xcond_fc1_w': 8.0,
     'L3_xcond_fc1_b': 8.0,
     'L3_xcond_fc2_w': 8.0,
     'L3_xcond_fc2_b': 41.785,
     'L2_xcond_ca_proj_w': 4.132}
    for name, (base, spread) in spreads.items():
        noise = np.random.default_rng([zlib.crc32(name.encode()), seed]).standard_normal(out[name].shape)
        drawn = base * np.exp(spread * noise) if base else spread * noise
        out[name] = jnp.asarray(drawn.astype(out[name].dtype))
    for name, factor in factors.items():
        out[name] = (out[name] * factor).astype(out[name].dtype)
    return out
```

```python
from contextlib import ExitStack

import concourse.bass as bass
import numpy as np
from concourse import mybir
from concourse.alu_op_type import AluOpType as ALU

B, N, D, NH, HD, S = 16, 56, 128, 16, 8, 1500
L = 4
T = B * N
HALF = T // 2
KC = 125
NCH = S // KC
TH = 500
PAIR = 2 * N
NP = NH // 2
G, GH = 4, 4
HQ = NH * N
GQ = GH * N
RA = 3 * N
VS = HD + 3
VG = 66
KR = 98
SCALE = float(HD) ** -0.5
EPS = 1e-6
MASKED = 2
NORM_CTX = 0
AFFINE = 1
EXACT_GELU = 2

W1 = {}
for _n, _w in (("mod", 6 * D), ("q", D), ("k", D), ("v", D), ("pA", D), ("pB", D), ("cpA", D), ("cpB", D),
               ("qr", G * 96), ("kc", D), ("vc", D)):
    W1[_n] = (sum(w for _, w in W1.values()), _w)
W1_COLS = sum(w for _, w in W1.values())
W2_COLS = 8 * D
BI = {}
for _n, _w in (("mod", 6), ("q", 1), ("k", 1), ("vA", 1), ("vB", 1), ("cvA", 1), ("cvB", 1), ("p", 1), ("cp", 1),
               ("qr", G), ("kc", 1), ("f1", 4), ("f2", 1), ("g2", 1), ("b2", 1)):
    BI[_n] = (sum(w for _, w in BI.values()), _w)
BI_COLS = sum(w for _, w in BI.values())
CO = {}
for _n, _w in (("mean", D), ("ident", D), ("selA", D), ("selB", D), ("head16", NH), ("head4", GH), ("third", 3),
               ("rows", 4), ("eps", 1)):
    CO[_n] = (sum(w for _, w in CO.values()), _w)
CO_COLS = sum(w for _, w in CO.values())


class PsumUses:

    def __init__(self):
        self.base, self.total = {}, [0, 0, 0]

    def phase(self, name, seq, repeat=1):
        per = [len(range(s, len(seq), 3)) for s in range(3)]
        self.base[name] = (list(self.total), per, {u: i for i, u in enumerate(seq)})
        for s in range(3):
            self.total[s] += per[s] * repeat

    def at(self, phase, use, turn=0):
        base, per, place = self.base[phase]
        i = place[use]
        return i % 3, turn * per[i % 3] + (base[i % 3] + i // 3)


def cross_uses(with_max, with_kv):
    seq = []
    for c in range(NCH):
        if with_max:
            seq.append(f"M{c}")
        seq.append(f"C{c}")
        if with_kv:
            seq += {1: ["K0"], 3: ["K1"], 5: ["V0"], 9: ["V1"]}.get(c, [])
    if with_max:
        seq.append("R")
    if with_kv:
        seq.append("V2")
    return seq


def psum_plan():
    uses = PsumUses()
    uses.phase("ctx_first", ["m0", "m1"])
    uses.phase("ctx", ["m0", "m1", "v0", "v1"], B - 1)
    uses.phase("ctx_last", ["v0", "v1"])
    for l in range(L):
        uses.phase(f"kv0_{l}", ["K0", "K1", "V0", "V1", "V2"])
        uses.phase(f"kv1_{l}", ["K0", "K1", "V0", "V1", "V2"])
        uses.phase(f"A{l}", ["mod", "mean", "var", "q", "k"])
        uses.phase(f"self_first{l}", ["S", "V"])
        uses.phase(f"self{l}", ["S", "V", "T"], B - 1)
        uses.phase(f"self_last{l}", ["T"])
        uses.phase(f"B{l}", ["dA", "dB", "p", "mean", "var", "q0", "q1", "q2", "q3"])
        uses.phase(f"max0_{l}", [f"M{c}" for c in range(NCH)] + ["R"])
        uses.phase(f"cross{l}", cross_uses(True, True), B - 2)
        uses.phase(f"cross14_{l}", cross_uses(True, False))
        uses.phase(f"cross15_{l}", cross_uses(False, False))
        uses.phase(f"C{l}", ["dA", "dB", "p", "mean", "var", "h0", "h1", "h2", "h3", "y"])
    return uses


def stack_dmas(l):
    return 3 * G + (l == MASKED)


def stack_count(l, half):
    return half * (16 * stack_dmas(l)) + 16 * ((B // 2) * sum(stack_dmas(k) for k in range(l)) + stack_dmas(l))


def blocks_kernel(nc, x_d, cond_d, ctx_d, mask_d, w1_d, w2_d, bias_d, const_d, out_d):
    F32, F32R, U8 = mybir.dt.float32, mybir.dt.float32r, mybir.dt.uint8
    ACT, AX = mybir.ActivationFunctionType, mybir.AxisListType
    uses = psum_plan()
    ctx = ExitStack()
    with ctx:
        def sb(name, shape, dt=F32):
            return ctx.enter_context(nc.sbuf_tensor(name, shape, dt))

        def sem(name):
            return ctx.enter_context(nc.semaphore(name))

        ctx_norm_d = nc.dram_tensor("ctx_norm", (B, D, S), F32, kind="Internal").ap()

        w1 = sb("w1", [D, W1_COLS])
        w2 = sb("w2", [D, W2_COLS])
        bias = sb("bias", [D, L * BI_COLS])
        const = sb("const", [D, CO_COLS])
        cond = sb("cond", [D, B])
        silu = sb("silu", [D, B])
        x = sb("x", [D, T])
        norm_work = sb("norm_work", [D, 4 * T])
        xc = norm_work[:, 0:T]
        sq = norm_work[:, T:2 * T]
        rstd = norm_work[:, 2 * T:3 * T]
        xn = norm_work[:, 3 * T:4 * T]
        qk = sb("qk", [D, 2 * T])
        qT, kT = qk[:, 0:T], qk[:, T:2 * T]
        mod = sb("mod", [D, 6, B])
        proj_bias = sb("proj_bias", [D, 2])
        work = sb("work", [D, 4 * T])
        hidden = [work[:, j * T:(j + 1) * T] for j in range(4)]
        q_blocks = [work[:, 0:HQ], work[:, HQ:2 * HQ]]
        probs_T = [work[0:N, 2 * HQ:3 * HQ], work[0:N, 3 * HQ:4 * HQ]]
        probs_self = [sq[0:PAIR, 0:NP * N], sq[0:PAIR, NP * N:2 * NP * N]]
        x_batch = sb("x_batch", [D, 2, N])
        v_self = sb("v_self", [N, 2, G, VG])
        heads_a = sb("heads_a", [D, T])
        heads_b = sb("heads_b", [D, T])
        masked = sb("masked", [D, 3, N])
        part_max = sb("part_max", [PAIR, 3, NP])
        neg_max = sb("neg_max", [PAIR, NP])
        neg_max_self = sb("neg_max_self", [PAIR, NP])
        ctx_T = sb("ctx_T", [D, 2, S])
        k_hi = sb("k_hi", [D, S], F32R)
        k_lo = sb("k_lo", [D, S], F32R)
        ctx_centred = [t[:, :].bitcast(F32) for t in (k_hi, k_lo)]
        ctx_squares = [work[:, 0:S], work[:, 2 * T:2 * T + S]]
        deviation = qk[:, 0:S]
        ctx_out = [norm_work[:, 0:S], norm_work[:, 2 * T:2 * T + S]]
        k_stack = [sb(f"k_stack{i}", [KR, G, S], F32R) for i in range(2)]
        q_split = sb("q_split", [96, G, T], F32R)
        q_max = [sb(f"q_max{i}", [KR, HQ], F32R) for i in range(2)]
        q_score = [sb(f"q_score{i}", [KR, HQ], F32R) for i in range(2)]
        v_ctx = [sb(f"v_ctx{i}", [KC, NCH, G, VG]) for i in range(2)]
        probs = sb("probs", [KC, 3, HQ])
        mask_u8 = sb("mask_u8", [97, S], U8)
        mask_row = sb("mask_row", [97, S], F32R)

        slot = [ctx.enter_context(nc.psum_tensor(f"slot{i}", [D, 2, 512], F32)) for i in range(3)]
        acc_a = ctx.enter_context(nc.psum_tensor("acc_a", [D, 512], F32))
        acc_b = ctx.enter_context(nc.psum_tensor("acc_b", [D, 512], F32))

        psum_full = [sem(f"psum_full{i}") for i in range(3)]
        psum_free = [sem(f"psum_free{i}") for i in range(3)]
        const_loaded, x_loaded, w1_loaded, w2_loaded = sem("const_loaded"), sem("x_loaded"), sem("w1_loaded"), sem("w2_loaded")
        raw_loaded = [sem(f"raw_loaded{i}") for i in range(2)]
        norm_stored = [sem(f"norm_stored{i}") for i in range(2)]
        ctx_loaded = [sem(f"ctx_loaded{i}") for i in range(2)]
        stack_loaded = [[sem(f"stack_loaded{i}_{k}") for k in range(3)] for i in range(2)]
        mask_loaded, mask_row_ready = sem("mask_loaded"), sem("mask_row_ready")
        ctx_squared, ctx_rstd, ctx_normed = sem("ctx_squared"), sem("ctx_rstd"), sem("ctx_normed")
        exp_cond, silu_ready = sem("exp_cond"), sem("silu_ready")
        x_squared, rstd_ready, xn_ready, x_ready = sem("x_squared"), sem("rstd_ready"), sem("xn_ready"), sem("x_ready")
        heads_ready, qhi_ready = sem("heads_ready"), sem("qhi_ready")
        self_operands, self_probs, self_done = sem("self_operands"), sem("self_probs"), sem("self_done")
        hi_ready, qmax_ready, qscore_ready, self_max = sem("hi_ready"), sem("qmax_ready"), sem("qscore_ready"), sem("self_max")
        max_ready, shift_ready, probs_used, acc_free = sem("max_ready"), sem("shift_ready"), sem("probs_used"), sem("acc_free")
        waits_met = sem("waits_met")
        pool_init, rows_init, dve_step, stored = sem("pool_init"), sem("rows_init"), sem("dve_step"), sem("stored")

        block = ctx.enter_context(nc.Block())

        def W(name, a=0, b=None):
            o, w = W1[name]
            return w1[:, o + a:o + (w if b is None else b)]

        def bi(l, name, n=0, rows=slice(0, D), width=1):
            o = l * BI_COLS + BI[name][0] + n
            return bias[rows, o:o + width]

        def co(name, rows=slice(0, D)):
            o, w = CO[name]
            return const[rows, o:o + w]

        def full(e, phase, use, turn=0):
            s, n = uses.at(phase, use, turn)
            e.wait_ge(psum_full[s], n + 1)
            return slot[s]

        def freed(e, phase, use, turn=0):
            s, n = uses.at(phase, use, turn)
            e.wait_ge(psum_free[s], n + 2)

        def claim(pe, phase, use, turn=0):
            s, n = uses.at(phase, use, turn)
            pe.wait_ge(psum_free[s], n + 1)
            return slot[s]

        def wait_alone(e, semaphore, count):
            e.wait_ge(semaphore, count)
            if not isinstance(count, int):
                e.sem_inc(waits_met, 1)

        def slot_free(phase, use):
            return psum_free[uses.at(phase, use)[0]]

        def slot_full(phase, use):
            return psum_full[uses.at(phase, use)[0]]

        def halves(t, rows=slice(0, D)):
            return t[rows, :, 0:HALF]

        def two(t):
            return t.rearrange("p (a n) -> p a n", a=2)

        def by_batch(t):
            return t.rearrange("p (b n) -> p b n", n=N)

        def per_token(m, nb=B):
            return m.unsqueeze(2).to_broadcast([D, nb, N])

        def thirds(part):
            return (0, 2) if part[1] == "0" else (2, 1)

        def keys(t, part):
            s0, ns = thirds(part)
            return t[:, s0 * TH:(s0 + ns) * TH].rearrange("p (a n) -> p a n", n=TH)

        def value_columns(v):
            return v[:, :, 0:GH * VS].rearrange("p a (t v) -> p a t v", v=VS)[:, :, :, 0:HD]

        def turns(e, body, last):
            with e.Fori(0, (B - 2) // 2, 1) as i:
                body(i * 2, 0, i)
                body(i * 2 + 1, 1, i + 0)
            last()

        @block.sync
        def _(sp):
            sp.dma_start(const[:, :], const_d).then_inc(const_loaded, 16)
            sp.dma_start(bias[:, :], bias_d).then_inc(const_loaded, 16)
            sp.dma_start(cond[:, :], cond_d).then_inc(const_loaded, 16)
            for p in range(2):
                sp.dma_start(ctx_T[:, p, :], ctx_d[p]).then_inc(raw_loaded[p], 16)
            sp.dma_start(x[:, :], x_d).then_inc(x_loaded, 16)
            sp.dma_start(w1[:, :], w1_d[0]).then_inc(w1_loaded, 16)
            sp.dma_start(w2[:, :], w2_d[0]).then_inc(w2_loaded, 16)

            def store_norm(b, p):
                wait_alone(sp, ctx_normed, b + 2)
                sp.dma_start(ctx_norm_d[bass.ds(b, 1)].rearrange("o d s -> (o d) s"), ctx_out[p])\
                    .then_inc(norm_stored[p], 16)

            def ctx_turn(b, p):
                s, n = uses.at("ctx", "m1", b)
                wait_alone(sp, psum_free[s], n + 2)
                sp.dma_start(ctx_T[:, 1 - p, :], ctx_d[bass.ds(b + 3, 1)].rearrange("o d s -> (o d) s"))\
                    .then_inc(raw_loaded[1 - p], 16)
                store_norm(b, p)

            freed(sp, "ctx_first", "m1")
            sp.dma_start(ctx_T[:, 0, :], ctx_d[2]).then_inc(raw_loaded[0], 16)
            with sp.Fori(0, (B - 4) // 2, 1) as i:
                ctx_turn(i * 2, 0)
                ctx_turn(i * 2 + 1, 1)
            ctx_turn(B - 4, 0)
            for b in range(B - 3, B):
                store_norm(b, b % 2)
            for p in range(2):
                sp.wait_ge(norm_stored[p], 16 * (B // 2 + 1))

            def load_ctx(l, b, p):
                src = ctx_norm_d if l == NORM_CTX else ctx_d
                sp.dma_start(ctx_T[:, p, :], src[bass.ds(b, 1)].rearrange("o d s -> (o d) s"))\
                    .then_inc(ctx_loaded[p], 16)

            def load_mask(b, before):
                if before:
                    wait_alone(sp, mask_row_ready, b)
                sp.dma_start(mask_u8[96:97, :].bitcast(mybir.dt.int32), mask_d[bass.ds(b, 1)]).then_inc(mask_loaded, 16)

            def place(l, b, p, k, phase, turn):
                n = slice(k * TH, (k + 1) * TH)
                s, count = uses.at(phase, "K0" if k < 2 else "K1", turn)
                wait_alone(sp, psum_free[s], count + 2)
                for g in range(G):
                    rows = slice(32 * g, 32 * g + 32)
                    for at, part in ((0, k_hi), (32, k_lo), (64, k_hi)):
                        sp.dma_start(k_stack[p][at:at + 32, g, n].bitcast(F32), part[rows, n].bitcast(F32)).then_inc(stack_loaded[p][k], 16)
                if l == MASKED:
                    if k == 0:
                        sp.wait_ge(mask_row_ready, b + 1)
                    sp.dma_start(k_stack[p][96:97, :, n].bitcast(F32),
                                 mask_row[96:97, n].bitcast(F32).unsqueeze(1).to_broadcast([1, G, TH]))\
                        .then_inc(stack_loaded[p][k], 16)

            for l in range(L):
                if l > 0:
                    freed(sp, f"cross{l - 1}", "V2", B - 3)
                for p in range(2):
                    load_ctx(l, p, p)
                if l > 0:
                    sp.wait_ge(x_ready, 3 * (l - 1) + 2)
                    sp.dma_start(w1[:, :], w1_d[l]).then_inc(w1_loaded, 16)
                    sp.wait_ge(x_ready, 3 * l)
                    sp.dma_start(w2[:, :], w2_d[l]).then_inc(w2_loaded, 16)
                for b in range(2):
                    if l == MASKED:
                        load_mask(b, b > 0)
                    for k in range(3):
                        place(l, b, b, k, f"kv{b}_{l}", 0)
                    freed(sp, f"kv{b}_{l}", "V2")
                    load_ctx(l, b + 2, b)

                def cross_turn(b, p, more, l=l):
                    if l == MASKED:
                        load_mask(b + 2, True)
                    for k in range(3):
                        s, n = uses.at(f"cross{l}", f"C{4 * k + 3}", b)
                        wait_alone(sp, psum_free[s], n + 2)
                        place(l, b + 2, p, k, f"cross{l}", b)
                    if more:
                        s, n = uses.at(f"cross{l}", "V2", b)
                        wait_alone(sp, psum_free[s], n + 2)
                        load_ctx(l, b + 4, p)

                with sp.Fori(0, (B - 4) // 2, 1) as i:
                    cross_turn(i * 2, 0, True)
                    cross_turn(i * 2 + 1, 1, True)
                cross_turn(B - 4, 0, False)
                cross_turn(B - 3, 1, False)
            sp.wait_ge(x_ready, 3 * L)
            sp.dma_start(out_d, x[:, :]).then_inc(stored, 16)
            sp.wait_ge(stored, 16)

        @block.gpsimd
        def _(pool):
            for i in range(2):
                pool.memset(v_ctx[i][:, :, :, :], 0.0).then_inc(pool_init, 1)
            pool.memset(v_self[:, :, :, :], 0.0).then_inc(pool_init, 1)
            pool.wait_ge(pool_init, 3)
            for t in range(GH):
                c = VS * t + HD
                for i in range(2):
                    pool.memset(v_ctx[i][:, :, :, c:c + 1], 1.0).then_inc(pool_init, 1)
                pool.memset(v_self[:, :, :, c:c + 1], 1.0).then_inc(pool_init, 1)
            pool.wait_ge(const_loaded, 48)

            def make_mask_row(l, b, p):
                pool.wait_ge(mask_loaded, b * 16 + 16)
                for k in range(3):
                    wait_alone(pool, stack_loaded[1 - p][k], mask_placed(b, p))
                pool.tensor_scalar(mask_row[96:97, :], mask_u8[96:97, :], -1e38, 1e38, ALU.mult, ALU.mult)\
                    .then_inc(mask_row_ready, 1)
                wait_alone(pool, mask_row_ready, b + 1)

            def mask_placed(b, p):
                per = 16 * stack_dmas(MASKED)
                base = stack_count(MASKED, 0) - per
                return (b * (per // 2) + base) if p == 0 else (b * (per // 2) + (base + per // 2))

            def self_operands_of(b, p):
                at = bass.ds(b * N, N)
                pool.tensor_tensor(out=by_batch(q_blocks[p]), in0=qT[:, at].unsqueeze(1).to_broadcast([D, NH, N]),
                                   in1=co("head16").unsqueeze(2).to_broadcast([D, NH, N]), op=ALU.mult)\
                    .then_inc(self_operands, 1)
                pool.tensor_copy(x_batch[:, p, :], xn[:, at]).then_inc(self_operands, 1)

            def expand(dst, b):
                for g in range(G):
                    last = pool.tensor_tensor(
                        out=by_batch(dst[0:96, g * GQ:(g + 1) * GQ]),
                        in0=q_split[:, g, bass.ds(b * N, N)].bitcast(F32).unsqueeze(1).to_broadcast([96, GH, N]),
                        in1=co("head4", slice(0, 96)).unsqueeze(2).to_broadcast([96, GH, N]), op=ALU.mult)
                return last

            for l in range(L):
                if l == MASKED:
                    for b in range(2):
                        make_mask_row(l, b, b)
                freed(pool, f"A{l}", "k")
                self_operands_of(0, 0)
                self_operands_of(1, 1)

                def self_turn(b, p, i, l=l):
                    wait_alone(pool, self_done, b + (B * l + 2))
                    self_operands_of(b + 2, p)

                turns(pool, self_turn, lambda: None)

                freed(pool, f"B{l}", "q3")
                expand(q_max[0], 0).then_inc(qmax_ready, 1)
                expand(q_score[0], 0).then_inc(qscore_ready, 1)
                expand(q_max[1], 1).then_inc(qmax_ready, 1)

                def next_scores(b, p, l=l):
                    wait_alone(pool, probs_used, b * NCH + (NCH * B * l + 3))
                    expand(q_score[1 - p], b + 1).then_inc(qscore_ready, 1)

                def cross_turn(b, p, i, l=l):
                    next_scores(b, p)
                    wait_alone(pool, max_ready, b + (B * l + 1))
                    expand(q_max[p], b + 2).then_inc(qmax_ready, 1)
                    if l == MASKED:
                        make_mask_row(l, b + 2, p)

                turns(pool, cross_turn, lambda: next_scores(B - 2, 0))

        @block.scalar
        def _(act):
            act.wait_ge(const_loaded, 48)
            eps = co("eps")
            act.preload_act_table_set("natural_log_exp_and_others")
            act.activation(silu[:, :], cond[:, :], ACT.Exp, scale=-1.0).then_inc(exp_cond, 1)

            def ctx_square(p):
                act.activation(ctx_squares[p], ctx_centred[p], ACT.Square).then_inc(ctx_squared, 1)

            def ctx_deviation(phase, turn):
                for part in ("v0", "v1"):
                    t = full(act, phase, part, turn)
                    act.activation(keys(deviation, part), t[:, 0:thirds(part)[1], 0:TH], ACT.Ln, bias=eps)\
                        .then_inc(slot_free(phase, part), 1)
                for part in ("v0", "v1"):
                    freed(act, phase, part, turn)
                act.activation(deviation, deviation, ACT.Exp, scale=-0.5).then_inc(ctx_rstd, 1)

            def ctx_turn(b, p, i):
                freed(act, "ctx", "m1", b)
                ctx_square(1 - p)
                act.wait_ge(ctx_normed, b + 1)
                ctx_deviation("ctx", b)

            def ctx_end():
                ctx_turn(B - 2, 0, 7)
                act.wait_ge(ctx_normed, B)
                ctx_deviation("ctx_last", 0)

            freed(act, "ctx_first", "m1")
            ctx_square(0)
            turns(act, ctx_turn, ctx_end)

            def norm(phase, k):
                freed(act, phase, "mean")
                act.activation(sq[:, :], xc[:, :], ACT.Square).then_inc(x_squared, 1)
                t = full(act, phase, "var")
                act.activation(two(rstd[:, :]), halves(t), ACT.Ln, bias=eps).then_inc(slot_free(phase, "var"), 1)
                freed(act, phase, "var")
                act.activation(rstd[:, :], rstd[:, :], ACT.Exp, scale=-0.5).then_inc(rstd_ready, 1)

            def keys_high(phase, turn, l, b, p, part):
                t = full(act, phase, part, turn)
                s0, ns = thirds(part)
                if b is not None:
                    for k in range(s0, s0 + ns):
                        act.wait_ge(stack_loaded[1 - p][k], b)
                act.activation(keys(k_hi, part), t[:, 0:ns, 0:TH], ACT.Identity, bias=bi(l, "kc")).then_inc(hi_ready, 1)

            def values(phase, turn, p, part):
                t = full(act, phase, part, turn)
                k = int(part[1])
                act.activation(value_columns(v_ctx[p][:, 4 * k:4 * k + 4, :, :].rearrange("p c g v -> p (c g) v")),
                               t[0:KC, 0, 0:4 * D].rearrange("p (a t d) -> p a t d", t=GH, d=HD), ACT.Copy)\
                    .then_inc(slot_free(phase, part), 1)

            def exps(phase, turn, c, n):
                t = full(act, phase, f"C{c}", turn)
                act.wait_ge(probs_used, n + 1)
                act.activation(two(probs[:, c % 3, :]), t[0:KC, :, 0:HALF], ACT.Exp, scale=SCALE)\
                    .then_inc(slot_free(phase, f"C{c}"), 1)

            act.wait_ge(pool_init, 3 + 3 * GH)
            for l in range(L):
                for b in range(2):
                    for part in ("K0", "K1"):
                        before = None if l == 0 and b == 0 else stack_count(l, b // 2) if b else stack_count(l - 1, 7)
                        keys_high(f"kv{b}_{l}", 0, l, before, b, part)
                    for part in ("V0", "V1", "V2"):
                        values(f"kv{b}_{l}", 0, b, part)
                norm(f"A{l}", 3 * l)
                for part, dst in (("q", qT), ("k", kT)):
                    t = full(act, f"A{l}", part)
                    act.activation(two(dst[:, :]), halves(t), ACT.Identity, bias=bi(l, part))\
                        .then_inc(slot_free(f"A{l}", part), 1)

                def self_exp(phase, turn, p):
                    freed(act, phase, "S", turn)
                    act.activation(probs_self[p], probs_self[p], ACT.Exp, scale=SCALE).then_inc(self_probs, 1)

                def self_values(phase, turn, p):
                    t = full(act, phase, "V", turn)
                    act.activation(value_columns(v_self[:, p, :, :]),
                                   t[0:N, 0, 0:D].rearrange("p (a t d) -> p a t d", t=GH, d=HD), ACT.Copy)\
                        .then_inc(slot_free(phase, "V"), 1)

                def self_transposed(phase, turn, p):
                    t = full(act, phase, "T", turn)
                    act.activation(two(probs_T[p]), halves(t, slice(0, N)), ACT.Copy).then_inc(slot_free(phase, "T"), 1)

                def self_turn(b, p, i, l=l):
                    self_values(f"self{l}", b, 1 - p)
                    self_transposed(f"self{l}", b, p)
                    self_exp(f"self{l}", b, 1 - p)

                def self_end(l=l):
                    self_turn(B - 2, 0, 7)
                    self_transposed(f"self_last{l}", 0, 1)

                self_values(f"self_first{l}", 0, 0)
                self_exp(f"self_first{l}", 0, 0)
                turns(act, self_turn, self_end)
                norm(f"B{l}", 3 * l + 1)
                for g in range(G):
                    t = full(act, f"B{l}", f"q{g}")
                    act.activation(two(q_split[:, g, :]), halves(t, slice(0, 96)), ACT.Identity,
                                   bias=bi(l, "qr", g, slice(0, 96))).then_inc(qhi_ready, 1)

                def cross_turn(phase, turn, b, p, kv, l=l):
                    for use in cross_uses(kv is not None, kv is not None):
                        if use[0] == "C":
                            c = int(use[1:])
                            exps(phase, turn, c, b * NCH + (NCH * B * l + c))
                        elif use[0] == "K":
                            keys_high(phase, turn, l, kv, p, use)
                        elif use[0] == "V":
                            k = int(use[1])
                            act.wait_ge(probs_used, b * NCH + (NCH * B * l + 4 * (k + 1) + 3))
                            values(phase, turn, p, use)

                def turn(b, p, i, l=l):
                    cross_turn(f"cross{l}", b, b, p, i * (16 * stack_dmas(l)) + (stack_count(l, 0) + (16 * stack_dmas(l) if p else 0)))

                def end(l=l):
                    cross_turn(f"cross14_{l}", 0, B - 2, 0, None)
                    cross_turn(f"cross15_{l}", 0, B - 1, 1, None)

                turns(act, turn, end)
                norm(f"C{l}", 3 * l + 2)
                for j in range(4):
                    t = full(act, f"C{l}", f"h{j}")
                    act.activation(two(hidden[j]), halves(t), ACT.Gelu if l == EXACT_GELU else ACT.Gelu_apprx_tanh,
                                   bias=bi(l, "f1", j)).then_inc(slot_free(f"C{l}", f"h{j}"), 1)
                if l < L - 1:
                    act.preload_act_table_set("natural_log_exp_and_others")

        @block.vector
        def _(dve):
            steps = [0]

            def step(ins):
                steps[0] += 1
                ins.then_inc(dve_step, 1)
                dve.wait_ge(dve_step, steps[0])

            dve.wait_ge(const_loaded, 48)
            rows = slice(96, KR)
            k_rows, q_rows, shift_rows = (const[rows, CO["rows"][0] + j:CO["rows"][0] + j + 1] for j in range(3))

            def fill_key_rows():
                for i in range(2):
                    dve.tensor_copy(k_stack[i][rows, :, :].rearrange("p g n -> p (g n)"), k_rows.to_broadcast([2, G * S]))\
                        .then_inc(rows_init, 1)

            fill_key_rows()
            for i in range(2):
                dve.tensor_copy(q_max[i][rows, :], q_rows.to_broadcast([2, HQ])).then_inc(rows_init, 1)

            dve.wait_ge(exp_cond, 1)
            step(dve.tensor_scalar(silu[:, :], silu[:, :], 1.0, None, ALU.add))
            step(dve.reciprocal(silu[:, :], silu[:, :]))
            dve.tensor_tensor(out=silu[:, :], in0=silu[:, :], in1=cond[:, :], op=ALU.mult).then_inc(silu_ready, 1)

            def ctx_centre(phase, turn, p):
                for part in ("m0", "m1"):
                    t = full(dve, phase, part, turn)
                    dve.tensor_tensor(out=keys(ctx_centred[p], part), in0=keys(ctx_T[:, p, :], part), in1=t[:, 0:thirds(part)[1], 0:TH], op=ALU.subtract)\
                        .then_inc(slot_free(phase, part), 1)

            def ctx_divide(b, p, half):
                dve.wait_ge(norm_stored[p], half * 16 + 16)
                dve.wait_ge(ctx_rstd, b + 1)
                dve.tensor_tensor(out=ctx_out[p], in0=ctx_centred[p], in1=deviation, op=ALU.mult)\
                    .then_inc(ctx_normed, 1)

            def ctx_turn(b, p, i):
                dve.wait_ge(ctx_normed, b + 1)
                ctx_centre("ctx", b, 1 - p)
                ctx_divide(b, p, i)

            def ctx_end():
                ctx_turn(B - 2, 0, 7)
                ctx_divide(B - 1, 1, 7)

            ctx_centre("ctx_first", 0, 0)
            turns(dve, ctx_turn, ctx_end)

            def norm(phase, l, k, which):
                t = full(dve, phase, "mean")
                dve.tensor_tensor(out=two(xc[:, :]), in0=two(x[:, :]), in1=halves(t), op=ALU.subtract)\
                    .then_inc(slot_free(phase, "mean"), 1)
                dve.wait_ge(rstd_ready, k + 1)
                ins = dve.tensor_tensor(out=xn[:, :], in0=xc[:, :], in1=rstd[:, :], op=ALU.mult)
                if which in (0, 2):
                    step(ins)
                    scale, shift = (mod[:, 1, :], mod[:, 0, :]) if which == 0 else (mod[:, 4, :], mod[:, 3, :])
                    step(dve.tensor_tensor(out=by_batch(xn[:, :]), in0=by_batch(xn[:, :]), in1=per_token(scale), op=ALU.mult))
                    ins = dve.tensor_tensor(out=by_batch(xn[:, :]), in0=by_batch(xn[:, :]), in1=per_token(shift), op=ALU.add)
                elif l == AFFINE:
                    step(ins)
                    ins = dve.tensor_scalar(xn[:, :], xn[:, :], bi(l, "g2"), bi(l, "b2"), ALU.mult, ALU.add)
                ins.then_inc(xn_ready, 1)

            def gated(phase, use, b_ap, gate):
                t = full(dve, phase, use)
                for h in range(2):
                    ins = dve.scalar_tensor_tensor(out=by_batch(xn[:, h * HALF:(h + 1) * HALF]), in0=by_batch(t[:, h, 0:HALF]),
                                                   scalar=b_ap, in1=per_token(gate[:, h * 8:(h + 1) * 8], 8),
                                                   op0=ALU.add, op1=ALU.mult)
                    if h == 0:
                        step(ins)
                ins.then_inc(slot_free(phase, use), 1)
                freed(dve, phase, use)
                dve.tensor_tensor(out=x[:, :], in0=x[:, :], in1=xn[:, :], op=ALU.add).then_inc(x_ready, 1)

            def normalise_heads(phase):
                for use, den, heads, dst in (("dA", rstd, heads_a, qT), ("dB", sq, heads_b, kT)):
                    t = full(dve, phase, use)
                    dve.reciprocal(two(den[:, :]), halves(t)).then_inc(slot_free(phase, use), 1)
                    freed(dve, phase, use)
                    dve.tensor_tensor(out=dst[:, :], in0=heads[:, :], in1=den[:, :], op=ALU.mult).then_inc(heads_ready, 1)

            masks3 = co("third").unsqueeze(2).to_broadcast([D, 3, N])
            extracted = [0]

            def extract(b, count):
                dve.tensor_tensor(out=masked[:, :, :], in0=acc_a[:, 0:RA].rearrange("p (t n) -> p t n", n=N), in1=masks3,
                                  op=ALU.mult).then_inc(acc_free, 1)
                dve.wait_ge(acc_free, count)
                at = bass.ds(b * N, N)
                dve.tensor_reduce(out=heads_a[:, at], in_=masked[:, :, :].rearrange("p t n -> p n t"), axis=AX.X, op=ALU.add)\
                    .then_inc(acc_free, 1)
                dve.tensor_copy(heads_b[:, at], acc_b[:, 0:N]).then_inc(acc_free, 1)

            def reduce_tile(phase, turn, c):
                t = full(dve, phase, f"M{c}", turn)
                pair = 2 * (c % 4)
                dve.reduce_max(part_max[:, c // 4, pair:pair + 2], t[0:PAIR, :, 0:TH], AX.X)\
                    .then_inc(slot_free(phase, f"M{c}"), 1)

            def shift(phase, turn, b, p, count):
                freed(dve, phase, f"M{NCH - 1}", turn)
                dve.tensor_reduce(out=neg_max[:, :], in_=part_max[:, :, :].rearrange("q s p -> q p s"), axis=AX.X, op=ALU.max,
                                  negate=True).then_inc(max_ready, 1)
                t = full(dve, phase, "R", turn)
                dve.tensor_scalar(two(q_score[p][rows, :]), t[rows, :, 0:HALF], shift_rows, q_rows, ALU.mult, ALU.add)\
                    .then_inc(slot_free(phase, "R"), 1)

            def keys_low(phase, turn, l, part, count):
                dve.wait_ge(hi_ready, count)
                s0, ns = thirds(part)
                s, _ = uses.at(phase, part)
                dve.scalar_tensor_tensor(out=keys(k_lo, part), in0=slot[s][:, 0:ns, 0:TH], scalar=bi(l, "kc"),
                                         in1=keys(k_hi[:, :].bitcast(F32), part), op0=ALU.add, op1=ALU.subtract)\
                    .then_inc(slot_free(phase, part), 1)

            for l in range(L):
                if l == MASKED + 1:
                    fill_key_rows()
                for b in range(2):
                    for n, part in enumerate(("K0", "K1")):
                        keys_low(f"kv{b}_{l}", 0, l, part, 2 * (B * l + b) + n + 1)
                t = full(dve, f"A{l}", "mod")
                step(dve.tensor_tensor(out=mod[:, :, :], in0=t[:, 0, 0:6 * B].rearrange("p (k b) -> p k b", b=B),
                                       in1=bi(l, "mod", width=6).unsqueeze(2).to_broadcast([D, 6, B]), op=ALU.add))
                for k in (1, 4):
                    step(dve.tensor_scalar(mod[:, k, :], mod[:, k, :], 1.0, None, ALU.add))
                dve.tensor_tensor(out=proj_bias[:, :], in0=t[:, 0, 6 * B:6 * B + 2], in1=bi(l, "p", width=2), op=ALU.add)\
                    .then_inc(slot_free(f"A{l}", "mod"), 1)
                norm(f"A{l}", l, 3 * l, 0)

                def self_shift(phase, turn, p, ready):
                    t = full(dve, phase, "S", turn)
                    dve.wait_ge(self_done, ready)
                    scores = by_batch(t[0:PAIR, 0, 0:NP * N])
                    dve.tensor_reduce(out=neg_max_self[:, :], in_=scores, axis=AX.X, op=ALU.max, negate=True)\
                        .then_inc(self_max, 1)
                    return scores

                def self_less(phase, scores, p):
                    dve.tensor_tensor(out=by_batch(probs_self[p]), in0=scores,
                                      in1=neg_max_self[:, :].unsqueeze(2).to_broadcast([PAIR, NP, N]), op=ALU.add)\
                        .then_inc(slot_free(phase, "S"), 1)

                def self_turn(b, p, i, l=l):
                    scores = self_shift(f"self{l}", b, 1 - p, b + (B * l + 1))
                    dve.wait_ge(self_max, b + (B * l + 2))
                    self_less(f"self{l}", scores, 1 - p)
                    dve.wait_ge(self_done, b + (B * l + 2))
                    extract(b, b * 3 + (3 * 2 * B * l + 4))

                def self_end(l=l):
                    self_turn(B - 2, 0, 7)
                    dve.wait_ge(self_done, B * (l + 1) + 1)
                    extract(B - 1, 3 * (2 * B * l + B - 1) + 4)

                scores = self_shift(f"self_first{l}", 0, 0, B * l + 1)
                dve.wait_ge(self_max, B * l + 1)
                self_less(f"self_first{l}", scores, 0)
                turns(dve, self_turn, self_end)
                normalise_heads(f"B{l}")
                gated(f"B{l}", "p", proj_bias[:, 0:1], mod[:, 2, :])
                norm(f"B{l}", l, 3 * l + 1, 1)
                for g in range(G):
                    t = full(dve, f"B{l}", f"q{g}")
                    dve.wait_ge(qhi_ready, G * l + g + 1)
                    low = two(q_split[64:96, g, :])
                    dve.scalar_tensor_tensor(out=low, in0=halves(t, slice(64, 96)), scalar=bi(l, "qr", g, slice(64, 96)),
                                             in1=two(q_split[64:96, g, :].bitcast(F32)), op0=ALU.add, op1=ALU.subtract)\
                        .then_inc(slot_free(f"B{l}", f"q{g}"), 1)
                for c in range(NCH):
                    reduce_tile(f"max0_{l}", 0, c)
                shift(f"max0_{l}", 0, 0, 0, B * l + 1)

                def cross_turn(phase, turn, b, p, with_max, hi, l=l):
                    for use in cross_uses(with_max, hi is not None):
                        if use[0] == "M":
                            reduce_tile(phase, turn, int(use[1:]))
                        elif use[0] == "K":
                            keys_low(phase, turn, l, use, hi + int(use[1]))
                    if with_max:
                        shift(phase, turn, b + 1, 1 - p, b + (B * l + 2))
                    dve.wait_ge(probs_used, b * NCH + (NCH * (B * l + 1) + 3))
                    extract(b, b * 3 + (3 * (2 * B * l + B) + 4))

                def turn(b, p, i, l=l):
                    cross_turn(f"cross{l}", b, b, p, True, b * 2 + (2 * (B * l + 2) + 1))

                def end(l=l):
                    cross_turn(f"cross14_{l}", 0, B - 2, 0, True, None)
                    cross_turn(f"cross15_{l}", 0, B - 1, 1, False, None)

                turns(dve, turn, end)
                normalise_heads(f"C{l}")
                t = full(dve, f"C{l}", "p")
                dve.scalar_tensor_tensor(out=two(xn[:, :]), in0=halves(t), scalar=proj_bias[:, 1:2], in1=two(x[:, :]),
                                         op0=ALU.add, op1=ALU.add).then_inc(slot_free(f"C{l}", "p"), 1)
                freed(dve, f"C{l}", "p")
                dve.tensor_copy(x[:, :], xn[:, :]).then_inc(x_ready, 1)
                norm(f"C{l}", l, 3 * l + 2, 2)
                gated(f"C{l}", "y", bi(l, "f2"), mod[:, 5, :])

        @block.tensor
        def _(pe):
            for i in range(3):
                pe.sem_inc(psum_free[i], 1)
            pe.sem_inc(probs_used, 3)
            pe.sem_inc(acc_free, 3)
            pe.sem_inc(self_done, 1)
            pe.sem_inc(ctx_normed, 1)
            for p in range(2):
                pe.sem_inc(norm_stored[p], 16)
            pe.wait_ge(const_loaded, 48)

            def ctx_sum(phase, turn, parts, src):
                for part in parts:
                    t = claim(pe, phase, part, turn)
                    s0, ns = thirds(part)
                    for a in range(ns):
                        mm = pe.matmul(t[:, a, 0:TH], co("mean"), src[:, (s0 + a) * TH:(s0 + a + 1) * TH], start=True, stop=True)
                    mm.then_inc(slot_full(phase, part), 1)

            def ctx_turn(b, p, i):
                pe.wait_ge(raw_loaded[1 - p], i * 16 + 16 * (1 + p))
                ctx_sum("ctx", b, ("m0", "m1"), ctx_T[:, 1 - p, :])
                pe.wait_ge(ctx_squared, b + 1)
                ctx_sum("ctx", b, ("v0", "v1"), ctx_squares[p])

            def ctx_end():
                ctx_turn(B - 2, 0, 7)
                pe.wait_ge(ctx_squared, B)
                ctx_sum("ctx_last", 0, ("v0", "v1"), ctx_squares[1])

            pe.wait_ge(raw_loaded[0], 16)
            ctx_sum("ctx_first", 0, ("m0", "m1"), ctx_T[:, 0, :])
            turns(pe, ctx_turn, ctx_end)

            def dense(phase, use, terms, rows=D):
                t = claim(pe, phase, use)
                for a in range(2):
                    for n, (lhsT, rhs) in enumerate(terms):
                        mm = pe.matmul(t[0:rows, a, 0:HALF], lhsT, rhs[:, a * HALF:(a + 1) * HALF], start=(n == 0),
                                       stop=(n == len(terms) - 1))
                mm.then_inc(slot_full(phase, use), 1)

            def norm(phase, k):
                if k == 0:
                    pe.wait_ge(x_loaded, 16)
                else:
                    pe.wait_ge(x_ready, k)
                dense(phase, "mean", [(co("mean"), x)])
                pe.wait_ge(x_squared, k + 1)
                dense(phase, "var", [(co("mean"), sq)])
                pe.wait_ge(xn_ready, k + 1)

            def keys_product(phase, turn, p, part):
                t = claim(pe, phase, part, turn)
                s0, ns = thirds(part)
                for a in range(ns):
                    mm = pe.matmul(t[:, a, 0:TH], W("kc"), ctx_T[:, p, (s0 + a) * TH:(s0 + a + 1) * TH], start=True, stop=True)
                mm.then_inc(slot_full(phase, part), 1)

            def values_product(phase, turn, p, part):
                t = claim(pe, phase, part, turn)
                k = int(part[1])
                for c in range(4):
                    at = (4 * k + c) * KC
                    mm = pe.matmul(t[0:KC, 0, c * D:(c + 1) * D], ctx_T[:, p, at:at + KC], W("vc"), start=True, stop=True)
                mm.then_inc(slot_full(phase, part), 1)

            def weigh(v, pr, first, last):
                for lo, acc, r0, rn in ((0, acc_a, 0, RA), (33, acc_b, RA, N)):
                    for g in range(G):
                        mm = pe.matmul(acc[32 * g:32 * g + 32, 0:rn], v[:, g, lo:lo + 32], pr[:, GQ * g + r0:GQ * g + r0 + rn],
                                       start=first, stop=last)
                return mm

            for l in range(L):
                pe.wait_ge(w1_loaded, 16 * (l + 1))
                for b in range(2):
                    pe.wait_ge(ctx_loaded[b], 16 * (B // 2) * l + 16)
                    for part in ("K0", "K1"):
                        keys_product(f"kv{b}_{l}", 0, b, part)
                    for part in ("V0", "V1", "V2"):
                        values_product(f"kv{b}_{l}", 0, b, part)

                if l == 0:
                    pe.wait_ge(silu_ready, 1)
                t = claim(pe, f"A{l}", "mod")
                for k in range(6):
                    pe.matmul(t[:, 0, k * B:(k + 1) * B], W("mod", k * D, (k + 1) * D), silu[:, :], start=True, stop=True)
                for n, w in enumerate(("p", "cp")):
                    v = ("vA", "vB") if n == 0 else ("cvA", "cvB")
                    pe.matmul(t[:, 0, 6 * B + n:6 * B + n + 1], W(w + "A"), bi(l, v[0]), start=True, stop=False)
                    mm = pe.matmul(t[:, 0, 6 * B + n:6 * B + n + 1], W(w + "B"), bi(l, v[1]), start=False, stop=True)
                mm.then_inc(slot_full(f"A{l}", "mod"), 1)
                norm(f"A{l}", 3 * l)
                dense(f"A{l}", "q", [(W("q"), xn)])
                dense(f"A{l}", "k", [(W("k"), xn)])
                freed(pe, f"A{l}", "k")

                def self_scores(phase, turn, b, p, l=l):
                    pe.wait_ge(self_operands, b * 2 + (2 * B * l + 2))
                    t = claim(pe, phase, "S", turn)
                    for n in range(NP):
                        mm = pe.matmul(t[0:PAIR, 0, n * N:(n + 1) * N], q_blocks[p][:, n * PAIR:(n + 1) * PAIR],
                                       kT[:, bass.ds(b * N, N)], start=True, stop=True)
                    mm.then_inc(slot_full(phase, "S"), 1)
                    t = claim(pe, phase, "V", turn)
                    pe.matmul(t[0:N, 0, 0:D], x_batch[:, p, :], W("v"), start=True, stop=True)\
                        .then_inc(slot_full(phase, "V"), 1)

                def self_weigh(phase, turn, b, p, l=l):
                    pe.wait_ge(self_probs, b + (B * l + 1))
                    s, n = uses.at(phase, "T", turn)
                    wait_alone(pe, psum_free[s], n + 1)
                    t = slot[s]
                    for n in range(NP):
                        c = (n % 4) * PAIR
                        mm = pe.transpose(t[0:N, n // 4, c:c + PAIR], probs_self[p][:, n * N:(n + 1) * N],
                                          co("ident", slice(0, PAIR))[:, 0:PAIR])
                    mm.then_inc(slot_full(phase, "T"), 1)
                    freed(pe, phase, "T", turn)
                    wait_alone(pe, acc_free, b * 3 + (3 * 2 * B * l + 3))
                    weigh(v_self[:, p, :, :], probs_T[p], True, True).then_inc(self_done, 1)

                def self_turn(b, p, i, l=l):
                    self_scores(f"self{l}", b, b + 1, 1 - p)
                    self_weigh(f"self{l}", b, b, p)

                def self_end(l=l):
                    self_turn(B - 2, 0, 7)
                    self_weigh(f"self_last{l}", 0, B - 1, 1)

                self_scores(f"self_first{l}", 0, 0, 0)
                turns(pe, self_turn, self_end)

                def project(phase, layer_half, wa, wb, l=l):
                    pe.wait_ge(acc_free, 3 * (2 * B * l + B * (1 + layer_half)) + 3)
                    dense(phase, "dA", [(co("selA"), heads_a)])
                    dense(phase, "dB", [(co("selB"), heads_b)])
                    pe.wait_ge(heads_ready, 4 * l + 2 * layer_half + 2)
                    dense(phase, "p", [(wa, qT), (wb, kT)])

                project(f"B{l}", 0, W("pA"), W("pB"))
                norm(f"B{l}", 3 * l + 1)
                for g in range(G):
                    dense(f"B{l}", f"q{g}", [(W("qr", 96 * g, 96 * g + 96), xn)], 96)

                def max_tile(phase, turn, p, c):
                    t = claim(pe, phase, f"M{c}", turn)
                    k = c // 4
                    for a in range(2):
                        n = 2 * (c % 4) + a
                        mm = pe.matmul(t[0:PAIR, a, 0:TH], q_max[p][0:KR - 1, n * PAIR:(n + 1) * PAIR],
                                       k_stack[p][0:KR - 1, n // 2, k * TH:(k + 1) * TH], start=True, stop=True)
                    mm.then_inc(slot_full(phase, f"M{c}"), 1)

                def max_rows(phase, turn, count):
                    t = claim(pe, phase, "R", turn)
                    pe.wait_ge(max_ready, count)
                    for n in range(NP):
                        c = (n % 4) * PAIR
                        mm = pe.matmul(t[96:KR, n // 4, c:c + PAIR], neg_max[:, n:n + 1].to_broadcast([PAIR, 2]),
                                       co("ident", slice(0, PAIR))[:, 0:PAIR], start=True, stop=True)
                    mm.then_inc(slot_full(phase, "R"), 1)

                def score_chunk(phase, turn, p, c):
                    t = claim(pe, phase, f"C{c}", turn)
                    for g in range(G):
                        mm = pe.matmul(t[0:KC, g // 2, (g % 2) * GQ:(g % 2 + 1) * GQ], k_stack[p][:, g, c * KC:(c + 1) * KC],
                                       q_score[p][:, g * GQ:(g + 1) * GQ], start=True, stop=True)
                    mm.then_inc(slot_full(phase, f"C{c}"), 1)

                def weigh_chunk(phase, turn, p, c):
                    freed(pe, phase, f"C{c}", turn)
                    weigh(v_ctx[p][:, c, :, :], probs[:, c % 3, :], c == 0, c == NCH - 1).then_inc(probs_used, 1)

                def cross_turn(phase, turn, b, p, stack, ctx_count, l=l):
                    pe.wait_ge(qscore_ready, b + (B * l + 1))
                    for use in cross_uses(stack is not None, ctx_count is not None):
                        n = int(use[1:] or 0)
                        if use[0] == "M":
                            if n == 0:
                                pe.wait_ge(qmax_ready, b + (B * l + 2))
                            if n % 4 == 0:
                                pe.wait_ge(stack_loaded[1 - p][n // 4], stack)
                            max_tile(phase, turn, 1 - p, n)
                        elif use[0] == "C":
                            score_chunk(phase, turn, p, n)
                            if n == 1:
                                pe.wait_ge(acc_free, b * 3 + (3 * (2 * B * l + B) + 3))
                            if n > 0:
                                weigh_chunk(phase, turn, p, n - 1)
                        elif use == "K0":
                            pe.wait_ge(ctx_loaded[p], ctx_count)
                            keys_product(phase, turn, p, use)
                        elif use == "K1":
                            keys_product(phase, turn, p, use)
                        elif use[0] == "V":
                            if n == 2:
                                weigh_chunk(phase, turn, p, NCH - 1)
                            values_product(phase, turn, p, use)
                        elif use == "R":
                            max_rows(phase, turn, b + (B * l + 2))
                    if ctx_count is None:
                        weigh_chunk(phase, turn, p, NCH - 1)

                pe.wait_ge(qmax_ready, B * l + 1)
                if l == 0:
                    pe.wait_ge(rows_init, 4)
                elif l == MASKED + 1:
                    pe.wait_ge(rows_init, 6)
                for c in range(NCH):
                    if c % 4 == 0:
                        pe.wait_ge(stack_loaded[0][c // 4], stack_count(l, 0))
                    max_tile(f"max0_{l}", 0, 0, c)
                max_rows(f"max0_{l}", 0, B * l + 1)

                def turn(b, p, i, l=l):
                    per = 16 * stack_dmas(l)
                    cross_turn(f"cross{l}", b, b, p, i * per + (stack_count(l, 0) + (per if p else 0)),
                               i * 16 + (16 * (B // 2) * l + 32))

                def end(l=l):
                    cross_turn(f"cross14_{l}", 0, B - 2, 0, stack_count(l, 7), None)
                    cross_turn(f"cross15_{l}", 0, B - 1, 1, None, None)

                turns(pe, turn, end)

                project(f"C{l}", 1, W("cpA"), W("cpB"))
                norm(f"C{l}", 3 * l + 2)
                pe.wait_ge(w2_loaded, 16 * (l + 1))
                for j in range(4):
                    dense(f"C{l}", f"h{j}", [(w2[:, j * D:(j + 1) * D], xn)])
                for j in range(4):
                    freed(pe, f"C{l}", f"h{j}")
                dense(f"C{l}", "y", [(w2[:, (4 + j) * D:(5 + j) * D], hidden[j]) for j in range(4)])


def constants():
    c = np.zeros((D, CO_COLS), np.float32)

    def put(name, a):
        o, w = CO[name]
        c[:, o:o + w] = a

    r = np.arange(D)
    first = np.minimum(r % 32 // VS, 2)
    put("mean", np.full((D, D), 1.0 / D, np.float32))
    put("ident", np.eye(D, dtype=np.float32))
    put("selA", (r[:, None] == (r // 32 * 32 + first * VS + HD)[None, :]).astype(np.float32))
    put("selB", (r[:, None] == (r // 32 * 32 + HD)[None, :]).astype(np.float32))
    put("head16", (r[:, None] // HD == np.arange(NH)[None, :]).astype(np.float32))
    put("head4", (r[:, None] % 32 // HD == np.arange(GH)[None, :]).astype(np.float32))
    put("third", (first[:, None] == np.arange(3)[None, :]).astype(np.float32))
    rows = np.zeros((D, 4), np.float32)
    rows[97, 0] = 1.0
    rows[96, 1] = 1.0
    rows[97, 2] = 1.0
    put("rows", rows)
    put("eps", np.full((D, 1), EPS, np.float32))
    return c


def by_rows(w):
    a, b = np.zeros((D, w.shape[1]), w.dtype), np.zeros((D, w.shape[1]), w.dtype)
    for g in range(G):
        for t in range(GH):
            src = w[(GH * g + t) * HD:(GH * g + t + 1) * HD]
            if t < 3:
                a[32 * g + VS * t:32 * g + VS * t + HD] = src
            else:
                b[32 * g:32 * g + HD] = src
    return a, b


def kernel(**inputs):
    import concourse.bacc as bacc
    from concourse.bass_utils import run_bass_kernel_spmd

    a = {k: np.asarray(v) for k, v in inputs.items()}
    names = [
        dict(mod="W_mod", bmod="b_mod", qkv="W_qkv", bqkv="b_qkv", p="W_proj", bp="b_proj", q="W_qc", bq="b_qc", kv="W_kvc",
             bkv="b_kvc", cp="W_cproj", bcp="b_cproj", f1="W_mlp1", bf1="b_mlp1", f2="W_mlp2", bf2="b_mlp2"),
        dict(mod="ada_w", bmod="ada_b", qkv="qkv_w", bqkv="qkv_b", p="self_o_w", bp="self_o_b", q="q_w", bq="q_b", kv="kv_w",
             bkv="kv_b", cp="cross_o_w", bcp="cross_o_b", f1="mlp_w1", bf1="mlp_b1", f2="mlp_w2", bf2="mlp_b2"),
        dict(mod="ada_w", bmod="ada_b", qkv="qkv_w", bqkv="qkv_b", p="sa_proj_w", bp="sa_proj_b", q="q_w", bq="q_b",
             kv="kv_w", bkv="kv_b", cp="ca_proj_w", bcp="ca_proj_b", f1="fc1_w", bf1="fc1_b", f2="fc2_w", bf2="fc2_b"),
        dict(mod="adaln_w", bmod="adaln_b", qkv="qkv_w", bqkv="qkv_b", p="sa_proj_w", bp="sa_proj_b", q="q_w", bq="q_b",
             kv="kv_w", bkv="kv_b", cp="ca_proj_w", bcp="ca_proj_b", f1="fc1_w", bf1="fc1_b", f2="fc2_w", bf2="fc2_b"),
    ]
    w1 = np.zeros((L, D, W1_COLS), np.float32)
    w2 = np.zeros((L, D, W2_COLS), np.float32)
    bias = np.zeros((D, L * BI_COLS), np.float32)
    for l, name in enumerate(names):
        p = {k: a[f"L{l}_xcond_{v}"] for k, v in name.items()}
        parts = {"mod": p["mod"], "q": p["qkv"][:, 0:D], "k": p["qkv"][:, D:2 * D], "v": p["qkv"][:, 2 * D:3 * D],
                 "kc": p["kv"][:, 0:D], "vc": p["kv"][:, D:2 * D]}
        parts["pA"], parts["pB"] = by_rows(p["p"])
        parts["cpA"], parts["cpB"] = by_rows(p["cp"])
        parts["qr"] = np.concatenate([p["q"][:, 32 * g:32 * g + 32] for g in range(G) for _ in range(3)], axis=1)
        for k, m in parts.items():
            w1[l, :, W1[k][0]:W1[k][0] + W1[k][1]] = m
        w2[l, :, 0:4 * D] = p["f1"]
        w2[l, :, 4 * D:8 * D] = p["f2"].reshape(4, D, D).transpose(1, 0, 2).reshape(D, 4 * D)
        cols = {"mod": p["bmod"].reshape(6, D).T, "q": p["bqkv"][0:D, None], "k": p["bqkv"][D:2 * D, None],
                "p": p["bp"][:, None], "cp": p["bcp"][:, None], "kc": p["bkv"][0:D, None],
                "f1": p["bf1"].reshape(4, D).T, "f2": p["bf2"][:, None]}
        cols["vA"], cols["vB"] = by_rows(p["bqkv"][2 * D:3 * D, None])
        cols["cvA"], cols["cvB"] = by_rows(p["bkv"][D:2 * D, None])
        if l == AFFINE:
            cols["g2"], cols["b2"] = a["L1_xcond_norm2_g"][:, None], a["L1_xcond_norm2_b"][:, None]
        for k, m in cols.items():
            o = l * BI_COLS + BI[k][0]
            bias[:, o:o + BI[k][1]] = m
        for g in range(G):
            for r in range(3):
                bias[32 * r:32 * r + 32, l * BI_COLS + BI["qr"][0] + g] = p["bq"][32 * g:32 * g + 32]

    arrays = {
        "x_in": np.ascontiguousarray(a["x"].reshape(T, D).T),
        "cond_in": np.ascontiguousarray(a["cond_1024"].T),
        "ctx_in": np.ascontiguousarray(a["ctx_1024"].transpose(0, 2, 1)),
        "mask_in": np.ascontiguousarray(a["mask_BxS2_bf0"]).view(np.int32),
        "w1_in": w1, "w2_in": w2, "bias_in": bias, "const_in": constants(),
    }
    nc = bacc.Bacc("TRN2", target_bir_lowering=False, num_devices=1)
    args = [nc.dram_tensor(k, v.shape, mybir.dt.from_np(v.dtype), kind="ExternalInput").ap() for k, v in arrays.items()]
    out = nc.dram_tensor("out", (D, T), mybir.dt.float32, kind="ExternalOutput").ap()
    blocks_kernel(nc, *args, out)
    r = run_bass_kernel_spmd(nc, [arrays], core_ids=[0])
    return np.ascontiguousarray(r.results[0]["out"].T).reshape(B, N, D)
```

```python
from contextlib import ExitStack

import concourse.bass as bass
import numpy as np
from concourse import mybir
from concourse.alu_op_type import AluOpType as ALU

B, N, D, NH, HD, S = 16, 56, 128, 16, 8, 1500
L = 4
T = B * N
HALF = T // 2
KC = 125
NCH = S // KC
TH = 500
PAIR = 2 * N
NP = NH // 2
G, GH = 4, 4
HQ = NH * N
GQ = GH * N
RA = 3 * N
VS = HD + 3
VG = 66
KR = 98
SCALE = float(HD) ** -0.5
EPS = 1e-6
MASKED = 2
NORM_CTX = 0
AFFINE = 1
EXACT_GELU = 2

W1 = {}
for _n, _w in (("mod", 6 * D), ("q", D), ("k", D), ("v", D), ("pA", D), ("pB", D), ("cpA", D), ("cpB", D),
               ("qr", G * 96), ("kc", D), ("vc", D)):
    W1[_n] = (sum(w for _, w in W1.values()), _w)
W1_COLS = sum(w for _, w in W1.values())
W2_COLS = 8 * D
BI = {}
for _n, _w in (("mod", 6), ("q", 1), ("k", 1), ("vA", 1), ("vB", 1), ("cvA", 1), ("cvB", 1), ("p", 1), ("cp", 1),
               ("qr", G), ("kc", 1), ("f1", 4), ("f2", 1), ("g2", 1), ("b2", 1)):
    BI[_n] = (sum(w for _, w in BI.values()), _w)
BI_COLS = sum(w for _, w in BI.values())
CO = {}
for _n, _w in (("mean", D), ("ident", D), ("selA", D), ("selB", D), ("head16", NH), ("head4", GH), ("third", 3),
               ("rows", 4), ("eps", 1)):
    CO[_n] = (sum(w for _, w in CO.values()), _w)
CO_COLS = sum(w for _, w in CO.values())


class PsumUses:

    def __init__(self):
        self.base, self.total = {}, [0, 0, 0]

    def phase(self, name, seq, repeat=1):
        per = [len(range(s, len(seq), 3)) for s in range(3)]
        self.base[name] = (list(self.total), per, {u: i for i, u in enumerate(seq)})
        for s in range(3):
            self.total[s] += per[s] * repeat

    def at(self, phase, use, turn=0):
        base, per, place = self.base[phase]
        i = place[use]
        return i % 3, turn * per[i % 3] + (base[i % 3] + i // 3)


def cross_uses(with_max, with_kv):
    order = ("M0 C0 M1 C1 M2 C2 M3 C3 M4 C4 M5 K0 C5 V0 M6 C6 M7 K1 C7 C8 M8 M9 C9 M10 C10 M11 K2 C11 R V1")
    return [u for u in order.split() if u[0] == "C" or (with_max and u[0] in "MR") or (with_kv and u[0] in "KV")]


KV_USES = ["K0", "K1", "K2", "V0", "V1"]


def psum_plan():
    uses = PsumUses()
    uses.phase("ctx_first", ["m0", "m1"])
    uses.phase("ctx", ["m0", "m1", "v0", "v1"], B - 1)
    uses.phase("ctx_last", ["v0", "v1"])
    for l in range(L):
        uses.phase(f"kv0_{l}", KV_USES)
        uses.phase(f"kv1_{l}", KV_USES)
        uses.phase(f"A{l}", ["mod", "mean", "var", "q", "k"])
        uses.phase(f"self_first{l}", ["S0", "V0", "S1", "V1"])
        uses.phase(f"self{l}", ["T", "S", "V"], B - 2)
        uses.phase(f"self_last{l}", ["T0", "T1"])
        uses.phase(f"B{l}", ["dA", "dB", "p", "mean", "var", "q0", "q1", "q2", "q3"])
        uses.phase(f"max0_{l}", [f"M{c}" for c in range(NCH)] + ["R"])
        uses.phase(f"cross{l}", cross_uses(True, True), B - 2)
        uses.phase(f"cross14_{l}", cross_uses(True, False))
        uses.phase(f"cross15_{l}", cross_uses(False, False))
        uses.phase(f"C{l}", ["dA", "dB", "p", "mean", "var", "h0", "h1", "h2", "h3", "y"])
    return uses


def stack_dmas(l):
    return 3 * G + (l == MASKED)


def stack_count(l, half):
    return half * (16 * stack_dmas(l)) + 16 * ((B // 2) * sum(stack_dmas(k) for k in range(l)) + stack_dmas(l))


def blocks_kernel(nc, x_d, cond_d, ctx_d, mask_d, w1_d, w2_d, bias_d, const_d, out_d):
    F32, F32R, U8 = mybir.dt.float32, mybir.dt.float32r, mybir.dt.uint8
    ACT, AX = mybir.ActivationFunctionType, mybir.AxisListType
    uses = psum_plan()
    ctx = ExitStack()
    with ctx:
        def sb(name, shape, dt=F32):
            return ctx.enter_context(nc.sbuf_tensor(name, shape, dt))

        def sem(name):
            return ctx.enter_context(nc.semaphore(name))

        ctx_norm_d = nc.dram_tensor("ctx_norm", (B, D, S), F32, kind="Internal").ap()

        w1 = sb("w1", [D, W1_COLS])
        w2 = sb("w2", [D, W2_COLS])
        bias = sb("bias", [D, L * BI_COLS])
        const = sb("const", [D, CO_COLS])
        cond = sb("cond", [D, B])
        silu = sb("silu", [D, B])
        x = sb("x", [D, T])
        norm_work = sb("norm_work", [D, 4 * T])
        xc = norm_work[:, 0:T]
        sq = norm_work[:, T:2 * T]
        rstd = norm_work[:, 2 * T:3 * T]
        xn = norm_work[:, 3 * T:4 * T]
        qk = sb("qk", [D, 2 * T])
        qT, kT = qk[:, 0:T], qk[:, T:2 * T]
        mod = sb("mod", [D, 6, B])
        proj_bias = sb("proj_bias", [D, 2])
        work = sb("work", [D, 4 * T])
        hidden = [work[:, j * T:(j + 1) * T] for j in range(4)]
        q_blocks = [work[:, 0:HQ], work[:, HQ:2 * HQ]]
        probs_T = [work[0:N, 2 * HQ:3 * HQ], work[0:N, 3 * HQ:4 * HQ]]
        probs_self = [sq[0:PAIR, 0:NP * N], sq[0:PAIR, NP * N:2 * NP * N]]
        x_batch = sb("x_batch", [D, 2, N])
        k_batch = sb("k_batch", [D, 2, N])
        v_self = sb("v_self", [N, 2, G, VG])
        heads_a = sb("heads_a", [D, T])
        heads_b = sb("heads_b", [D, T])
        masked = sb("masked", [D, 3, N])
        part_max = sb("part_max", [PAIR, 3, NP])
        neg_max = sb("neg_max", [PAIR, NP])
        neg_max_self = sb("neg_max_self", [PAIR, 2, NP])
        ctx_T = sb("ctx_T", [D, 2, S])
        k_hi = sb("k_hi", [D, S], F32R)
        k_lo = sb("k_lo", [D, S], F32R)
        ctx_centred = [t[:, :].bitcast(F32) for t in (k_hi, k_lo)]
        ctx_squares = [work[:, 0:S], work[:, 2 * T:2 * T + S]]
        deviation = qk[:, 0:S]
        ctx_out = [norm_work[:, 0:S], norm_work[:, 2 * T:2 * T + S]]
        k_stack = [sb(f"k_stack{i}", [KR, G, S], F32R) for i in range(2)]
        q_split = sb("q_split", [96, G, T], F32R)
        q_max = [sb(f"q_max{i}", [KR, HQ], F32R) for i in range(2)]
        q_score = [sb(f"q_score{i}", [KR, HQ], F32R) for i in range(2)]
        v_ctx = [sb(f"v_ctx{i}", [KC, NCH, G, VG]) for i in range(2)]
        probs = sb("probs", [KC, 3, HQ])
        mask_u8 = sb("mask_u8", [97, S], U8)
        mask_row = sb("mask_row", [97, S], F32R)

        slot = [ctx.enter_context(nc.psum_tensor(f"slot{i}", [D, 2, 512], F32)) for i in range(3)]
        acc_a = ctx.enter_context(nc.psum_tensor("acc_a", [D, 512], F32))
        acc_b = ctx.enter_context(nc.psum_tensor("acc_b", [D, 512], F32))

        psum_full = [sem(f"psum_full{i}") for i in range(3)]
        psum_free = [sem(f"psum_free{i}") for i in range(3)]
        const_loaded, x_loaded, w1_loaded, w2_loaded = sem("const_loaded"), sem("x_loaded"), sem("w1_loaded"), sem("w2_loaded")
        raw_loaded = [sem(f"raw_loaded{i}") for i in range(2)]
        norm_stored = [sem(f"norm_stored{i}") for i in range(2)]
        ctx_loaded = [sem(f"ctx_loaded{i}") for i in range(2)]
        stack_loaded = [[sem(f"stack_loaded{i}_{k}") for k in range(2)] for i in range(2)]
        mask_loaded, mask_row_ready = sem("mask_loaded"), sem("mask_row_ready")
        ctx_squared, ctx_rstd, ctx_normed = sem("ctx_squared"), sem("ctx_rstd"), sem("ctx_normed")
        exp_cond, silu_ready = sem("exp_cond"), sem("silu_ready")
        x_squared, rstd_ready, xn_ready, x_ready = sem("x_squared"), sem("rstd_ready"), sem("xn_ready"), sem("x_ready")
        den_ready, heads_ready, qhi_ready = sem("den_ready"), sem("heads_ready"), sem("qhi_ready")
        self_operands, self_probs, self_done = sem("self_operands"), sem("self_probs"), sem("self_done")
        hi_ready, qmax_ready, qscore_ready, self_max = sem("hi_ready"), sem("qmax_ready"), sem("qscore_ready"), sem("self_max")
        max_ready, shift_ready, probs_used, acc_free = sem("max_ready"), sem("shift_ready"), sem("probs_used"), sem("acc_free")
        waits_met = sem("waits_met")
        pool_init, rows_init, dve_step, stored = sem("pool_init"), sem("rows_init"), sem("dve_step"), sem("stored")

        block = ctx.enter_context(nc.Block())

        def W(name, a=0, b=None):
            o, w = W1[name]
            return w1[:, o + a:o + (w if b is None else b)]

        def bi(l, name, n=0, rows=slice(0, D), width=1):
            o = l * BI_COLS + BI[name][0] + n
            return bias[rows, o:o + width]

        def co(name, rows=slice(0, D)):
            o, w = CO[name]
            return const[rows, o:o + w]

        def full(e, phase, use, turn=0):
            s, n = uses.at(phase, use, turn)
            e.wait_ge(psum_full[s], n + 1)
            return slot[s]

        def freed(e, phase, use, turn=0):
            s, n = uses.at(phase, use, turn)
            e.wait_ge(psum_free[s], n + 2)

        def claim(pe, phase, use, turn=0):
            s, n = uses.at(phase, use, turn)
            pe.wait_ge(psum_free[s], n + 1)
            return slot[s]

        def wait_alone(e, semaphore, count):
            e.wait_ge(semaphore, count)
            if not isinstance(count, int):
                e.sem_inc(waits_met, 1)

        def slot_free(phase, use):
            return psum_free[uses.at(phase, use)[0]]

        def slot_full(phase, use):
            return psum_full[uses.at(phase, use)[0]]

        def halves(t, rows=slice(0, D)):
            return t[rows, :, 0:HALF]

        def two(t):
            return t.rearrange("p (a n) -> p a n", a=2)

        def by_batch(t):
            return t.rearrange("p (b n) -> p b n", n=N)

        def per_token(m, nb=B):
            return m.unsqueeze(2).to_broadcast([D, nb, N])

        def thirds(part):
            if part[0] == "K":
                return int(part[1]), 1
            return (0, 2) if part[1] == "0" else (2, 1)

        def value_chunks(part):
            return (0, 1) if part == "V0" else (4, 2)

        def keys(t, part):
            s0, ns = thirds(part)
            return t[:, s0 * TH:(s0 + ns) * TH].rearrange("p (a n) -> p a n", n=TH)

        def value_columns(v):
            return v[:, :, 0:GH * VS].rearrange("p a (t v) -> p a t v", v=VS)[:, :, :, 0:HD]

        def turns(e, body, last=None):
            with e.Fori(0, (B - 2) // 2, 1) as i:
                body(i * 2, 0, i)
                body(i * 2 + 1, 1, i + 0)
            if last:
                last()

        @block.sync
        def _(sp):
            sp.dma_start(const[:, :], const_d).then_inc(const_loaded, 16)
            sp.dma_start(bias[:, :], bias_d).then_inc(const_loaded, 16)
            sp.dma_start(cond[:, :], cond_d).then_inc(const_loaded, 16)
            for p in range(2):
                sp.dma_start(ctx_T[:, p, :], ctx_d[p]).then_inc(raw_loaded[p], 16)
            sp.dma_start(x[:, :], x_d).then_inc(x_loaded, 16)
            sp.dma_start(w1[:, :], w1_d[0]).then_inc(w1_loaded, 16)
            sp.dma_start(w2[:, :], w2_d[0]).then_inc(w2_loaded, 16)

            def store_norm(b, p):
                wait_alone(sp, ctx_normed, b + 2)
                sp.dma_start(ctx_norm_d[bass.ds(b, 1)].rearrange("o d s -> (o d) s"), ctx_out[p])\
                    .then_inc(norm_stored[p], 16)

            def ctx_turn(b, p):
                s, n = uses.at("ctx", "m1", b)
                wait_alone(sp, psum_free[s], n + 2)
                sp.dma_start(ctx_T[:, 1 - p, :], ctx_d[bass.ds(b + 3, 1)].rearrange("o d s -> (o d) s"))\
                    .then_inc(raw_loaded[1 - p], 16)
                store_norm(b, p)

            freed(sp, "ctx_first", "m1")
            sp.dma_start(ctx_T[:, 0, :], ctx_d[2]).then_inc(raw_loaded[0], 16)
            with sp.Fori(0, (B - 4) // 2, 1) as i:
                ctx_turn(i * 2, 0)
                ctx_turn(i * 2 + 1, 1)
            ctx_turn(B - 4, 0)
            for b in range(B - 3, B):
                store_norm(b, b % 2)
            for p in range(2):
                sp.wait_ge(norm_stored[p], 16 * (B // 2 + 1))

            def load_ctx(l, b, p):
                src = ctx_norm_d if l == NORM_CTX else ctx_d
                sp.dma_start(ctx_T[:, p, :], src[bass.ds(b, 1)].rearrange("o d s -> (o d) s"))\
                    .then_inc(ctx_loaded[p], 16)

            def load_mask(b, before):
                if before:
                    wait_alone(sp, mask_row_ready, b)
                sp.dma_start(mask_u8[96:97, :].bitcast(mybir.dt.int32), mask_d[bass.ds(b, 1)]).then_inc(mask_loaded, 16)

            def place(l, b, p, k, phase, turn):
                n = slice(0, 2 * TH) if k == 0 else slice(2 * TH, S)
                for part in (("K0", "K1"), ("K2",))[k]:
                    s, count = uses.at(phase, part, turn)
                    wait_alone(sp, psum_free[s], count + 2)
                for g in range(G):
                    rows = slice(32 * g, 32 * g + 32)
                    for at, half in ((0, k_hi), (32, k_lo), (64, k_hi)):
                        sp.dma_start(k_stack[p][at:at + 32, g, n].bitcast(F32), half[rows, n].bitcast(F32))\
                            .then_inc(stack_loaded[p][k], 16)
                if l == MASKED:
                    if k == 0:
                        sp.wait_ge(mask_row_ready, b + 1)
                    sp.dma_start(k_stack[p][96:97, :, n].bitcast(F32),
                                 mask_row[96:97, n].bitcast(F32).unsqueeze(1).to_broadcast([1, G, n.stop - n.start]))\
                        .then_inc(stack_loaded[p][k], 16)

            for l in range(L):
                if l > 0:
                    freed(sp, f"cross{l - 1}", "V1", B - 3)
                for p in range(2):
                    load_ctx(l, p, p)
                if l > 0:
                    sp.wait_ge(x_ready, 3 * (l - 1) + 2)
                    sp.dma_start(w1[:, :], w1_d[l]).then_inc(w1_loaded, 16)
                    sp.wait_ge(x_ready, 3 * l)
                    sp.dma_start(w2[:, :], w2_d[l]).then_inc(w2_loaded, 16)
                for b in range(2):
                    if l == MASKED:
                        load_mask(b, b > 0)
                    for k in range(2):
                        place(l, b, b, k, f"kv{b}_{l}", 0)
                    freed(sp, f"kv{b}_{l}", "V1")
                    load_ctx(l, b + 2, b)

                def cross_turn(b, p, more, l=l):
                    if l == MASKED:
                        load_mask(b + 2, True)
                    for k in range(2):
                        s, n = uses.at(f"cross{l}", f"C{4 * k + 7}", b)
                        wait_alone(sp, psum_free[s], n + 2)
                        place(l, b + 2, p, k, f"cross{l}", b)
                    if more:
                        s, n = uses.at(f"cross{l}", "V1", b)
                        wait_alone(sp, psum_free[s], n + 2)
                        load_ctx(l, b + 4, p)

                with sp.Fori(0, (B - 4) // 2, 1) as i:
                    cross_turn(i * 2, 0, True)
                    cross_turn(i * 2 + 1, 1, True)
                cross_turn(B - 4, 0, False)
                cross_turn(B - 3, 1, False)
            sp.wait_ge(x_ready, 3 * L)
            sp.dma_start(out_d, x[:, :]).then_inc(stored, 16)
            sp.wait_ge(stored, 16)

        @block.gpsimd
        def _(pool):
            for i in range(2):
                pool.memset(v_ctx[i][:, :, :, :], 0.0).then_inc(pool_init, 1)
            pool.memset(v_self[:, :, :, :], 0.0).then_inc(pool_init, 1)
            pool.wait_ge(pool_init, 3)
            for t in range(GH):
                c = VS * t + HD
                for i in range(2):
                    pool.memset(v_ctx[i][:, :, :, c:c + 1], 1.0).then_inc(pool_init, 1)
                pool.memset(v_self[:, :, :, c:c + 1], 1.0).then_inc(pool_init, 1)
            pool.wait_ge(const_loaded, 48)

            def make_mask_row(l, b, p):
                pool.wait_ge(mask_loaded, b * 16 + 16)
                for k in range(2):
                    wait_alone(pool, stack_loaded[1 - p][k], mask_placed(b, p))
                pool.tensor_scalar(mask_row[96:97, :], mask_u8[96:97, :], -1e38, 1e38, ALU.mult, ALU.mult)\
                    .then_inc(mask_row_ready, 1)
                wait_alone(pool, mask_row_ready, b + 1)

            def mask_placed(b, p):
                per = 16 * stack_dmas(MASKED)
                base = stack_count(MASKED, 0) - per
                return (b * (per // 2) + base) if p == 0 else (b * (per // 2) + (base + per // 2))

            def self_operands_of(b, p):
                at = bass.ds(b * N, N)
                pool.tensor_tensor(out=by_batch(q_blocks[p]), in0=qT[:, at].unsqueeze(1).to_broadcast([D, NH, N]),
                                   in1=co("head16").unsqueeze(2).to_broadcast([D, NH, N]), op=ALU.mult)\
                    .then_inc(self_operands, 1)
                pool.tensor_copy(k_batch[:, p, :], kT[:, at]).then_inc(self_operands, 1)
                pool.tensor_copy(x_batch[:, p, :], xn[:, at]).then_inc(self_operands, 1)

            def expand(dst, b):
                for g in range(G):
                    last = pool.tensor_tensor(
                        out=by_batch(dst[0:96, g * GQ:(g + 1) * GQ]),
                        in0=q_split[:, g, bass.ds(b * N, N)].bitcast(F32).unsqueeze(1).to_broadcast([96, GH, N]),
                        in1=co("head4", slice(0, 96)).unsqueeze(2).to_broadcast([96, GH, N]), op=ALU.mult)
                return last

            for l in range(L):
                if l == MASKED:
                    for b in range(2):
                        make_mask_row(l, b, b)
                freed(pool, f"A{l}", "k")
                self_operands_of(0, 0)
                self_operands_of(1, 1)

                def self_turn(b, p, phase, use, turn, l=l):
                    s, n = uses.at(phase, use, turn)
                    wait_alone(pool, psum_full[s], n + 1)
                    self_operands_of(b + 2, p)

                for b in range(2):
                    self_turn(b, b, f"self_first{l}", f"V{b}", 0)
                with pool.Fori(0, (B - 4) // 2, 1) as i:
                    self_turn(i * 2 + 2, 0, f"self{l}", "V", i * 2)
                    self_turn(i * 2 + 3, 1, f"self{l}", "V", i * 2 + 1)

                freed(pool, f"B{l}", "q3")
                expand(q_max[0], 0).then_inc(qmax_ready, 1)
                expand(q_score[0], 0).then_inc(qscore_ready, 1)
                expand(q_max[1], 1).then_inc(qmax_ready, 1)

                def next_scores(b, p, l=l):
                    wait_alone(pool, probs_used, b * NCH + (NCH * B * l + 3))
                    expand(q_score[1 - p], b + 1).then_inc(qscore_ready, 1)

                def cross_turn(b, p, i, l=l):
                    next_scores(b, p)
                    wait_alone(pool, max_ready, b + (B * l + 1))
                    expand(q_max[p], b + 2).then_inc(qmax_ready, 1)
                    if l == MASKED:
                        make_mask_row(l, b + 2, p)

                turns(pool, cross_turn, lambda: next_scores(B - 2, 0))

        @block.scalar
        def _(act):
            act.wait_ge(const_loaded, 48)
            eps = co("eps")
            act.preload_act_table_set("natural_log_exp_and_others")
            act.activation(silu[:, :], cond[:, :], ACT.Exp, scale=-1.0).then_inc(exp_cond, 1)

            def ctx_square(p):
                act.activation(ctx_squares[p], ctx_centred[p], ACT.Square).then_inc(ctx_squared, 1)

            def ctx_deviation(phase, turn):
                for part in ("v0", "v1"):
                    t = full(act, phase, part, turn)
                    act.activation(keys(deviation, part), t[:, 0:thirds(part)[1], 0:TH], ACT.Ln, bias=eps)\
                        .then_inc(slot_free(phase, part), 1)
                for part in ("v0", "v1"):
                    freed(act, phase, part, turn)
                act.activation(deviation, deviation, ACT.Exp, scale=-0.5).then_inc(ctx_rstd, 1)

            def ctx_turn(b, p, i):
                freed(act, "ctx", "m1", b)
                ctx_square(1 - p)
                act.wait_ge(ctx_normed, b + 1)
                ctx_deviation("ctx", b)

            def ctx_end():
                ctx_turn(B - 2, 0, 7)
                act.wait_ge(ctx_normed, B)
                ctx_deviation("ctx_last", 0)

            freed(act, "ctx_first", "m1")
            ctx_square(0)
            turns(act, ctx_turn, ctx_end)

            def norm(phase, k):
                freed(act, phase, "mean")
                act.activation(sq[:, :], xc[:, :], ACT.Square).then_inc(x_squared, 1)
                t = full(act, phase, "var")
                act.activation(two(rstd[:, :]), halves(t), ACT.Ln, bias=eps).then_inc(slot_free(phase, "var"), 1)
                freed(act, phase, "var")
                act.activation(rstd[:, :], rstd[:, :], ACT.Exp, scale=-0.5).then_inc(rstd_ready, 1)

            def reciprocals(phase):
                for use, den in (("dA", rstd), ("dB", sq)):
                    t = full(act, phase, use)
                    act.activation(two(den[:, :]), halves(t), ACT.Ln).then_inc(slot_free(phase, use), 1)
                    freed(act, phase, use)
                    act.activation(den[:, :], den[:, :], ACT.Exp, scale=-1.0).then_inc(den_ready, 1)

            def keys_high(phase, turn, l, b, p, part):
                t = full(act, phase, part, turn)
                s0, ns = thirds(part)
                if b is not None and part != "K1":
                    act.wait_ge(stack_loaded[1 - p][s0 // 2], b)
                act.activation(keys(k_hi, part), t[:, 0:ns, 0:TH], ACT.Identity, bias=bi(l, "kc")).then_inc(hi_ready, 1)

            def values(phase, turn, p, part):
                t = full(act, phase, part, turn)
                c0, banks = value_chunks(part)
                act.activation(value_columns(v_ctx[p][:, c0:c0 + 4 * banks, :, :].rearrange("p c g v -> p (c g) v")),
                               t[0:KC, 0:banks, :].rearrange("p k (a t d) -> p (k a) t d", t=GH, d=HD), ACT.Copy)\
                    .then_inc(slot_free(phase, part), 1)

            def exps(phase, turn, c, n):
                t = full(act, phase, f"C{c}", turn)
                act.wait_ge(probs_used, n + 1)
                act.activation(two(probs[:, c % 3, :]), t[0:KC, :, 0:HALF], ACT.Exp, scale=SCALE)\
                    .then_inc(slot_free(phase, f"C{c}"), 1)

            act.wait_ge(pool_init, 3 + 3 * GH)
            for l in range(L):
                for b in range(2):
                    for part in KV_USES[0:3]:
                        before = None if l == 0 and b == 0 else stack_count(l, b // 2) if b else stack_count(l - 1, 7)
                        keys_high(f"kv{b}_{l}", 0, l, before, b, part)
                    for part in KV_USES[3:]:
                        values(f"kv{b}_{l}", 0, b, part)
                norm(f"A{l}", 3 * l)
                for part, dst in (("q", qT), ("k", kT)):
                    t = full(act, f"A{l}", part)
                    act.activation(two(dst[:, :]), halves(t), ACT.Identity, bias=bi(l, part))\
                        .then_inc(slot_free(f"A{l}", part), 1)

                def self_exp(phase, use, turn, p):
                    freed(act, phase, use, turn)
                    act.activation(probs_self[p], probs_self[p], ACT.Exp, scale=SCALE).then_inc(self_probs, 1)

                def self_values(phase, use, turn, p):
                    t = full(act, phase, use, turn)
                    act.activation(value_columns(v_self[:, p, :, :]),
                                   t[0:N, 0, 0:D].rearrange("p (a t d) -> p a t d", t=GH, d=HD), ACT.Copy)\
                        .then_inc(slot_free(phase, use), 1)

                def self_transposed(phase, use, turn, p):
                    t = full(act, phase, use, turn)
                    act.activation(two(probs_T[p]), halves(t, slice(0, N)), ACT.Copy).then_inc(slot_free(phase, use), 1)

                def self_turn(b, p, i, l=l):
                    self_transposed(f"self{l}", "T", b, p)
                    self_exp(f"self{l}", "S", b, p)
                    self_values(f"self{l}", "V", b, p)

                for b in range(2):
                    self_exp(f"self_first{l}", f"S{b}", 0, b)
                    self_values(f"self_first{l}", f"V{b}", 0, b)
                turns(act, self_turn)
                for b in range(2):
                    self_transposed(f"self_last{l}", f"T{b}", 0, b)
                reciprocals(f"B{l}")
                norm(f"B{l}", 3 * l + 1)
                for g in range(G):
                    t = full(act, f"B{l}", f"q{g}")
                    act.activation(two(q_split[:, g, :]), halves(t, slice(0, 96)), ACT.Identity,
                                   bias=bi(l, "qr", g, slice(0, 96))).then_inc(qhi_ready, 1)

                def cross_turn(phase, turn, b, p, kv, l=l):
                    for use in cross_uses(kv is not None, kv is not None):
                        if use[0] == "C":
                            c = int(use[1:])
                            exps(phase, turn, c, b * NCH + (NCH * B * l + c))
                        elif use[0] == "K":
                            keys_high(phase, turn, l, kv, p, use)
                        elif use[0] == "V":
                            c0, banks = value_chunks(use)
                            act.wait_ge(probs_used, b * NCH + (NCH * B * l + c0 + 4 * banks + 3))
                            values(phase, turn, p, use)

                def turn(b, p, i, l=l):
                    cross_turn(f"cross{l}", b, b, p, i * (16 * stack_dmas(l)) + (stack_count(l, 0) + (16 * stack_dmas(l) if p else 0)))

                def end(l=l):
                    cross_turn(f"cross14_{l}", 0, B - 2, 0, None)
                    cross_turn(f"cross15_{l}", 0, B - 1, 1, None)

                turns(act, turn, end)
                reciprocals(f"C{l}")
                norm(f"C{l}", 3 * l + 2)
                for j in range(4):
                    t = full(act, f"C{l}", f"h{j}")
                    act.activation(two(hidden[j]), halves(t), ACT.Gelu if l == EXACT_GELU else ACT.Gelu_apprx_tanh,
                                   bias=bi(l, "f1", j)).then_inc(slot_free(f"C{l}", f"h{j}"), 1)
                if l < L - 1:
                    act.preload_act_table_set("natural_log_exp_and_others")

        @block.vector
        def _(dve):
            steps = [0]

            def step(ins):
                steps[0] += 1
                ins.then_inc(dve_step, 1)
                dve.wait_ge(dve_step, steps[0])

            dve.wait_ge(const_loaded, 48)
            rows = slice(96, KR)
            k_rows, q_rows, shift_rows = (const[rows, CO["rows"][0] + j:CO["rows"][0] + j + 1] for j in range(3))

            def fill_key_rows():
                for i in range(2):
                    dve.tensor_copy(k_stack[i][rows, :, :].rearrange("p g n -> p (g n)"), k_rows.to_broadcast([2, G * S]))\
                        .then_inc(rows_init, 1)

            fill_key_rows()
            for i in range(2):
                dve.tensor_copy(q_max[i][rows, :], q_rows.to_broadcast([2, HQ])).then_inc(rows_init, 1)

            dve.wait_ge(exp_cond, 1)
            step(dve.tensor_scalar(silu[:, :], silu[:, :], 1.0, None, ALU.add))
            step(dve.reciprocal(silu[:, :], silu[:, :]))
            dve.tensor_tensor(out=silu[:, :], in0=silu[:, :], in1=cond[:, :], op=ALU.mult).then_inc(silu_ready, 1)

            def ctx_centre(phase, turn, p):
                for part in ("m0", "m1"):
                    t = full(dve, phase, part, turn)
                    dve.tensor_tensor(out=keys(ctx_centred[p], part), in0=keys(ctx_T[:, p, :], part), in1=t[:, 0:thirds(part)[1], 0:TH], op=ALU.subtract)\
                        .then_inc(slot_free(phase, part), 1)

            def ctx_divide(b, p, half):
                dve.wait_ge(norm_stored[p], half * 16 + 16)
                dve.wait_ge(ctx_rstd, b + 1)
                dve.tensor_tensor(out=ctx_out[p], in0=ctx_centred[p], in1=deviation, op=ALU.mult)\
                    .then_inc(ctx_normed, 1)

            def ctx_turn(b, p, i):
                dve.wait_ge(ctx_normed, b + 1)
                ctx_centre("ctx", b, 1 - p)
                ctx_divide(b, p, i)

            def ctx_end():
                ctx_turn(B - 2, 0, 7)
                ctx_divide(B - 1, 1, 7)

            ctx_centre("ctx_first", 0, 0)
            turns(dve, ctx_turn, ctx_end)

            def norm(phase, l, k, which):
                t = full(dve, phase, "mean")
                dve.tensor_tensor(out=two(xc[:, :]), in0=two(x[:, :]), in1=halves(t), op=ALU.subtract)\
                    .then_inc(slot_free(phase, "mean"), 1)
                dve.wait_ge(rstd_ready, k + 1)
                ins = dve.tensor_tensor(out=xn[:, :], in0=xc[:, :], in1=rstd[:, :], op=ALU.mult)
                if which in (0, 2):
                    step(ins)
                    scale, shift = (mod[:, 1, :], mod[:, 0, :]) if which == 0 else (mod[:, 4, :], mod[:, 3, :])
                    step(dve.tensor_tensor(out=by_batch(xn[:, :]), in0=by_batch(xn[:, :]), in1=per_token(scale), op=ALU.mult))
                    ins = dve.tensor_tensor(out=by_batch(xn[:, :]), in0=by_batch(xn[:, :]), in1=per_token(shift), op=ALU.add)
                elif l == AFFINE:
                    step(ins)
                    ins = dve.tensor_scalar(xn[:, :], xn[:, :], bi(l, "g2"), bi(l, "b2"), ALU.mult, ALU.add)
                ins.then_inc(xn_ready, 1)

            def gated(phase, use, b_ap, gate):
                t = full(dve, phase, use)
                for h in range(2):
                    ins = dve.scalar_tensor_tensor(out=by_batch(xn[:, h * HALF:(h + 1) * HALF]), in0=by_batch(t[:, h, 0:HALF]),
                                                   scalar=b_ap, in1=per_token(gate[:, h * 8:(h + 1) * 8], 8),
                                                   op0=ALU.add, op1=ALU.mult)
                    if h == 0:
                        step(ins)
                ins.then_inc(slot_free(phase, use), 1)
                freed(dve, phase, use)
                dve.tensor_tensor(out=x[:, :], in0=x[:, :], in1=xn[:, :], op=ALU.add).then_inc(x_ready, 1)

            def normalise_heads(count):
                for n, (den, heads, dst) in enumerate(((rstd, heads_a, qT), (sq, heads_b, kT))):
                    dve.wait_ge(den_ready, count + n + 1)
                    dve.tensor_tensor(out=dst[:, :], in0=heads[:, :], in1=den[:, :], op=ALU.mult).then_inc(heads_ready, 1)

            masks3 = co("third").unsqueeze(2).to_broadcast([D, 3, N])
            extracted = [0]

            def extract(b, count):
                dve.tensor_tensor(out=masked[:, :, :], in0=acc_a[:, 0:RA].rearrange("p (t n) -> p t n", n=N), in1=masks3,
                                  op=ALU.mult).then_inc(acc_free, 1)
                dve.wait_ge(acc_free, count)
                at = bass.ds(b * N, N)
                dve.tensor_reduce(out=heads_a[:, at], in_=masked[:, :, :].rearrange("p t n -> p n t"), axis=AX.X, op=ALU.add)\
                    .then_inc(acc_free, 1)
                dve.tensor_copy(heads_b[:, at], acc_b[:, 0:N]).then_inc(acc_free, 1)

            def reduce_tile(phase, turn, c):
                t = full(dve, phase, f"M{c}", turn)
                pair = 2 * (c % 4)
                dve.reduce_max(part_max[:, c // 4, pair:pair + 2], t[0:PAIR, :, 0:TH], AX.X)\
                    .then_inc(slot_free(phase, f"M{c}"), 1)

            def negate_maxima(phase, turn):
                freed(dve, phase, f"M{NCH - 1}", turn)
                dve.tensor_reduce(out=neg_max[:, :], in_=part_max[:, :, :].rearrange("q s p -> q p s"), axis=AX.X, op=ALU.max,
                                  negate=True).then_inc(max_ready, 1)

            def shift(phase, turn, p):
                t = full(dve, phase, "R", turn)
                dve.tensor_scalar(two(q_score[p][rows, :]), t[rows, :, 0:HALF], shift_rows, q_rows, ALU.mult, ALU.add)\
                    .then_inc(slot_free(phase, "R"), 1)

            def keys_low(phase, turn, l, part, count):
                dve.wait_ge(hi_ready, count)
                s0, ns = thirds(part)
                s, _ = uses.at(phase, part)
                dve.scalar_tensor_tensor(out=keys(k_lo, part), in0=slot[s][:, 0:ns, 0:TH], scalar=bi(l, "kc"),
                                         in1=keys(k_hi[:, :].bitcast(F32), part), op0=ALU.add, op1=ALU.subtract)\
                    .then_inc(slot_free(phase, part), 1)

            for l in range(L):
                if l == MASKED + 1:
                    fill_key_rows()
                for b in range(2):
                    for n, part in enumerate(KV_USES[0:3]):
                        keys_low(f"kv{b}_{l}", 0, l, part, 3 * (B * l + b) + n + 1)
                t = full(dve, f"A{l}", "mod")
                step(dve.tensor_tensor(out=mod[:, :, :], in0=t[:, 0, 0:6 * B].rearrange("p (k b) -> p k b", b=B),
                                       in1=bi(l, "mod", width=6).unsqueeze(2).to_broadcast([D, 6, B]), op=ALU.add))
                for k in (1, 4):
                    step(dve.tensor_scalar(mod[:, k, :], mod[:, k, :], 1.0, None, ALU.add))
                dve.tensor_tensor(out=proj_bias[:, :], in0=t[:, 0, 6 * B:6 * B + 2], in1=bi(l, "p", width=2), op=ALU.add)\
                    .then_inc(slot_free(f"A{l}", "mod"), 1)
                norm(f"A{l}", l, 3 * l, 0)

                def self_scores_less_max(phase, use, turn, b, p, l=l):
                    t = full(dve, phase, use, turn)
                    scores = by_batch(t[0:PAIR, 0, 0:NP * N])
                    dve.tensor_reduce(out=neg_max_self[:, p, :], in_=scores, axis=AX.X, op=ALU.max, negate=True)\
                        .then_inc(self_max, 1)
                    dve.wait_ge(self_max, b + (B * l + 1))
                    dve.tensor_tensor(out=by_batch(probs_self[p]), in0=scores,
                                      in1=neg_max_self[:, p, :].unsqueeze(2).to_broadcast([PAIR, NP, N]), op=ALU.add)\
                        .then_inc(slot_free(phase, use), 1)

                def self_extract(b, l=l):
                    dve.wait_ge(self_done, b + (B * l + 2))
                    extract(b, b * 3 + (3 * 2 * B * l + 4))

                def self_turn(b, p, i, l=l):
                    full(dve, f"self{l}", "T", b)
                    self_scores_less_max(f"self{l}", "S", b, b + 2, p)
                    self_extract(b)

                for b in range(2):
                    self_scores_less_max(f"self_first{l}", f"S{b}", 0, b, b)
                turns(dve, self_turn)
                for b in range(B - 2, B):
                    self_extract(b)
                normalise_heads(4 * l)
                gated(f"B{l}", "p", proj_bias[:, 0:1], mod[:, 2, :])
                norm(f"B{l}", l, 3 * l + 1, 1)
                for g in range(G):
                    t = full(dve, f"B{l}", f"q{g}")
                    dve.wait_ge(qhi_ready, G * l + g + 1)
                    low = two(q_split[64:96, g, :])
                    dve.scalar_tensor_tensor(out=low, in0=halves(t, slice(64, 96)), scalar=bi(l, "qr", g, slice(64, 96)),
                                             in1=two(q_split[64:96, g, :].bitcast(F32)), op0=ALU.add, op1=ALU.subtract)\
                        .then_inc(slot_free(f"B{l}", f"q{g}"), 1)
                for c in range(NCH):
                    reduce_tile(f"max0_{l}", 0, c)
                negate_maxima(f"max0_{l}", 0)
                shift(f"max0_{l}", 0, 0)

                def cross_turn(phase, turn, b, p, with_max, hi, l=l):
                    for use in cross_uses(with_max, hi is not None):
                        if use[0] == "M":
                            reduce_tile(phase, turn, int(use[1:]))
                            if use == f"M{NCH - 1}":
                                negate_maxima(phase, turn)
                        elif use[0] == "K":
                            keys_low(phase, turn, l, use, hi + int(use[1]))
                        elif use == "R":
                            shift(phase, turn, 1 - p)
                    dve.wait_ge(probs_used, b * NCH + (NCH * (B * l + 1) + 3))
                    extract(b, b * 3 + (3 * (2 * B * l + B) + 4))

                def turn(b, p, i, l=l):
                    cross_turn(f"cross{l}", b, b, p, True, b * 3 + (3 * (B * l + 2) + 1))

                def end(l=l):
                    cross_turn(f"cross14_{l}", 0, B - 2, 0, True, None)
                    cross_turn(f"cross15_{l}", 0, B - 1, 1, False, None)

                turns(dve, turn, end)
                normalise_heads(4 * l + 2)
                t = full(dve, f"C{l}", "p")
                dve.scalar_tensor_tensor(out=two(xn[:, :]), in0=halves(t), scalar=proj_bias[:, 1:2], in1=two(x[:, :]),
                                         op0=ALU.add, op1=ALU.add).then_inc(slot_free(f"C{l}", "p"), 1)
                freed(dve, f"C{l}", "p")
                dve.tensor_copy(x[:, :], xn[:, :]).then_inc(x_ready, 1)
                norm(f"C{l}", l, 3 * l + 2, 2)
                gated(f"C{l}", "y", bi(l, "f2"), mod[:, 5, :])

        @block.tensor
        def _(pe):
            for i in range(3):
                pe.sem_inc(psum_free[i], 1)
            pe.sem_inc(probs_used, 3)
            pe.sem_inc(acc_free, 3)
            pe.sem_inc(self_done, 1)
            pe.sem_inc(ctx_normed, 1)
            for p in range(2):
                pe.sem_inc(norm_stored[p], 16)
            pe.wait_ge(const_loaded, 48)

            def ctx_sum(phase, turn, parts, src):
                for part in parts:
                    t = claim(pe, phase, part, turn)
                    s0, ns = thirds(part)
                    for a in range(ns):
                        mm = pe.matmul(t[:, a, 0:TH], co("mean"), src[:, (s0 + a) * TH:(s0 + a + 1) * TH], start=True, stop=True)
                    mm.then_inc(slot_full(phase, part), 1)

            def ctx_turn(b, p, i):
                pe.wait_ge(raw_loaded[1 - p], i * 16 + 16 * (1 + p))
                ctx_sum("ctx", b, ("m0", "m1"), ctx_T[:, 1 - p, :])
                pe.wait_ge(ctx_squared, b + 1)
                ctx_sum("ctx", b, ("v0", "v1"), ctx_squares[p])

            def ctx_end():
                ctx_turn(B - 2, 0, 7)
                pe.wait_ge(ctx_squared, B)
                ctx_sum("ctx_last", 0, ("v0", "v1"), ctx_squares[1])

            pe.wait_ge(raw_loaded[0], 16)
            ctx_sum("ctx_first", 0, ("m0", "m1"), ctx_T[:, 0, :])
            turns(pe, ctx_turn, ctx_end)

            def dense(phase, use, terms, rows=D):
                t = claim(pe, phase, use)
                for a in range(2):
                    for n, (lhsT, rhs) in enumerate(terms):
                        mm = pe.matmul(t[0:rows, a, 0:HALF], lhsT, rhs[:, a * HALF:(a + 1) * HALF], start=(n == 0),
                                       stop=(n == len(terms) - 1))
                mm.then_inc(slot_full(phase, use), 1)

            def norm(phase, k):
                if k == 0:
                    pe.wait_ge(x_loaded, 16)
                else:
                    pe.wait_ge(x_ready, k)
                dense(phase, "mean", [(co("mean"), x)])
                pe.wait_ge(x_squared, k + 1)
                dense(phase, "var", [(co("mean"), sq)])
                pe.wait_ge(xn_ready, k + 1)

            def keys_product(phase, turn, p, part):
                t = claim(pe, phase, part, turn)
                s0, ns = thirds(part)
                for a in range(ns):
                    mm = pe.matmul(t[:, a, 0:TH], W("kc"), ctx_T[:, p, (s0 + a) * TH:(s0 + a + 1) * TH], start=True, stop=True)
                mm.then_inc(slot_full(phase, part), 1)

            def values_product(phase, turn, p, part):
                t = claim(pe, phase, part, turn)
                c0, banks = value_chunks(part)
                for c in range(4 * banks):
                    at = (c0 + c) * KC
                    mm = pe.matmul(t[0:KC, c // 4, c % 4 * D:(c % 4 + 1) * D], ctx_T[:, p, at:at + KC], W("vc"),
                                   start=True, stop=True)
                mm.then_inc(slot_full(phase, part), 1)

            def weigh(v, pr, first, last):
                for lo, acc, r0, rn in ((0, acc_a, 0, RA), (33, acc_b, RA, N)):
                    for g in range(G):
                        mm = pe.matmul(acc[32 * g:32 * g + 32, 0:rn], v[:, g, lo:lo + 32], pr[:, GQ * g + r0:GQ * g + r0 + rn],
                                       start=first, stop=last)
                return mm

            for l in range(L):
                pe.wait_ge(w1_loaded, 16 * (l + 1))
                for b in range(2):
                    pe.wait_ge(ctx_loaded[b], 16 * (B // 2) * l + 16)
                    for part in KV_USES[0:3]:
                        keys_product(f"kv{b}_{l}", 0, b, part)
                    for part in KV_USES[3:]:
                        values_product(f"kv{b}_{l}", 0, b, part)

                if l == 0:
                    pe.wait_ge(silu_ready, 1)
                t = claim(pe, f"A{l}", "mod")
                for k in range(6):
                    pe.matmul(t[:, 0, k * B:(k + 1) * B], W("mod", k * D, (k + 1) * D), silu[:, :], start=True, stop=True)
                for n, w in enumerate(("p", "cp")):
                    v = ("vA", "vB") if n == 0 else ("cvA", "cvB")
                    pe.matmul(t[:, 0, 6 * B + n:6 * B + n + 1], W(w + "A"), bi(l, v[0]), start=True, stop=False)
                    mm = pe.matmul(t[:, 0, 6 * B + n:6 * B + n + 1], W(w + "B"), bi(l, v[1]), start=False, stop=True)
                mm.then_inc(slot_full(f"A{l}", "mod"), 1)
                norm(f"A{l}", 3 * l)
                dense(f"A{l}", "q", [(W("q"), xn)])
                dense(f"A{l}", "k", [(W("k"), xn)])
                freed(pe, f"A{l}", "k")

                def self_scores(phase, use, turn, b, p, l=l):
                    pe.wait_ge(self_operands, b * 3 + (3 * B * l + 3))
                    t = claim(pe, phase, use, turn)
                    for n in range(NP):
                        mm = pe.matmul(t[0:PAIR, 0, n * N:(n + 1) * N], q_blocks[p][:, n * PAIR:(n + 1) * PAIR],
                                       k_batch[:, p, :], start=True, stop=True)
                    mm.then_inc(slot_full(phase, use), 1)

                def self_values(phase, use, turn, p):
                    t = claim(pe, phase, use, turn)
                    pe.matmul(t[0:N, 0, 0:D], x_batch[:, p, :], W("v"), start=True, stop=True)\
                        .then_inc(slot_full(phase, use), 1)

                def self_transpose(phase, use, turn, b, p, l=l):
                    pe.wait_ge(self_probs, b + (B * l + 1))
                    s, n = uses.at(phase, use, turn)
                    wait_alone(pe, psum_free[s], n + 1)
                    t = slot[s]
                    for n in range(NP):
                        c = (n % 4) * PAIR
                        mm = pe.transpose(t[0:N, n // 4, c:c + PAIR], probs_self[p][:, n * N:(n + 1) * N],
                                          co("ident", slice(0, PAIR))[:, 0:PAIR])
                    mm.then_inc(slot_full(phase, use), 1)

                def self_weigh(phase, use, turn, b, p, l=l):
                    freed(pe, phase, use, turn)
                    wait_alone(pe, acc_free, b * 3 + (3 * 2 * B * l + 3))
                    weigh(v_self[:, p, :, :], probs_T[p], True, True).then_inc(self_done, 1)

                def self_turn(b, p, i, l=l):
                    self_transpose(f"self{l}", "T", b, b, p)
                    self_scores(f"self{l}", "S", b, b + 2, p)
                    self_weigh(f"self{l}", "T", b, b, p)
                    self_values(f"self{l}", "V", b, p)

                for b in range(2):
                    self_scores(f"self_first{l}", f"S{b}", 0, b, b)
                    self_values(f"self_first{l}", f"V{b}", 0, b)
                turns(pe, self_turn)
                for b in range(2):
                    self_transpose(f"self_last{l}", f"T{b}", 0, B - 2 + b, b)
                for b in range(2):
                    self_weigh(f"self_last{l}", f"T{b}", 0, B - 2 + b, b)

                def project(phase, layer_half, wa, wb, l=l):
                    pe.wait_ge(acc_free, 3 * (2 * B * l + B * (1 + layer_half)) + 3)
                    dense(phase, "dA", [(co("selA"), heads_a)])
                    dense(phase, "dB", [(co("selB"), heads_b)])
                    pe.wait_ge(heads_ready, 4 * l + 2 * layer_half + 2)
                    dense(phase, "p", [(wa, qT), (wb, kT)])

                project(f"B{l}", 0, W("pA"), W("pB"))
                norm(f"B{l}", 3 * l + 1)
                for g in range(G):
                    dense(f"B{l}", f"q{g}", [(W("qr", 96 * g, 96 * g + 96), xn)], 96)

                def max_tile(phase, turn, p, c):
                    t = claim(pe, phase, f"M{c}", turn)
                    k = c // 4
                    for a in range(2):
                        n = 2 * (c % 4) + a
                        mm = pe.matmul(t[0:PAIR, a, 0:TH], q_max[p][0:KR - 1, n * PAIR:(n + 1) * PAIR],
                                       k_stack[p][0:KR - 1, n // 2, k * TH:(k + 1) * TH], start=True, stop=True)
                    mm.then_inc(slot_full(phase, f"M{c}"), 1)

                def max_rows(phase, turn, count):
                    t = claim(pe, phase, "R", turn)
                    pe.wait_ge(max_ready, count)
                    for n in range(NP):
                        c = (n % 4) * PAIR
                        mm = pe.matmul(t[96:KR, n // 4, c:c + PAIR], neg_max[:, n:n + 1].to_broadcast([PAIR, 2]),
                                       co("ident", slice(0, PAIR))[:, 0:PAIR], start=True, stop=True)
                    mm.then_inc(slot_full(phase, "R"), 1)

                def score_chunk(phase, turn, p, c):
                    t = claim(pe, phase, f"C{c}", turn)
                    for g in range(G):
                        mm = pe.matmul(t[0:KC, g // 2, (g % 2) * GQ:(g % 2 + 1) * GQ], k_stack[p][:, g, c * KC:(c + 1) * KC],
                                       q_score[p][:, g * GQ:(g + 1) * GQ], start=True, stop=True)
                    mm.then_inc(slot_full(phase, f"C{c}"), 1)

                def weigh_chunk(phase, turn, p, c):
                    freed(pe, phase, f"C{c}", turn)
                    weigh(v_ctx[p][:, c, :, :], probs[:, c % 3, :], c == 0, c == NCH - 1).then_inc(probs_used, 1)

                def cross_turn(phase, turn, b, p, stack, ctx_count, l=l):
                    pe.wait_ge(qscore_ready, b + (B * l + 1))
                    for use in cross_uses(stack is not None, ctx_count is not None):
                        n = int(use[1:] or 0)
                        if use[0] == "M":
                            if n == 0:
                                pe.wait_ge(qmax_ready, b + (B * l + 2))
                            if n in (0, 8):
                                pe.wait_ge(stack_loaded[1 - p][n // 8], stack)
                            max_tile(phase, turn, 1 - p, n)
                        elif use[0] == "C":
                            score_chunk(phase, turn, p, n)
                            if n == 1:
                                pe.wait_ge(acc_free, b * 3 + (3 * (2 * B * l + B) + 3))
                            if n > 0:
                                weigh_chunk(phase, turn, p, n - 1)
                        elif use == "K0":
                            pe.wait_ge(ctx_loaded[p], ctx_count)
                            keys_product(phase, turn, p, use)
                        elif use[0] == "K":
                            keys_product(phase, turn, p, use)
                        elif use[0] == "V":
                            if n == 1:
                                weigh_chunk(phase, turn, p, NCH - 1)
                            values_product(phase, turn, p, use)
                        elif use == "R":
                            max_rows(phase, turn, b + (B * l + 2))
                    if ctx_count is None:
                        weigh_chunk(phase, turn, p, NCH - 1)

                pe.wait_ge(qmax_ready, B * l + 1)
                if l == 0:
                    pe.wait_ge(rows_init, 4)
                elif l == MASKED + 1:
                    pe.wait_ge(rows_init, 6)
                for c in range(NCH):
                    if c in (0, 8):
                        pe.wait_ge(stack_loaded[0][c // 8], stack_count(l, 0))
                    max_tile(f"max0_{l}", 0, 0, c)
                max_rows(f"max0_{l}", 0, B * l + 1)

                def turn(b, p, i, l=l):
                    per = 16 * stack_dmas(l)
                    cross_turn(f"cross{l}", b, b, p, i * per + (stack_count(l, 0) + (per if p else 0)),
                               i * 16 + (16 * (B // 2) * l + 32))

                def end(l=l):
                    cross_turn(f"cross14_{l}", 0, B - 2, 0, stack_count(l, 7), None)
                    cross_turn(f"cross15_{l}", 0, B - 1, 1, None, None)

                turns(pe, turn, end)

                project(f"C{l}", 1, W("cpA"), W("cpB"))
                norm(f"C{l}", 3 * l + 2)
                pe.wait_ge(w2_loaded, 16 * (l + 1))
                for j in range(4):
                    dense(f"C{l}", f"h{j}", [(w2[:, j * D:(j + 1) * D], xn)])
                for j in range(4):
                    freed(pe, f"C{l}", f"h{j}")
                dense(f"C{l}", "y", [(w2[:, (4 + j) * D:(5 + j) * D], hidden[j]) for j in range(4)])


def constants():
    c = np.zeros((D, CO_COLS), np.float32)

    def put(name, a):
        o, w = CO[name]
        c[:, o:o + w] = a

    r = np.arange(D)
    first = np.minimum(r % 32 // VS, 2)
    put("mean", np.full((D, D), 1.0 / D, np.float32))
    put("ident", np.eye(D, dtype=np.float32))
    put("selA", (r[:, None] == (r // 32 * 32 + first * VS + HD)[None, :]).astype(np.float32))
    put("selB", (r[:, None] == (r // 32 * 32 + HD)[None, :]).astype(np.float32))
    put("head16", (r[:, None] // HD == np.arange(NH)[None, :]).astype(np.float32))
    put("head4", (r[:, None] % 32 // HD == np.arange(GH)[None, :]).astype(np.float32))
    put("third", (first[:, None] == np.arange(3)[None, :]).astype(np.float32))
    rows = np.zeros((D, 4), np.float32)
    rows[97, 0] = 1.0
    rows[96, 1] = 1.0
    rows[97, 2] = 1.0
    put("rows", rows)
    put("eps", np.full((D, 1), EPS, np.float32))
    return c


def by_rows(w):
    a, b = np.zeros((D, w.shape[1]), w.dtype), np.zeros((D, w.shape[1]), w.dtype)
    for g in range(G):
        for t in range(GH):
            src = w[(GH * g + t) * HD:(GH * g + t + 1) * HD]
            if t < 3:
                a[32 * g + VS * t:32 * g + VS * t + HD] = src
            else:
                b[32 * g:32 * g + HD] = src
    return a, b


def kernel(**inputs):
    import concourse.bacc as bacc
    from concourse.bass_utils import run_bass_kernel_spmd

    a = {k: np.asarray(v) for k, v in inputs.items()}
    names = [
        dict(mod="W_mod", bmod="b_mod", qkv="W_qkv", bqkv="b_qkv", p="W_proj", bp="b_proj", q="W_qc", bq="b_qc", kv="W_kvc",
             bkv="b_kvc", cp="W_cproj", bcp="b_cproj", f1="W_mlp1", bf1="b_mlp1", f2="W_mlp2", bf2="b_mlp2"),
        dict(mod="ada_w", bmod="ada_b", qkv="qkv_w", bqkv="qkv_b", p="self_o_w", bp="self_o_b", q="q_w", bq="q_b", kv="kv_w",
             bkv="kv_b", cp="cross_o_w", bcp="cross_o_b", f1="mlp_w1", bf1="mlp_b1", f2="mlp_w2", bf2="mlp_b2"),
        dict(mod="ada_w", bmod="ada_b", qkv="qkv_w", bqkv="qkv_b", p="sa_proj_w", bp="sa_proj_b", q="q_w", bq="q_b",
             kv="kv_w", bkv="kv_b", cp="ca_proj_w", bcp="ca_proj_b", f1="fc1_w", bf1="fc1_b", f2="fc2_w", bf2="fc2_b"),
        dict(mod="adaln_w", bmod="adaln_b", qkv="qkv_w", bqkv="qkv_b", p="sa_proj_w", bp="sa_proj_b", q="q_w", bq="q_b",
             kv="kv_w", bkv="kv_b", cp="ca_proj_w", bcp="ca_proj_b", f1="fc1_w", bf1="fc1_b", f2="fc2_w", bf2="fc2_b"),
    ]
    w1 = np.zeros((L, D, W1_COLS), np.float32)
    w2 = np.zeros((L, D, W2_COLS), np.float32)
    bias = np.zeros((D, L * BI_COLS), np.float32)
    for l, name in enumerate(names):
        p = {k: a[f"L{l}_xcond_{v}"] for k, v in name.items()}
        parts = {"mod": p["mod"], "q": p["qkv"][:, 0:D], "k": p["qkv"][:, D:2 * D], "v": p["qkv"][:, 2 * D:3 * D],
                 "kc": p["kv"][:, 0:D], "vc": p["kv"][:, D:2 * D]}
        parts["pA"], parts["pB"] = by_rows(p["p"])
        parts["cpA"], parts["cpB"] = by_rows(p["cp"])
        parts["qr"] = np.concatenate([p["q"][:, 32 * g:32 * g + 32] for g in range(G) for _ in range(3)], axis=1)
        for k, m in parts.items():
            w1[l, :, W1[k][0]:W1[k][0] + W1[k][1]] = m
        w2[l, :, 0:4 * D] = p["f1"]
        w2[l, :, 4 * D:8 * D] = p["f2"].reshape(4, D, D).transpose(1, 0, 2).reshape(D, 4 * D)
        cols = {"mod": p["bmod"].reshape(6, D).T, "q": p["bqkv"][0:D, None], "k": p["bqkv"][D:2 * D, None],
                "p": p["bp"][:, None], "cp": p["bcp"][:, None], "kc": p["bkv"][0:D, None],
                "f1": p["bf1"].reshape(4, D).T, "f2": p["bf2"][:, None]}
        cols["vA"], cols["vB"] = by_rows(p["bqkv"][2 * D:3 * D, None])
        cols["cvA"], cols["cvB"] = by_rows(p["bkv"][D:2 * D, None])
        if l == AFFINE:
            cols["g2"], cols["b2"] = a["L1_xcond_norm2_g"][:, None], a["L1_xcond_norm2_b"][:, None]
        for k, m in cols.items():
            o = l * BI_COLS + BI[k][0]
            bias[:, o:o + BI[k][1]] = m
        for g in range(G):
            for r in range(3):
                bias[32 * r:32 * r + 32, l * BI_COLS + BI["qr"][0] + g] = p["bq"][32 * g:32 * g + 32]

    arrays = {
        "x_in": np.ascontiguousarray(a["x"].reshape(T, D).T),
        "cond_in": np.ascontiguousarray(a["cond_1024"].T),
        "ctx_in": np.ascontiguousarray(a["ctx_1024"].transpose(0, 2, 1)),
        "mask_in": np.ascontiguousarray(a["mask_BxS2_bf0"]).view(np.int32),
        "w1_in": w1, "w2_in": w2, "bias_in": bias, "const_in": constants(),
    }
    nc = bacc.Bacc("TRN2", target_bir_lowering=False, num_devices=1)
    args = [nc.dram_tensor(k, v.shape, mybir.dt.from_np(v.dtype), kind="ExternalInput").ap() for k, v in arrays.items()]
    out = nc.dram_tensor("out", (D, T), mybir.dt.float32, kind="ExternalOutput").ap()
    blocks_kernel(nc, *args, out)
    r = run_bass_kernel_spmd(nc, [arrays], core_ids=[0])
    return np.ascontiguousarray(r.results[0]["out"].T).reshape(B, N, D)
```

```python
from contextlib import ExitStack

import concourse.bass as bass
import numpy as np
from concourse import mybir
from concourse.alu_op_type import AluOpType as ALU

B, N, D, NH, HD, S = 16, 56, 128, 16, 8, 1500
L = 4
T = B * N
HALF = T // 2
KC = 125
NCH = S // KC
TH = 500
PAIR = 2 * N
NP = NH // 2
G, GH = 4, 4
HQ = NH * N
GQ = GH * N
RA = 3 * N
VS = HD + 3
VG = 66
KR = 98
LAG = 2
SCALE = float(HD) ** -0.5
EPS = 1e-6
MASKED = 2
NORM_CTX = 0
AFFINE = 1
EXACT_GELU = 2

W1 = {}
for _n, _w in (("mod", 6 * D), ("q", D), ("k", D), ("v", D), ("pA", D), ("pB", D), ("cpA", D), ("cpB", D),
               ("qr", G * 96)):
    W1[_n] = (sum(w for _, w in W1.values()), _w)
W1_COLS = sum(w for _, w in W1.values())
W2_COLS = 8 * D
HALVES = (0, 1)
BI = {}
for _n, _w in (("mod", 6), ("q", 1), ("k", 1), ("vA", 1), ("vB", 1), ("cvA", 1), ("cvB", 1), ("p", 1), ("cp", 1),
               ("qr", G), ("kc", 1), ("f1", 4), ("f2", 1), ("g2", 1), ("b2", 1)):
    BI[_n] = (sum(w for _, w in BI.values()), _w)
BI_COLS = sum(w for _, w in BI.values())
CO = {}
for _n, _w in (("mean", D), ("ident", D), ("selA", D), ("selB", D), ("head16", NH), ("head4", GH), ("third", 3),
               ("rows", 4), ("eps", 1)):
    CO[_n] = (sum(w for _, w in CO.values()), _w)
CO_COLS = sum(w for _, w in CO.values())


class PsumUses:

    def __init__(self):
        self.base, self.total = {}, [0, 0, 0]

    def phase(self, name, seq, repeat=1):
        per = [len(range(s, len(seq), 3)) for s in range(3)]
        self.base[name] = (list(self.total), per, {u: i for i, u in enumerate(seq)})
        for s in range(3):
            self.total[s] += per[s] * repeat

    def at(self, phase, use, turn=0):
        base, per, place = self.base[phase]
        i = place[use]
        return i % 3, turn * per[i % 3] + (base[i % 3] + i // 3)


def cross_uses(with_max, with_kv):
    order = ("M0 C0 M1 C1 M2 C2 M3 C3 M4 C4 M5 K0 C5 V0 M6 C6 M7 K1 C7 C8 M8 C9 M9 C10 M10 M11 K2 C11 R V1")
    if not with_kv:
        order = "M0 M1 C0 M2 C1 M3 C2 M4 C3 M5 C4 M6 C5 M7 C6 M8 C7 M9 C8 M10 C9 M11 C10 C11 R"
    return [u for u in order.split() if with_max or u[0] not in "MR"]


KV_USES = ["K0", "K1", "K2", "V0", "V1"]
FIRST_MAX = "M0 M1 M2 M3 V0 M4 M5 M6 M7 M8 M9 M10 M11 R V1".split()


def psum_plan():
    uses = PsumUses()
    uses.phase("ctx_first", ["m0", "m1"])
    uses.phase("ctx", ["m0", "m1", "v0"], B - 1)
    uses.phase("ctx_last", ["v0"])
    uses.phase("kv", KV_USES)
    for l in range(L):
        uses.phase(f"A{l}", ["mean0", "mean1", "mod", "var0", "var1", "q0", "k0", "q1", "k1"] + KV_USES[0:3])
        uses.phase(f"self{l}", ["S", "T", "H"], B)
        uses.phase(f"B{l}", ["dA0", "dB0", "dA1", "dB1", "p0", "p1", "mean0", "mean1", "var0", "var1"]
                   + [f"c{g}{h}" for h in HALVES for g in range(G)])
        uses.phase(f"max0_{l}", FIRST_MAX)
        uses.phase(f"cross{l}", cross_uses(True, True), B - 2)
        uses.phase(f"cross14_{l}", cross_uses(True, False))
        uses.phase(f"cross15_{l}", cross_uses(False, False))
        uses.phase(f"C{l}", (KV_USES[0:3] if l < L - 1 else []) + ["dA0", "dB0", "dA1", "dB1"]
                   + (KV_USES[3:] if l < L - 1 else []) + ["p0", "p1", "mean0", "mean1", "var0", "var1"]
                   + [f"h{j}{h}" for h in HALVES for j in range(4)] + ["y0", "y1"])
    return uses


def kv_phase(l, b, part):
    if b:
        return f"A{l}" if part[0] == "K" else f"max0_{l}"
    return f"C{l - 1}" if l else "kv"


def stack_dmas(l):
    return 3 * G + (l == MASKED)


def stack_count(l, half):
    return half * (16 * stack_dmas(l)) + 16 * ((B // 2) * sum(stack_dmas(k) for k in range(l)) + stack_dmas(l))


def blocks_kernel(nc, x_d, cond_d, ctx_d, mask_d, w1_d, wkv_d, w2_d, bias_d, const_d, out_d):
    F32, F32R, U8 = mybir.dt.float32, mybir.dt.float32r, mybir.dt.uint8
    ACT, AX = mybir.ActivationFunctionType, mybir.AxisListType
    uses = psum_plan()
    ctx = ExitStack()
    with ctx:
        def sb(name, shape, dt=F32):
            return ctx.enter_context(nc.sbuf_tensor(name, shape, dt))

        def sem(name):
            return ctx.enter_context(nc.semaphore(name))

        ctx_norm_d = nc.dram_tensor("ctx_norm", (B, D, S), F32, kind="Internal").ap()

        w1 = sb("w1", [D, W1_COLS])
        w2 = sb("w2", [D, W2_COLS])
        w_kv = sb("w_kv", [D, 2, 2 * D])
        bias = sb("bias", [D, L * BI_COLS])
        const = sb("const", [D, CO_COLS])
        cond = sb("cond", [D, B])
        silu = sb("silu", [D, B])
        x = sb("x", [D, T])
        norm_work = sb("norm_work", [D, 4 * T])
        xc = norm_work[:, 0:T]
        sq = norm_work[:, T:2 * T]
        rstd = norm_work[:, 2 * T:3 * T]
        xn = norm_work[:, 3 * T:4 * T]
        qk = sb("qk", [D, 2 * T])
        qT, kT = qk[:, 0:T], qk[:, T:2 * T]
        mod = sb("mod", [D, 6, B])
        proj_bias = sb("proj_bias", [D, 2])
        work = sb("work", [D, 4 * T])
        hidden = [work[:, j * T:(j + 1) * T] for j in range(4)]
        q_blocks = [work[:, 0:HQ], work[:, HQ:2 * HQ]]
        probs_T = [work[0:N, 2 * HQ:3 * HQ], work[0:N, 3 * HQ:4 * HQ]]
        self_raw = [sq[0:N, :], rstd[0:N, :]]
        x_batch = sb("x_batch", [D, 2, N])
        k_batch = sb("k_batch", [D, 2, N])
        v_self = sb("v_self", [N, 2, G, VG])
        heads_a = sb("heads_a", [D, T])
        heads_b = sb("heads_b", [D, T])
        masked = sb("masked", [D, 3, N])
        part_max = sb("part_max", [PAIR, 3, NP])
        neg_max = sb("neg_max", [PAIR, NP])
        neg_max_self = sb("neg_max_self", [PAIR, NP], F32R)
        ident_r = sb("ident_r", [PAIR, PAIR], F32R)
        ctx_T = sb("ctx_T", [D, 2, S])
        k_hi = sb("k_hi", [D, S], F32R)
        k_lo = sb("k_lo", [D, S], F32R)
        ctx_centred = [t[:, :].bitcast(F32) for t in (k_hi, k_lo)]
        ctx_squares = [work[:, 0:S], work[:, 2 * T:2 * T + S]]
        deviation = qk[:, 0:S]
        ctx_out = [norm_work[:, 0:S], norm_work[:, 2 * T:2 * T + S]]
        k_stack = [sb(f"k_stack{i}", [KR, G, S], F32R) for i in range(2)]
        q_split = sb("q_split", [96, G, T], F32R)
        q_max = [sb(f"q_max{i}", [KR, HQ], F32R) for i in range(2)]
        q_score = [sb(f"q_score{i}", [KR, HQ], F32R) for i in range(2)]
        v_ctx = [sb(f"v_ctx{i}", [KC, NCH, G, VG]) for i in range(2)]
        probs = sb("probs", [KC, 3, HQ])
        mask_u8 = sb("mask_u8", [97, S], U8)
        mask_row = sb("mask_row", [97, S], F32R)

        slot = [ctx.enter_context(nc.psum_tensor(f"slot{i}", [D, 2, 512], F32)) for i in range(3)]
        acc_a = ctx.enter_context(nc.psum_tensor("acc_a", [D, 512], F32))
        acc_b = ctx.enter_context(nc.psum_tensor("acc_b", [D, 512], F32))

        psum_full = [sem(f"psum_full{i}") for i in range(3)]
        psum_free = [sem(f"psum_free{i}") for i in range(3)]
        const_loaded, x_loaded, w1_loaded, w2_loaded = sem("const_loaded"), sem("x_loaded"), sem("w1_loaded"), sem("w2_loaded")
        wkv_loaded = sem("wkv_loaded")
        raw_loaded = [sem(f"raw_loaded{i}") for i in range(2)]
        norm_stored = [sem(f"norm_stored{i}") for i in range(2)]
        ctx_loaded = [sem(f"ctx_loaded{i}") for i in range(2)]
        stack_loaded = [[sem(f"stack_loaded{i}_{k}") for k in range(2)] for i in range(2)]
        mask_loaded, mask_row_ready = sem("mask_loaded"), sem("mask_row_ready")
        ctx_squared, ctx_rstd, ctx_normed = sem("ctx_squared"), sem("ctx_rstd"), sem("ctx_normed")
        last_var_ready, last_var_read = sem("last_var_ready"), sem("last_var_read")
        exp_cond, silu_ready = sem("exp_cond"), sem("silu_ready")
        x_squared, rstd_ready, xn_ready, x_ready = sem("x_squared"), sem("rstd_ready"), sem("xn_ready"), sem("x_ready")
        den_ready, heads_ready, qhi_ready = sem("den_ready"), sem("heads_ready"), sem("qhi_ready")
        self_operands, self_probs, self_done = sem("self_operands"), sem("self_probs"), sem("self_done")
        hi_ready, qmax_ready, qscore_ready, self_max = sem("hi_ready"), sem("qmax_ready"), sem("qscore_ready"), sem("self_max")
        max_ready, probs_used, acc_free = sem("max_ready"), sem("probs_used"), sem("acc_free")
        waits_met = sem("waits_met")
        pool_init, rows_init, dve_step, stored = sem("pool_init"), sem("rows_init"), sem("dve_step"), sem("stored")

        block = ctx.enter_context(nc.Block())

        def W(name, a=0, b=None):
            o, w = W1[name]
            return w1[:, o + a:o + (w if b is None else b)]

        def bi(l, name, n=0, rows=slice(0, D), width=1):
            o = l * BI_COLS + BI[name][0] + n
            return bias[rows, o:o + width]

        def co(name, rows=slice(0, D)):
            o, w = CO[name]
            return const[rows, o:o + w]

        def full(e, phase, use, turn=0):
            s, n = uses.at(phase, use, turn)
            e.wait_ge(psum_full[s], n + 1)
            return slot[s]

        def freed(e, phase, use, turn=0):
            s, n = uses.at(phase, use, turn)
            e.wait_ge(psum_free[s], n + 2)

        def claim(pe, phase, use, turn=0):
            s, n = uses.at(phase, use, turn)
            pe.wait_ge(psum_free[s], n + 1)
            return slot[s]

        def wait_alone(e, semaphore, count):
            e.wait_ge(semaphore, count)
            if not isinstance(count, int):
                e.sem_inc(waits_met, 1)

        def slot_free(phase, use):
            return psum_free[uses.at(phase, use)[0]]

        def slot_full(phase, use):
            return psum_full[uses.at(phase, use)[0]]

        def half_of(t, h):
            return t[:, h * HALF:(h + 1) * HALF]

        def halves(t, rows=slice(0, D)):
            return t[rows, :, 0:HALF]

        def two(t):
            return t.rearrange("p (a n) -> p a n", a=2)

        def by_batch(t):
            return t.rearrange("p (b n) -> p b n", n=N)

        def per_token(m, nb=B):
            return m.unsqueeze(2).to_broadcast([D, nb, N])

        def thirds(part):
            if part[0] == "K":
                return int(part[1]), 1
            return (0, 2) if part[1] == "0" else (2, 1)

        def value_chunks(part):
            return (0, 1) if part == "V0" else (4, 2)

        def keys(t, part):
            s0, ns = thirds(part)
            return t[:, s0 * TH:(s0 + ns) * TH].rearrange("p (a n) -> p a n", n=TH)

        def value_columns(v):
            return v[:, :, 0:GH * VS].rearrange("p a (t v) -> p a t v", v=VS)[:, :, :, 0:HD]

        def turns(e, body, last=None):
            with e.Fori(0, (B - 2) // 2, 1) as i:
                body(i * 2, 0, i)
                body(i * 2 + 1, 1, i)
            if last:
                last()

        @block.sync
        def _(sp):
            sp.dma_start(const[:, :], const_d).then_inc(const_loaded, 16)
            sp.dma_start(bias[:, :], bias_d).then_inc(const_loaded, 16)
            sp.dma_start(cond[:, :], cond_d).then_inc(const_loaded, 16)
            for p in range(2):
                sp.dma_start(ctx_T[:, p, :], ctx_d[p]).then_inc(raw_loaded[p], 16)
            sp.dma_start(x[:, :], x_d).then_inc(x_loaded, 16)
            sp.dma_start(w_kv[:, 0, :], wkv_d[0]).then_inc(wkv_loaded, 16)
            sp.dma_start(w1[:, :], w1_d[0]).then_inc(w1_loaded, 16)
            sp.dma_start(w2[:, :], w2_d[0]).then_inc(w2_loaded, 16)

            def store_norm(b, p):
                wait_alone(sp, ctx_normed, b + 2)
                sp.dma_start(ctx_norm_d[bass.ds(b, 1)].rearrange("o d s -> (o d) s"), ctx_out[p])\
                    .then_inc(norm_stored[p], 16)

            def ctx_turn(b, p):
                s, n = uses.at("ctx", "m1", b)
                wait_alone(sp, psum_free[s], n + 2)
                sp.dma_start(ctx_T[:, 1 - p, :], ctx_d[bass.ds(b + 3, 1)].rearrange("o d s -> (o d) s"))\
                    .then_inc(raw_loaded[1 - p], 16)
                store_norm(b, p)

            freed(sp, "ctx_first", "m1")
            sp.dma_start(ctx_T[:, 0, :], ctx_d[2]).then_inc(raw_loaded[0], 16)
            with sp.Fori(0, (B - 4) // 2, 1) as i:
                ctx_turn(i * 2, 0)
                ctx_turn(i * 2 + 1, 1)
            ctx_turn(B - 4, 0)
            for b in range(B - 3, B):
                store_norm(b, b % 2)
            for p in range(2):
                sp.wait_ge(norm_stored[p], 16 * (B // 2 + 1))

            def load_ctx(l, b, p):
                src = ctx_norm_d if l == NORM_CTX else ctx_d
                sp.dma_start(ctx_T[:, p, :], src[bass.ds(b, 1)].rearrange("o d s -> (o d) s"))\
                    .then_inc(ctx_loaded[p], 16)

            def load_mask(b, before):
                if before:
                    wait_alone(sp, mask_row_ready, b)
                sp.dma_start(mask_u8[96:97, :].bitcast(mybir.dt.int32), mask_d[bass.ds(b, 1)]).then_inc(mask_loaded, 16)

            def place(l, b, p, k, phase, turn):
                n = slice(0, 2 * TH) if k == 0 else slice(2 * TH, S)
                for part in (("K0", "K1"), ("K2",))[k]:
                    s, count = uses.at(phase, part, turn)
                    wait_alone(sp, psum_free[s], count + 2)
                for g in range(G):
                    rows = slice(32 * g, 32 * g + 32)
                    for at, half in ((0, k_hi), (32, k_lo), (64, k_hi)):
                        sp.dma_start(k_stack[p][at:at + 32, g, n].bitcast(F32), half[rows, n].bitcast(F32))\
                            .then_inc(stack_loaded[p][k], 16)
                if l == MASKED:
                    if k == 0:
                        sp.wait_ge(mask_row_ready, b + 1)
                    sp.dma_start(k_stack[p][96:97, :, n].bitcast(F32),
                                 mask_row[96:97, n].bitcast(F32).unsqueeze(1).to_broadcast([1, G, n.stop - n.start]))\
                        .then_inc(stack_loaded[p][k], 16)

            for l in range(L):
                if l > 0:
                    freed(sp, f"cross{l - 1}", "V1", B - 3)
                    sp.dma_start(w_kv[:, l % 2, :], wkv_d[l]).then_inc(wkv_loaded, 16)
                for p in range(2):
                    load_ctx(l, p, p)
                for b in range(2):
                    if l == MASKED:
                        load_mask(b, b > 0)
                    for k in range(2):
                        place(l, b, b, k, kv_phase(l, b, "K"), 0)
                    freed(sp, kv_phase(l, b, "V1"), "V1")
                    load_ctx(l, b + 2, b)
                    if l > 0 and b == 0:
                        freed(sp, f"C{l - 1}", "p1")
                        sp.dma_start(w1[:, :], w1_d[l]).then_inc(w1_loaded, 16)
                        sp.wait_ge(x_ready, 4 * l)
                        sp.dma_start(w2[:, :], w2_d[l]).then_inc(w2_loaded, 16)

                def cross_turn(b, p, more, l=l):
                    if l == MASKED:
                        load_mask(b + 2, True)
                    for k in range(2):
                        s, n = uses.at(f"cross{l}", f"C{4 * k + 7}", b)
                        wait_alone(sp, psum_free[s], n + 2)
                        place(l, b + 2, p, k, f"cross{l}", b)
                    if more:
                        s, n = uses.at(f"cross{l}", "V1", b)
                        wait_alone(sp, psum_free[s], n + 2)
                        load_ctx(l, b + 4, p)

                with sp.Fori(0, (B - 4) // 2, 1) as i:
                    cross_turn(i * 2, 0, True)
                    cross_turn(i * 2 + 1, 1, True)
                cross_turn(B - 4, 0, False)
                cross_turn(B - 3, 1, False)
            for h in HALVES:
                sp.wait_ge(x_ready, 4 * L - 1 + h)
                sp.dma_start(half_of(out_d, h), half_of(x, h)).then_inc(stored, 16)
            sp.wait_ge(stored, 32)

        @block.gpsimd
        def _(pool):
            for i in range(2):
                pool.memset(v_ctx[i][:, :, :, :], 0.0).then_inc(pool_init, 1)
            pool.memset(v_self[:, :, :, :], 0.0).then_inc(pool_init, 1)
            pool.wait_ge(pool_init, 3)
            for t in range(GH):
                c = VS * t + HD
                for i in range(2):
                    pool.memset(v_ctx[i][:, :, :, c:c + 1], 1.0).then_inc(pool_init, 1)
                pool.memset(v_self[:, :, :, c:c + 1], 1.0).then_inc(pool_init, 1)
            pool.wait_ge(const_loaded, 48)

            def make_mask_row(l, b, p):
                pool.wait_ge(mask_loaded, b * 16 + 16)
                for k in range(2):
                    wait_alone(pool, stack_loaded[1 - p][k], mask_placed(b, p))
                pool.tensor_scalar(mask_row[96:97, :], mask_u8[96:97, :], -1e38, 1e38, ALU.mult, ALU.mult)\
                    .then_inc(mask_row_ready, 1)
                wait_alone(pool, mask_row_ready, b + 1)

            def mask_placed(b, p):
                per = 16 * stack_dmas(MASKED)
                base = stack_count(MASKED, 0) - per
                return (b * (per // 2) + base) if p == 0 else (b * (per // 2) + (base + per // 2))

            def self_operands_of(b, p):
                at = bass.ds(b * N, N)
                pool.tensor_tensor(out=by_batch(q_blocks[p]), in0=qT[:, at].unsqueeze(1).to_broadcast([D, NH, N]),
                                   in1=co("head16").unsqueeze(2).to_broadcast([D, NH, N]), op=ALU.mult)\
                    .then_inc(self_operands, 1)
                pool.tensor_copy(k_batch[:, p, :], kT[:, at]).then_inc(self_operands, 1)
                pool.tensor_copy(x_batch[:, p, :], xn[:, at]).then_inc(self_operands, 1)

            def expand(dst, b):
                for g in range(G):
                    last = pool.tensor_tensor(
                        out=by_batch(dst[0:96, g * GQ:(g + 1) * GQ]),
                        in0=q_split[:, g, bass.ds(b * N, N)].bitcast(F32).unsqueeze(1).to_broadcast([96, GH, N]),
                        in1=co("head4", slice(0, 96)).unsqueeze(2).to_broadcast([96, GH, N]), op=ALU.mult)
                return last

            for l in range(L):
                if l == MASKED:
                    for b in range(2):
                        make_mask_row(l, b, b)
                freed(pool, f"A{l}", "k0")
                self_operands_of(0, 0)
                self_operands_of(1, 1)
                freed(pool, f"A{l}", "k1")

                def self_turn(b, p, i, l=l):
                    s, n = uses.at(f"self{l}", "T", b)
                    wait_alone(pool, psum_full[s], n + 1)
                    self_operands_of(b + 2, p)

                turns(pool, self_turn)

                freed(pool, f"B{l}", "c30")
                expand(q_max[0], 0).then_inc(qmax_ready, 1)
                expand(q_score[0], 0).then_inc(qscore_ready, 1)
                expand(q_max[1], 1).then_inc(qmax_ready, 1)
                freed(pool, f"B{l}", "c31")

                def next_scores(b, p, l=l):
                    wait_alone(pool, probs_used, b * NCH + (NCH * B * l + 3))
                    expand(q_score[1 - p], b + 1).then_inc(qscore_ready, 1)

                def cross_turn(b, p, i, l=l):
                    next_scores(b, p)
                    wait_alone(pool, max_ready, b + (B * l + 1))
                    expand(q_max[p], b + 2).then_inc(qmax_ready, 1)
                    if l == MASKED:
                        make_mask_row(l, b + 2, p)

                turns(pool, cross_turn, lambda: next_scores(B - 2, 0))

        @block.scalar
        def _(act):
            act.wait_ge(const_loaded, 48)
            eps = co("eps")
            act.preload_act_table_set("natural_log_exp_and_others")
            act.activation(silu[:, :], cond[:, :], ACT.Exp, scale=-1.0).then_inc(exp_cond, 1)

            def ctx_square(p):
                act.activation(ctx_squares[p], ctx_centred[p], ACT.Square).then_inc(ctx_squared, 1)

            def ctx_log(phase, turn, b):
                t = full(act, phase, "v0", turn)
                act.activation(keys(deviation, "v0"), t[:, 0:2, 0:TH], ACT.Ln, bias=eps).then_inc(slot_free(phase, "v0"), 1)
                act.wait_ge(last_var_ready, b + 1)
                act.activation(deviation[:, 2 * TH:S], acc_a[:, 0:TH], ACT.Ln, bias=eps).then_inc(last_var_read, 1)

            def ctx_power(phase, turn, b):
                freed(act, phase, "v0", turn)
                act.wait_ge(last_var_read, b + 2)
                act.activation(deviation, deviation, ACT.Exp, scale=-0.5).then_inc(ctx_rstd, 1)

            def ctx_turn(b, p, i):
                act.wait_ge(ctx_normed, b + 1)
                ctx_log("ctx", b, b)
                ctx_power("ctx", b, b)
                freed(act, "ctx", "m1", b)
                ctx_square(1 - p)

            def ctx_end():
                ctx_turn(B - 2, 0, 7)
                act.wait_ge(ctx_normed, B)
                ctx_log("ctx_last", 0, B - 1)
                ctx_power("ctx_last", 0, B - 1)

            freed(act, "ctx_first", "m1")
            ctx_square(0)
            turns(act, ctx_turn, ctx_end)

            def norm(phase, k):
                for h in HALVES:
                    freed(act, phase, f"mean{h}")
                    act.activation(half_of(sq, h), half_of(xc, h), ACT.Square).then_inc(x_squared, 1)
                for h in HALVES:
                    t = full(act, phase, f"var{h}")
                    act.activation(half_of(rstd, h), t[:, 0, 0:HALF], ACT.Ln, bias=eps).then_inc(slot_free(phase, f"var{h}"), 1)
                    freed(act, phase, f"var{h}")
                    act.activation(half_of(rstd, h), half_of(rstd, h), ACT.Exp, scale=-0.5).then_inc(rstd_ready, 1)

            def reciprocals(phase):
                for h in HALVES:
                    for use, den in (("dA", rstd), ("dB", sq)):
                        t = full(act, phase, f"{use}{h}")
                        act.activation(half_of(den, h), t[:, 0, 0:HALF], ACT.Ln).then_inc(slot_free(phase, f"{use}{h}"), 1)
                    for use, den in (("dA", rstd), ("dB", sq)):
                        freed(act, phase, f"{use}{h}")
                        act.activation(half_of(den, h), half_of(den, h), ACT.Exp, scale=-1.0).then_inc(den_ready, 1)

            def keys_high(phase, turn, l, b, p, part):
                t = full(act, phase, part, turn)
                s0, ns = thirds(part)
                if b is not None and part != "K1":
                    act.wait_ge(stack_loaded[1 - p][s0 // 2], b)
                act.activation(keys(k_hi, part), t[:, 0:ns, 0:TH], ACT.Identity, bias=bi(l, "kc")).then_inc(hi_ready, 1)

            def values(phase, turn, p, part):
                t = full(act, phase, part, turn)
                c0, banks = value_chunks(part)
                act.activation(value_columns(v_ctx[p][:, c0:c0 + 4 * banks, :, :].rearrange("p c g v -> p (c g) v")),
                               t[0:KC, 0:banks, :].rearrange("p k (a t d) -> p (k a) t d", t=GH, d=HD), ACT.Copy)\
                    .then_inc(slot_free(phase, part), 1)

            def exps(phase, turn, c, n):
                t = full(act, phase, f"C{c}", turn)
                act.wait_ge(probs_used, n + 1)
                act.activation(two(probs[:, c % 3, :]), t[0:KC, :, 0:HALF], ACT.Exp, scale=SCALE)\
                    .then_inc(slot_free(phase, f"C{c}"), 1)

            def first_keys(l, b):
                for part in KV_USES[0:3]:
                    before = None if l == 0 and b == 0 else stack_count(l, 0) if b else stack_count(l - 1, 7)
                    keys_high(kv_phase(l, b, part), 0, l, before, b, part)

            def first_values(l, b):
                for part in KV_USES[3:]:
                    values(kv_phase(l, b, part), 0, b, part)

            act.wait_ge(pool_init, 3 + 3 * GH)
            for l in range(L):
                if l == 0:
                    first_keys(0, 0)
                    first_values(0, 0)
                norm(f"A{l}", 3 * l)
                for h in HALVES:
                    for part, dst in (("q", qT), ("k", kT)):
                        t = full(act, f"A{l}", f"{part}{h}")
                        act.activation(half_of(dst, h), t[:, 0, 0:HALF], ACT.Identity, bias=bi(l, part))\
                            .then_inc(slot_free(f"A{l}", f"{part}{h}"), 1)
                first_keys(l, 1)

                def self_copy(b, p, l=l):
                    t = full(act, f"self{l}", "S", b)
                    act.activation(two(self_raw[p]), halves(t, slice(0, N)), ACT.Copy).then_inc(slot_free(f"self{l}", "S"), 1)

                def self_exp(b, p, l=l):
                    freed(act, f"self{l}", "H", b)
                    act.activation(probs_T[p], probs_T[p], ACT.Exp, scale=SCALE).then_inc(self_probs, 1)

                def self_turn(b, p, i, l=l):
                    self_copy(b + 2, p)
                    self_exp(b + 1, 1 - p)

                for b in range(2):
                    self_copy(b, b)
                self_exp(0, 0)
                turns(act, self_turn)
                self_exp(B - 1, 1)
                reciprocals(f"B{l}")
                norm(f"B{l}", 3 * l + 1)
                for h in HALVES:
                    for g in range(G):
                        t = full(act, f"B{l}", f"c{g}{h}")
                        act.activation(half_of(q_split[:, g, :], h), t[0:96, 0, 0:HALF], ACT.Identity,
                                       bias=bi(l, "qr", g, slice(0, 96))).then_inc(qhi_ready, 1)

                first_values(l, 1)

                def cross_turn(phase, turn, b, p, kv, l=l):
                    for use in cross_uses(kv is not None, kv is not None):
                        if use[0] == "C":
                            c = int(use[1:])
                            exps(phase, turn, c, b * NCH + (NCH * B * l + c))
                        elif use[0] == "K":
                            keys_high(phase, turn, l, kv, p, use)
                        elif use[0] == "V":
                            c0, banks = value_chunks(use)
                            act.wait_ge(probs_used, b * NCH + (NCH * B * l + c0 + 4 * banks + 3))
                            values(phase, turn, p, use)

                def turn(b, p, i, l=l):
                    cross_turn(f"cross{l}", b, b, p, i * (16 * stack_dmas(l)) + (stack_count(l, 0) + (16 * stack_dmas(l) if p else 0)))

                def end(l=l):
                    cross_turn(f"cross14_{l}", 0, B - 2, 0, None)
                    cross_turn(f"cross15_{l}", 0, B - 1, 1, None)

                turns(act, turn, end)
                if l < L - 1:
                    first_keys(l + 1, 0)
                reciprocals(f"C{l}")
                if l < L - 1:
                    first_values(l + 1, 0)
                norm(f"C{l}", 3 * l + 2)
                for h in HALVES:
                    for j in range(4):
                        t = full(act, f"C{l}", f"h{j}{h}")
                        act.activation(half_of(hidden[j], h), t[:, 0, 0:HALF],
                                       ACT.Gelu if l == EXACT_GELU else ACT.Gelu_apprx_tanh,
                                       bias=bi(l, "f1", j)).then_inc(slot_free(f"C{l}", f"h{j}{h}"), 1)
                if l < L - 1:
                    act.preload_act_table_set("natural_log_exp_and_others")

        @block.vector
        def _(dve):
            steps = [0]

            def step(ins):
                steps[0] += 1
                ins.then_inc(dve_step, 1)
                dve.wait_ge(dve_step, steps[0])

            dve.wait_ge(const_loaded, 48)
            rows = slice(96, KR)
            k_rows, q_rows, shift_rows = (const[rows, CO["rows"][0] + j:CO["rows"][0] + j + 1] for j in range(3))

            def fill_key_rows():
                for i in range(2):
                    dve.tensor_copy(k_stack[i][rows, :, :].rearrange("p g n -> p (g n)"), k_rows.to_broadcast([2, G * S]))\
                        .then_inc(rows_init, 1)

            fill_key_rows()
            for i in range(2):
                dve.tensor_copy(q_max[i][rows, :], q_rows.to_broadcast([2, HQ])).then_inc(rows_init, 1)

            dve.tensor_copy(ident_r[:, :], co("ident", slice(0, PAIR))[:, 0:PAIR]).then_inc(rows_init, 1)
            dve.wait_ge(pool_init, 3 + 3 * GH)

            dve.wait_ge(exp_cond, 1)
            step(dve.tensor_scalar(silu[:, :], silu[:, :], 1.0, None, ALU.add))
            step(dve.reciprocal(silu[:, :], silu[:, :]))
            dve.tensor_tensor(out=silu[:, :], in0=silu[:, :], in1=cond[:, :], op=ALU.mult).then_inc(silu_ready, 1)

            def ctx_centre(phase, turn, p):
                for part in ("m0", "m1"):
                    t = full(dve, phase, part, turn)
                    dve.tensor_tensor(out=keys(ctx_centred[p], part), in0=keys(ctx_T[:, p, :], part),
                                      in1=t[:, 0:thirds(part)[1], 0:TH], op=ALU.subtract)\
                        .then_inc(slot_free(phase, part), 1)

            def ctx_divide(b, p, half):
                dve.wait_ge(norm_stored[p], half * 16 + 16)
                dve.wait_ge(ctx_rstd, b + 1)
                dve.tensor_tensor(out=ctx_out[p], in0=ctx_centred[p], in1=deviation, op=ALU.mult)\
                    .then_inc(ctx_normed, 1)

            def ctx_turn(b, p, i):
                dve.wait_ge(ctx_normed, b + 1)
                ctx_centre("ctx", b, 1 - p)
                ctx_divide(b, p, i)

            def ctx_end():
                ctx_turn(B - 2, 0, 7)
                ctx_divide(B - 1, 1, 7)

            ctx_centre("ctx_first", 0, 0)
            turns(dve, ctx_turn, ctx_end)

            def centre(phase):
                for h in HALVES:
                    t = full(dve, phase, f"mean{h}")
                    dve.tensor_tensor(out=half_of(xc, h), in0=half_of(x, h), in1=t[:, 0, 0:HALF], op=ALU.subtract)\
                        .then_inc(slot_free(phase, f"mean{h}"), 1)

            def divide(l, k, which):
                for h in HALVES:
                    at, of = half_of(xn, h), slice(8 * h, 8 * h + 8)
                    dve.wait_ge(rstd_ready, 2 * k + h + 1)
                    ins = dve.tensor_tensor(out=at, in0=half_of(xc, h), in1=half_of(rstd, h), op=ALU.mult)
                    if which in (0, 2):
                        step(ins)
                        scale, shift = (mod[:, 1, of], mod[:, 0, of]) if which == 0 else (mod[:, 4, of], mod[:, 3, of])
                        step(dve.tensor_tensor(out=by_batch(at), in0=by_batch(at), in1=per_token(scale, 8), op=ALU.mult))
                        ins = dve.tensor_tensor(out=by_batch(at), in0=by_batch(at), in1=per_token(shift, 8), op=ALU.add)
                    elif l == AFFINE:
                        step(ins)
                        ins = dve.tensor_scalar(at, at, bi(l, "g2"), bi(l, "b2"), ALU.mult, ALU.add)
                    ins.then_inc(xn_ready, 1)

            def gated(phase, use, b_ap, gate):
                for h in HALVES:
                    t = full(dve, phase, f"{use}{h}")
                    dve.scalar_tensor_tensor(out=by_batch(half_of(xn, h)), in0=by_batch(t[:, 0, 0:HALF]), scalar=b_ap,
                                             in1=per_token(gate[:, 8 * h:8 * h + 8], 8), op0=ALU.add, op1=ALU.mult)\
                        .then_inc(slot_free(phase, f"{use}{h}"), 1)
                    freed(dve, phase, f"{use}{h}")
                    dve.tensor_tensor(out=half_of(x, h), in0=half_of(x, h), in1=half_of(xn, h), op=ALU.add).then_inc(x_ready, 1)

            def normalise_heads(count):
                for h in HALVES:
                    for n, (den, heads, dst) in enumerate(((rstd, heads_a, qT), (sq, heads_b, kT))):
                        dve.wait_ge(den_ready, count + 2 * h + n + 1)
                        dve.tensor_tensor(out=half_of(dst, h), in0=half_of(heads, h), in1=half_of(den, h), op=ALU.mult)\
                            .then_inc(heads_ready, 1)

            masks3 = co("third").unsqueeze(2).to_broadcast([D, 3, N])

            def extract(b, count):
                dve.tensor_tensor(out=masked[:, :, :], in0=acc_a[:, 0:RA].rearrange("p (t n) -> p t n", n=N), in1=masks3,
                                  op=ALU.mult).then_inc(acc_free, 1)
                dve.wait_ge(acc_free, count)
                at = bass.ds(b * N, N)
                dve.tensor_reduce(out=heads_a[:, at], in_=masked[:, :, :].rearrange("p t n -> p n t"), axis=AX.X, op=ALU.add)\
                    .then_inc(acc_free, 1)
                dve.tensor_copy(heads_b[:, at], acc_b[:, 0:N]).then_inc(acc_free, 1)

            def reduce_tile(phase, turn, c):
                t = full(dve, phase, f"M{c}", turn)
                pair = 2 * (c % 4)
                dve.reduce_max(part_max[:, c // 4, pair:pair + 2], t[0:PAIR, :, 0:TH], AX.X)\
                    .then_inc(slot_free(phase, f"M{c}"), 1)

            def negate_maxima(phase, turn):
                freed(dve, phase, f"M{NCH - 1}", turn)
                dve.tensor_reduce(out=neg_max[:, :], in_=part_max[:, :, :].rearrange("q s p -> q p s"), axis=AX.X, op=ALU.max,
                                  negate=True).then_inc(max_ready, 1)

            def shift(phase, turn, p):
                t = full(dve, phase, "R", turn)
                dve.tensor_scalar(two(q_score[p][rows, :]), t[rows, :, 0:HALF], shift_rows, q_rows, ALU.mult, ALU.add)\
                    .then_inc(slot_free(phase, "R"), 1)

            def keys_low(phase, turn, l, part, count):
                dve.wait_ge(hi_ready, count)
                s0, ns = thirds(part)
                s, _ = uses.at(phase, part)
                dve.scalar_tensor_tensor(out=keys(k_lo, part), in0=slot[s][:, 0:ns, 0:TH], scalar=bi(l, "kc"),
                                         in1=keys(k_hi[:, :].bitcast(F32), part), op0=ALU.add, op1=ALU.subtract)\
                    .then_inc(slot_free(phase, part), 1)

            def first_keys_low(l, b):
                for n, part in enumerate(KV_USES[0:3]):
                    keys_low(kv_phase(l, b, part), 0, l, part, 3 * (B * l + b) + n + 1)

            for l in range(L):
                if l == 0:
                    first_keys_low(0, 0)
                centre(f"A{l}")
                t = full(dve, f"A{l}", "mod")
                step(dve.tensor_tensor(out=mod[:, :, :], in0=t[:, 0, 0:6 * B].rearrange("p (k b) -> p k b", b=B),
                                       in1=bi(l, "mod", width=6).unsqueeze(2).to_broadcast([D, 6, B]), op=ALU.add))
                for k in (1, 4):
                    step(dve.tensor_scalar(mod[:, k, :], mod[:, k, :], 1.0, None, ALU.add))
                dve.tensor_tensor(out=proj_bias[:, :], in0=t[:, 0, 6 * B:6 * B + 2], in1=bi(l, "p", width=2), op=ALU.add)\
                    .then_inc(slot_free(f"A{l}", "mod"), 1)
                divide(l, 3 * l, 0)
                first_keys_low(l, 1)

                def self_maxima(b, p, l=l):
                    t = full(dve, f"self{l}", "T", b)
                    dve.tensor_reduce(out=neg_max_self[:, :], in_=by_batch(t[0:PAIR, 0, 0:NP * N]), axis=AX.X, op=ALU.max,
                                      negate=True).then_inc(self_max, 1)
                    dve.tensor_copy(value_columns(v_self[:, p, :, :]),
                                    t[0:N, 1, 0:D].rearrange("p (a t d) -> p a t d", t=GH, d=HD))\
                        .then_inc(slot_free(f"self{l}", "T"), 1)

                def self_shift(b, p, l=l):
                    t = full(dve, f"self{l}", "H", b)
                    dve.tensor_tensor(out=two(probs_T[p]), in0=two(self_raw[p]), in1=halves(t, slice(0, N)), op=ALU.add)\
                        .then_inc(slot_free(f"self{l}", "H"), 1)

                def self_extract(b, l=l):
                    dve.wait_ge(self_done, b + (B * l + 2))
                    extract(b, b * 3 + (3 * 2 * B * l + 4))

                def self_turn(b, p, i, l=l):
                    self_shift(b + 1, 1 - p)
                    self_extract(b)
                    self_maxima(b + 2, p)

                self_maxima(0, 0)
                self_shift(0, 0)
                self_maxima(1, 1)
                turns(dve, self_turn)
                self_shift(B - 1, 1)
                for b in range(B - 2, B):
                    self_extract(b)
                normalise_heads(8 * l)
                gated(f"B{l}", "p", proj_bias[:, 0:1], mod[:, 2, :])
                centre(f"B{l}")
                divide(l, 3 * l + 1, 1)
                for h in HALVES:
                    for g in range(G):
                        t = full(dve, f"B{l}", f"c{g}{h}")
                        dve.wait_ge(qhi_ready, 2 * G * l + G * h + g + 1)
                        dve.scalar_tensor_tensor(out=half_of(q_split[64:96, g, :], h), in0=t[64:96, 0, 0:HALF],
                                                 scalar=bi(l, "qr", g, slice(64, 96)),
                                                 in1=half_of(q_split[64:96, g, :].bitcast(F32), h), op0=ALU.add,
                                                 op1=ALU.subtract).then_inc(slot_free(f"B{l}", f"c{g}{h}"), 1)
                for c in range(NCH):
                    reduce_tile(f"max0_{l}", 0, c)
                negate_maxima(f"max0_{l}", 0)
                shift(f"max0_{l}", 0, 0)

                def cross_turn(phase, turn, b, p, with_max, hi, l=l):
                    for use in cross_uses(with_max, hi is not None):
                        if use[0] == "M":
                            reduce_tile(phase, turn, int(use[1:]))
                            if use == f"M{NCH - 1}":
                                negate_maxima(phase, turn)
                        elif use[0] == "K":
                            keys_low(phase, turn, l, use, hi + int(use[1]))
                        elif use == "R":
                            shift(phase, turn, 1 - p)
                    dve.wait_ge(probs_used, b * NCH + (NCH * (B * l + 1) + 3))
                    extract(b, b * 3 + (3 * (2 * B * l + B) + 4))

                def turn(b, p, i, l=l):
                    cross_turn(f"cross{l}", b, b, p, True, b * 3 + (3 * (B * l + 2) + 1))

                def end(l=l):
                    cross_turn(f"cross14_{l}", 0, B - 2, 0, True, None)
                    cross_turn(f"cross15_{l}", 0, B - 1, 1, False, None)

                turns(dve, turn, end)
                if l == MASKED:
                    fill_key_rows()
                if l < L - 1:
                    first_keys_low(l + 1, 0)
                normalise_heads(8 * l + 4)
                for h in HALVES:
                    t = full(dve, f"C{l}", f"p{h}")
                    dve.scalar_tensor_tensor(out=half_of(x, h), in0=t[:, 0, 0:HALF], scalar=proj_bias[:, 1:2], in1=half_of(x, h),
                                             op0=ALU.add, op1=ALU.add).then_inc(slot_free(f"C{l}", f"p{h}"), 1)
                centre(f"C{l}")
                divide(l, 3 * l + 2, 2)
                gated(f"C{l}", "y", bi(l, "f2"), mod[:, 5, :])

        @block.tensor
        def _(pe):
            for i in range(3):
                pe.sem_inc(psum_free[i], 1)
            pe.sem_inc(probs_used, 3)
            pe.sem_inc(acc_free, 3)
            pe.sem_inc(self_done, 1)
            pe.sem_inc(ctx_normed, 1)
            pe.sem_inc(last_var_read, 1)
            for p in range(2):
                pe.sem_inc(norm_stored[p], 16)
            pe.wait_ge(const_loaded, 48)

            def ctx_sum(phase, turn, parts, src):
                for part in parts:
                    t = claim(pe, phase, part, turn)
                    s0, ns = thirds(part)
                    for a in range(ns):
                        mm = pe.matmul(t[:, a, 0:TH], co("mean"), src[:, (s0 + a) * TH:(s0 + a + 1) * TH], start=True, stop=True)
                    mm.then_inc(slot_full(phase, part), 1)

            def last_variances(b, p):
                pe.wait_ge(last_var_read, b + 1)
                pe.matmul(acc_a[:, 0:TH], co("mean"), ctx_squares[p][:, 2 * TH:S], start=True, stop=True)\
                    .then_inc(last_var_ready, 1)

            def ctx_turn(b, p, i):
                pe.wait_ge(raw_loaded[1 - p], i * 16 + 16 * (1 + p))
                ctx_sum("ctx", b, ("m0", "m1"), ctx_T[:, 1 - p, :])
                pe.wait_ge(ctx_squared, b + 1)
                ctx_sum("ctx", b, ("v0",), ctx_squares[p])
                last_variances(b, p)

            def ctx_end():
                ctx_turn(B - 2, 0, 7)
                pe.wait_ge(ctx_squared, B)
                ctx_sum("ctx_last", 0, ("v0",), ctx_squares[1])
                last_variances(B - 1, 1)

            pe.wait_ge(raw_loaded[0], 16)
            ctx_sum("ctx_first", 0, ("m0", "m1"), ctx_T[:, 0, :])
            turns(pe, ctx_turn, ctx_end)

            def dense(phase, use, h, terms, rows=D):
                t = claim(pe, phase, f"{use}{h}")
                for n, (lhsT, rhs) in enumerate(terms):
                    mm = pe.matmul(t[0:rows, 0, 0:HALF], lhsT, half_of(rhs, h), start=(n == 0), stop=(n == len(terms) - 1))
                mm.then_inc(slot_full(phase, f"{use}{h}"), 1)

            def means(phase, k, x_done):
                for h in HALVES:
                    x_done(h)
                    dense(phase, "mean", h, [(co("mean"), x)])

            def variances(phase, k):
                for h in HALVES:
                    pe.wait_ge(x_squared, 2 * k + h + 1)
                    dense(phase, "var", h, [(co("mean"), sq)])

            def x_updated(before):
                return lambda h: pe.wait_ge(x_ready, before + h + 1)

            def keys_product(phase, turn, l, p, part):
                t = claim(pe, phase, part, turn)
                s0, ns = thirds(part)
                for a in range(ns):
                    mm = pe.matmul(t[:, a, 0:TH], w_kv[:, l % 2, 0:D], ctx_T[:, p, (s0 + a) * TH:(s0 + a + 1) * TH], start=True, stop=True)
                mm.then_inc(slot_full(phase, part), 1)

            def values_product(phase, turn, l, p, part):
                t = claim(pe, phase, part, turn)
                c0, banks = value_chunks(part)
                for c in range(4 * banks):
                    at = (c0 + c) * KC
                    mm = pe.matmul(t[0:KC, c // 4, c % 4 * D:(c % 4 + 1) * D], ctx_T[:, p, at:at + KC], w_kv[:, l % 2, D:2 * D],
                                   start=True, stop=True)
                mm.then_inc(slot_full(phase, part), 1)

            def weigh(v, pr, first, last):
                for lo, acc, r0, rn in ((0, acc_a, 0, RA), (33, acc_b, RA, N)):
                    for g in range(G):
                        mm = pe.matmul(acc[32 * g:32 * g + 32, 0:rn], v[:, g, lo:lo + 32], pr[:, GQ * g + r0:GQ * g + r0 + rn],
                                       start=first, stop=last)
                return mm

            def first_keys(l, b):
                pe.wait_ge(wkv_loaded, 16 * (l + 1))
                pe.wait_ge(ctx_loaded[b], 16 * (B // 2) * l + 16)
                for part in KV_USES[0:3]:
                    keys_product(kv_phase(l, b, part), 0, l, b, part)

            def first_values(l, b):
                for part in KV_USES[3:]:
                    values_product(kv_phase(l, b, part), 0, l, b, part)

            first_keys(0, 0)
            first_values(0, 0)
            for l in range(L):
                means(f"A{l}", 3 * l, x_updated(4 * l - 2) if l else lambda h: pe.wait_ge(x_loaded, 16))
                pe.wait_ge(w1_loaded, 16 * (l + 1))
                if l == 0:
                    pe.wait_ge(silu_ready, 1)
                t = claim(pe, f"A{l}", "mod")
                for k in range(6):
                    pe.matmul(t[:, 0, k * B:(k + 1) * B], W("mod", k * D, (k + 1) * D), silu[:, :], start=True, stop=True)
                for n, w in enumerate(("p", "cp")):
                    v = ("vA", "vB") if n == 0 else ("cvA", "cvB")
                    pe.matmul(t[:, 0, 6 * B + n:6 * B + n + 1], W(w + "A"), bi(l, v[0]), start=True, stop=False)
                    mm = pe.matmul(t[:, 0, 6 * B + n:6 * B + n + 1], W(w + "B"), bi(l, v[1]), start=False, stop=True)
                mm.then_inc(slot_full(f"A{l}", "mod"), 1)
                variances(f"A{l}", 3 * l)
                for h in HALVES:
                    pe.wait_ge(xn_ready, 6 * l + h + 1)
                    dense(f"A{l}", "q", h, [(W("q"), xn)])
                    dense(f"A{l}", "k", h, [(W("k"), xn)])
                first_keys(l, 1)

                def self_scores(b, p, l=l):
                    pe.wait_ge(self_operands, b * 3 + (3 * B * l + 3))
                    s, n = uses.at(f"self{l}", "S", b)
                    wait_alone(pe, psum_free[s], n + 1)
                    for a in range(2):
                        mm = pe.matmul(slot[s][0:N, a, 0:HALF], k_batch[:, p, :], half_of(q_blocks[p], a), start=True, stop=True)
                    mm.then_inc(psum_full[s], 1)

                def self_transpose(b, p, l=l):
                    s, n = uses.at(f"self{l}", "T", b)
                    pe.wait_ge(psum_free[s], n + 1)
                    raw, n = uses.at(f"self{l}", "S", b)
                    wait_alone(pe, psum_free[raw], n + 2)
                    for n in range(NP):
                        pe.transpose(slot[s][0:PAIR, 0, n * N:(n + 1) * N], self_raw[p][:, n * PAIR:(n + 1) * PAIR],
                                     co("ident", slice(0, N))[:, 0:N])
                    pe.matmul(slot[s][0:N, 1, 0:D], x_batch[:, p, :], W("v"), start=True, stop=True).then_inc(psum_full[s], 1)

                def self_max_rows(b, l=l):
                    s, n = uses.at(f"self{l}", "H", b)
                    pe.wait_ge(psum_free[s], n + 1)
                    wait_alone(pe, self_max, b + (B * l + 1))
                    for n in range(NP):
                        c = n % 4 * PAIR
                        mm = pe.matmul(slot[s][0:N, n // 4, c:c + PAIR], neg_max_self[:, n:n + 1].to_broadcast([PAIR, N]),
                                       ident_r[:, :], start=True, stop=True)
                    mm.then_inc(psum_full[s], 1)

                def self_weigh(b, p, l=l):
                    freed(pe, f"self{l}", "T", b)
                    pe.wait_ge(self_probs, b + (B * l + 1))
                    wait_alone(pe, acc_free, b * 3 + (3 * 2 * B * l + 3))
                    weigh(v_self[:, p, :, :], probs_T[p], True, True).then_inc(self_done, 1)

                def self_turn(b, p, i, l=l):
                    self_scores(b + 2, p)
                    self_max_rows(b + 1)
                    self_weigh(b, p)
                    self_transpose(b + 2, p)

                self_scores(0, 0)
                self_transpose(0, 0)
                self_scores(1, 1)
                self_max_rows(0)
                self_transpose(1, 1)
                turns(pe, self_turn)
                self_max_rows(B - 1)
                self_weigh(B - 2, 0)
                self_weigh(B - 1, 1)

                def denominators(phase, layer_half, l=l):
                    pe.wait_ge(acc_free, 3 * (2 * B * l + B * (1 + layer_half)) + 3)
                    for h in HALVES:
                        dense(phase, "dA", h, [(co("selA"), heads_a)])
                        dense(phase, "dB", h, [(co("selB"), heads_b)])

                def project(phase, layer_half, wa, wb, l=l):
                    for h in HALVES:
                        pe.wait_ge(heads_ready, 8 * l + 4 * layer_half + 2 * h + 2)
                        dense(phase, "p", h, [(wa, qT), (wb, kT)])

                denominators(f"B{l}", 0)
                project(f"B{l}", 0, W("pA"), W("pB"))
                means(f"B{l}", 3 * l + 1, x_updated(4 * l))
                variances(f"B{l}", 3 * l + 1)
                for h in HALVES:
                    pe.wait_ge(xn_ready, 2 * (3 * l + 1) + h + 1)
                    for g in range(G):
                        dense(f"B{l}", f"c{g}", h, [(W("qr", 96 * g, 96 * g + 96), xn)], 96)

                def max_tile(phase, turn, p, c):
                    t = claim(pe, phase, f"M{c}", turn)
                    k = c // 4
                    for a in range(2):
                        n = 2 * (c % 4) + a
                        mm = pe.matmul(t[0:PAIR, a, 0:TH], q_max[p][0:KR - 1, n * PAIR:(n + 1) * PAIR],
                                       k_stack[p][0:KR - 1, n // 2, k * TH:(k + 1) * TH], start=True, stop=True)
                    mm.then_inc(slot_full(phase, f"M{c}"), 1)

                def max_rows(phase, turn, count):
                    t = claim(pe, phase, "R", turn)
                    pe.wait_ge(max_ready, count)
                    for n in range(NP):
                        c = (n % 4) * PAIR
                        mm = pe.matmul(t[96:KR, n // 4, c:c + PAIR], neg_max[:, n:n + 1].to_broadcast([PAIR, 2]),
                                       co("ident", slice(0, PAIR))[:, 0:PAIR], start=True, stop=True)
                    mm.then_inc(slot_full(phase, "R"), 1)

                def score_chunk(phase, turn, p, c):
                    t = claim(pe, phase, f"C{c}", turn)
                    for g in range(G):
                        mm = pe.matmul(t[0:KC, g // 2, (g % 2) * GQ:(g % 2 + 1) * GQ], k_stack[p][:, g, c * KC:(c + 1) * KC],
                                       q_score[p][:, g * GQ:(g + 1) * GQ], start=True, stop=True)
                    mm.then_inc(slot_full(phase, f"C{c}"), 1)

                def weigh_chunk(phase, turn, p, c):
                    freed(pe, phase, f"C{c}", turn)
                    weigh(v_ctx[p][:, c, :, :], probs[:, c % 3, :], c == 0, c == NCH - 1).then_inc(probs_used, 1)

                def last_chunks(phase, turn, p):
                    for c in range(NCH - LAG, NCH):
                        weigh_chunk(phase, turn, p, c)

                def cross_turn(phase, turn, b, p, stack, ctx_count, l=l):
                    pe.wait_ge(qscore_ready, b + (B * l + 1))
                    for use in cross_uses(stack is not None, ctx_count is not None):
                        n = int(use[1:] or 0)
                        if use[0] == "M":
                            if n == 0:
                                pe.wait_ge(qmax_ready, b + (B * l + 2))
                            if n in (0, 8):
                                pe.wait_ge(stack_loaded[1 - p][n // 8], stack)
                            max_tile(phase, turn, 1 - p, n)
                        elif use[0] == "C":
                            score_chunk(phase, turn, p, n)
                            if n == LAG:
                                pe.wait_ge(acc_free, b * 3 + (3 * (2 * B * l + B) + 3))
                            if n >= LAG:
                                weigh_chunk(phase, turn, p, n - LAG)
                        elif use[0] == "K":
                            if n == 0:
                                pe.wait_ge(ctx_loaded[p], ctx_count)
                            keys_product(phase, turn, l, p, use)
                        elif use[0] == "V":
                            if n == 1:
                                last_chunks(phase, turn, p)
                            values_product(phase, turn, l, p, use)
                        elif use == "R":
                            max_rows(phase, turn, b + (B * l + 2))
                    if ctx_count is None:
                        last_chunks(phase, turn, p)

                pe.wait_ge(qmax_ready, B * l + 1)
                if l == 0:
                    pe.wait_ge(rows_init, 5)
                elif l == MASKED + 1:
                    pe.wait_ge(rows_init, 7)
                for use in FIRST_MAX:
                    if use in ("M0", "M8"):
                        pe.wait_ge(stack_loaded[0][use == "M8"], stack_count(l, 0))
                    if use[0] == "M":
                        max_tile(f"max0_{l}", 0, 0, int(use[1:]))
                    elif use[0] == "V":
                        values_product(f"max0_{l}", 0, l, 1, use)
                    else:
                        max_rows(f"max0_{l}", 0, B * l + 1)

                def turn(b, p, i, l=l):
                    per = 16 * stack_dmas(l)
                    cross_turn(f"cross{l}", b, b, p, i * per + (stack_count(l, 0) + (per if p else 0)),
                               i * 16 + (16 * (B // 2) * l + 32))

                def end(l=l):
                    cross_turn(f"cross14_{l}", 0, B - 2, 0, stack_count(l, 7), None)
                    cross_turn(f"cross15_{l}", 0, B - 1, 1, None, None)

                turns(pe, turn, end)

                if l < L - 1:
                    first_keys(l + 1, 0)
                denominators(f"C{l}", 1)
                if l < L - 1:
                    first_values(l + 1, 0)
                project(f"C{l}", 1, W("cpA"), W("cpB"))
                means(f"C{l}", 3 * l + 2, lambda h: freed(pe, f"C{l}", f"p{h}"))
                variances(f"C{l}", 3 * l + 2)
                pe.wait_ge(w2_loaded, 16 * (l + 1))
                for h in HALVES:
                    pe.wait_ge(xn_ready, 2 * (3 * l + 2) + h + 1)
                    for j in range(4):
                        dense(f"C{l}", f"h{j}", h, [(w2[:, j * D:(j + 1) * D], xn)])
                for h in HALVES:
                    for j in range(4):
                        freed(pe, f"C{l}", f"h{j}{h}")
                    dense(f"C{l}", "y", h, [(w2[:, (4 + j) * D:(5 + j) * D], hidden[j]) for j in range(4)])


def constants():
    c = np.zeros((D, CO_COLS), np.float32)

    def put(name, a):
        o, w = CO[name]
        c[:, o:o + w] = a

    r = np.arange(D)
    first = np.minimum(r % 32 // VS, 2)
    put("mean", np.full((D, D), 1.0 / D, np.float32))
    put("ident", np.eye(D, dtype=np.float32))
    put("selA", (r[:, None] == (r // 32 * 32 + first * VS + HD)[None, :]).astype(np.float32))
    put("selB", (r[:, None] == (r // 32 * 32 + HD)[None, :]).astype(np.float32))
    put("head16", (r[:, None] // HD == np.arange(NH)[None, :]).astype(np.float32))
    put("head4", (r[:, None] % 32 // HD == np.arange(GH)[None, :]).astype(np.float32))
    put("third", (first[:, None] == np.arange(3)[None, :]).astype(np.float32))
    rows = np.zeros((D, 4), np.float32)
    rows[97, 0] = 1.0
    rows[96, 1] = 1.0
    rows[97, 2] = 1.0
    put("rows", rows)
    put("eps", np.full((D, 1), EPS, np.float32))
    return c


def by_rows(w):
    a, b = np.zeros((D, w.shape[1]), w.dtype), np.zeros((D, w.shape[1]), w.dtype)
    for g in range(G):
        for t in range(GH):
            src = w[(GH * g + t) * HD:(GH * g + t + 1) * HD]
            if t < 3:
                a[32 * g + VS * t:32 * g + VS * t + HD] = src
            else:
                b[32 * g:32 * g + HD] = src
    return a, b


def kernel(**inputs):
    import concourse.bacc as bacc
    from concourse.bass_utils import run_bass_kernel_spmd

    a = {k: np.asarray(v) for k, v in inputs.items()}
    names = [
        dict(mod="W_mod", bmod="b_mod", qkv="W_qkv", bqkv="b_qkv", p="W_proj", bp="b_proj", q="W_qc", bq="b_qc", kv="W_kvc",
             bkv="b_kvc", cp="W_cproj", bcp="b_cproj", f1="W_mlp1", bf1="b_mlp1", f2="W_mlp2", bf2="b_mlp2"),
        dict(mod="ada_w", bmod="ada_b", qkv="qkv_w", bqkv="qkv_b", p="self_o_w", bp="self_o_b", q="q_w", bq="q_b", kv="kv_w",
             bkv="kv_b", cp="cross_o_w", bcp="cross_o_b", f1="mlp_w1", bf1="mlp_b1", f2="mlp_w2", bf2="mlp_b2"),
        dict(mod="ada_w", bmod="ada_b", qkv="qkv_w", bqkv="qkv_b", p="sa_proj_w", bp="sa_proj_b", q="q_w", bq="q_b",
             kv="kv_w", bkv="kv_b", cp="ca_proj_w", bcp="ca_proj_b", f1="fc1_w", bf1="fc1_b", f2="fc2_w", bf2="fc2_b"),
        dict(mod="adaln_w", bmod="adaln_b", qkv="qkv_w", bqkv="qkv_b", p="sa_proj_w", bp="sa_proj_b", q="q_w", bq="q_b",
             kv="kv_w", bkv="kv_b", cp="ca_proj_w", bcp="ca_proj_b", f1="fc1_w", bf1="fc1_b", f2="fc2_w", bf2="fc2_b"),
    ]
    w1 = np.zeros((L, D, W1_COLS), np.float32)
    w_kv = np.zeros((L, D, 2 * D), np.float32)
    w2 = np.zeros((L, D, W2_COLS), np.float32)
    bias = np.zeros((D, L * BI_COLS), np.float32)
    for l, name in enumerate(names):
        p = {k: a[f"L{l}_xcond_{v}"] for k, v in name.items()}
        parts = {"mod": p["mod"], "q": p["qkv"][:, 0:D], "k": p["qkv"][:, D:2 * D], "v": p["qkv"][:, 2 * D:3 * D],
                 }
        parts["pA"], parts["pB"] = by_rows(p["p"])
        parts["cpA"], parts["cpB"] = by_rows(p["cp"])
        parts["qr"] = np.concatenate([p["q"][:, 32 * g:32 * g + 32] for g in range(G) for _ in range(3)], axis=1)
        for k, m in parts.items():
            w1[l, :, W1[k][0]:W1[k][0] + W1[k][1]] = m
        w_kv[l] = p["kv"]
        w2[l, :, 0:4 * D] = p["f1"]
        w2[l, :, 4 * D:8 * D] = p["f2"].reshape(4, D, D).transpose(1, 0, 2).reshape(D, 4 * D)
        cols = {"mod": p["bmod"].reshape(6, D).T, "q": p["bqkv"][0:D, None], "k": p["bqkv"][D:2 * D, None],
                "p": p["bp"][:, None], "cp": p["bcp"][:, None], "kc": p["bkv"][0:D, None],
                "f1": p["bf1"].reshape(4, D).T, "f2": p["bf2"][:, None]}
        cols["vA"], cols["vB"] = by_rows(p["bqkv"][2 * D:3 * D, None])
        cols["cvA"], cols["cvB"] = by_rows(p["bkv"][D:2 * D, None])
        if l == AFFINE:
            cols["g2"], cols["b2"] = a["L1_xcond_norm2_g"][:, None], a["L1_xcond_norm2_b"][:, None]
        for k, m in cols.items():
            o = l * BI_COLS + BI[k][0]
            bias[:, o:o + BI[k][1]] = m
        for g in range(G):
            for r in range(3):
                bias[32 * r:32 * r + 32, l * BI_COLS + BI["qr"][0] + g] = p["bq"][32 * g:32 * g + 32]

    arrays = {
        "x_in": np.ascontiguousarray(a["x"].reshape(T, D).T),
        "cond_in": np.ascontiguousarray(a["cond_1024"].T),
        "ctx_in": np.ascontiguousarray(a["ctx_1024"].transpose(0, 2, 1)),
        "mask_in": np.ascontiguousarray(a["mask_BxS2_bf0"]).view(np.int32),
        "w1_in": w1, "wkv_in": w_kv, "w2_in": w2, "bias_in": bias, "const_in": constants(),
    }
    nc = bacc.Bacc("TRN2", target_bir_lowering=False, num_devices=1)
    args = [nc.dram_tensor(k, v.shape, mybir.dt.from_np(v.dtype), kind="ExternalInput").ap() for k, v in arrays.items()]
    out = nc.dram_tensor("out", (D, T), mybir.dt.float32, kind="ExternalOutput").ap()
    blocks_kernel(nc, *args, out)
    r = run_bass_kernel_spmd(nc, [arrays], core_ids=[0])
    return np.ascontiguousarray(r.results[0]["out"].T).reshape(B, N, D)
```
